# Optimizing a Trainium2 kernel written in Bass

```python
import numpy as np
import jax
import jax.numpy as jnp

def _softmax(x, axis=-1):
    return jax.nn.softmax(x, axis=axis)

def _gelu(x):
    return jax.nn.gelu(x, approximate=True)

def _silu(x):
    return jax.nn.silu(x)

def _sigmoid(x):
    return jax.nn.sigmoid(x)

def _layernorm(x, axis=-1, eps=1e-05):
    m = jnp.mean(x, axis=axis, keepdims=True)
    v = jnp.var(x, axis=axis, keepdims=True)
    return (x - m) / jnp.sqrt(v + eps)

def _scatter_add(tgt, idx, src, axis=0):
    return tgt.at[idx].add(src)

def _segment_sum(src, seg, n):
    return jax.ops.segment_sum(src, seg, n)
kernel_name = 'mk_lm_tower_d1_tok_ids1024_r4_69df43'

def setup_inputs(seed: int=0):
    np.random.seed(seed)
    _w = jnp.asarray

    def _rec_inputs():
        import jax
        import jax.numpy as jnp
        _rk = jax.random.key(seed)
        x = jax.random.randint(jax.random.fold_in(_rk, 1), (32, 512), 0, 12564, jnp.int32)
        return x
    x = _rec_inputs()

    def _L0_tok_setup():
        import jax, jax.numpy as jnp
        import numpy as np
        TOKENS = 50257
        DIMS = 256
        BATCH = 4
        SEQ = 1024
        key = jax.random.key(seed)
        k1, k2 = jax.random.split(key)
        x = jax.random.randint(k1, (BATCH, SEQ), 0, TOKENS, dtype=jnp.int64 if jax.config.jax_enable_x64 else jnp.int32)
        W = jax.random.normal(k2, (DIMS, TOKENS), dtype=jnp.float32) * (1.0 / np.sqrt(TOKENS))
        return {'x': x, 'W': W}
    _L0_tok_all = _L0_tok_setup()
    _L0_tok_in = {k: v for k, v in _L0_tok_all.items() if k in ('W',)}
    del _L0_tok_all

    def _L0_attn_setup():
        import jax, jax.numpy as jnp
        import numpy as np
        D_MODEL = 256
        D_STATE = 32
        D_CONV = 4
        EXPAND = 2
        D_INNER = EXPAND * D_MODEL
        DT_RANK = D_MODEL // 16
        BATCH = 8
        SEQ = 256

        def _silu(x):
            return x * jax.nn.sigmoid(x)

        def _layernorm(x, g, b, eps=1e-05):
            m = x.mean(-1, keepdims=True)
            v = x.var(-1, keepdims=True)
            return (x - m) / jnp.sqrt(v + eps) * g + b

        def _mamba(x, Win, convw, convb, Wx, Wdt, bdt, Alog, Dp, Wout):
            Bn, Ln, _ = x.shape
            xz = jnp.einsum('bld,ed->ble', x, Win)
            u, z = jnp.split(xz, 2, axis=-1)
            up = jnp.pad(u, ((0, 0), (D_CONV - 1, 0), (0, 0)))
            uc = convb
            for k in range(D_CONV):
                uc = uc + up[:, k:k + Ln, :] * convw[:, k]
            uc = _silu(uc)
            x_dbl = jnp.einsum('bld,ed->ble', uc, Wx)
            dt = jax.nn.softplus(jnp.einsum('blr,dr->bld', x_dbl[..., :DT_RANK], Wdt) + bdt)
            Bv = x_dbl[..., DT_RANK:DT_RANK + D_STATE]
            Cv = x_dbl[..., DT_RANK + D_STATE:]
            A = -jnp.exp(Alog)

            def step(h, ins):
                dt_t, B_t, C_t, u_t = ins
                dA = jnp.exp(dt_t[..., None] * A)
                h = dA * h + (dt_t * u_t)[..., None] * B_t[:, None, :]
                y = jnp.einsum('bdn,bn->bd', h, C_t)
                return (h, y)
            h0 = jnp.zeros((Bn, D_INNER, D_STATE), x.dtype)
            xs = (dt.transpose(1, 0, 2), Bv.transpose(1, 0, 2), Cv.transpose(1, 0, 2), uc.transpose(1, 0, 2))
            _, ys = jax.lax.scan(step, h0, xs)
            y = ys.transpose(1, 0, 2) + uc * Dp
            y = y * _silu(z)
            return jnp.einsum('bld,ed->ble', y, Wout)
        key = jax.random.key(seed)
        ks = iter(jax.random.split(key, 64))

        def rn(shape, scale):
            return jax.random.normal(next(ks), shape, jnp.float32) * scale

        def direction_params():
            return dict(Win=rn((2 * D_INNER, D_MODEL), 0.02), convw=rn((D_INNER, D_CONV), 0.1), convb=jnp.zeros((D_INNER,), jnp.float32), Wx=rn((DT_RANK + 2 * D_STATE, D_INNER), 0.02), Wdt=rn((D_INNER, DT_RANK), 0.02), bdt=rn((D_INNER,), 0.5), Alog=jnp.log(jnp.broadcast_to(jnp.arange(1, D_STATE + 1, dtype=jnp.float32), (D_INNER, D_STATE))), Dp=jnp.ones((D_INNER,), jnp.float32), Wout=rn((D_MODEL, D_INNER), 0.02), ln_g=jnp.ones((D_MODEL,), jnp.float32), ln_b=jnp.zeros((D_MODEL,), jnp.float32))
        f = direction_params()
        b = direction_params()
        inp = {'x': rn((BATCH, SEQ, D_MODEL), 1.0)}
        for k, v in f.items():
            inp[k + '_f'] = v
        for k, v in b.items():
            inp[k + '_b'] = v
        inp['Wfuse'] = rn((D_MODEL, 2 * D_MODEL), 0.02)
        inp['bfuse'] = jnp.zeros((D_MODEL,), jnp.float32)
        return inp
    _L0_attn_all = _L0_attn_setup()
    _L0_attn_in = {k: v for k, v in _L0_attn_all.items() if k in ('Win_f', 'convw_f', 'convb_f', 'Wx_f', 'Wdt_f', 'bdt_f', 'Alog_f', 'Dp_f', 'Wout_f', 'ln_g_f', 'ln_b_f', 'Win_b', 'convw_b', 'convb_b', 'Wx_b', 'Wdt_b', 'bdt_b', 'Alog_b', 'Dp_b', 'Wout_b', 'ln_g_b', 'ln_b_b', 'Wfuse', 'bfuse')}
    del _L0_attn_all

    def _L0_ffn_setup():
        import jax, jax.numpy as jnp
        import numpy as np
        NH, NKV, E, K = (16, 4, 8, 2)
        CAP_FACTOR = 1.25
        LN_EPS = 1e-05

        def _layer_norm(x, w, b):
            mu = jnp.mean(x, axis=-1, keepdims=True)
            var = jnp.mean(jnp.square(x - mu), axis=-1, keepdims=True)
            return (x - mu) * jax.lax.rsqrt(var + LN_EPS) * w + b
        key = jax.random.key(seed)
        ks = jax.random.split(key, 6)
        S, B, H, F = (512, 1, 256, 512)
        HD = H // NH
        qkv_out = NKV * (NH // NKV + 2) * HD
        f32 = jnp.float32
        return {'hidden_states': jax.random.normal(ks[0], (S, B, H), f32), 'ln1_weight': jnp.ones((H,), f32), 'ln1_bias': jnp.zeros((H,), f32), 'ln2_weight': jnp.ones((H,), f32), 'ln2_bias': jnp.zeros((H,), f32), 'qkv_weight': jax.random.normal(ks[1], (qkv_out, H), f32) * 0.02, 'proj_weight': jax.random.normal(ks[2], (H, H), f32) * 0.02, 'router_weight': jax.random.normal(ks[3], (H, E), f32) * 0.02, 'moe_w1': jax.random.normal(ks[4], (E, H, F), f32) * 0.02, 'moe_w2': jax.random.normal(ks[5], (F and E, F, H), f32)[:E] * 0.02 if False else jax.random.normal(ks[5], (E, F, H), f32) * 0.02}
    _L0_ffn_all = _L0_ffn_setup()
    _L0_ffn_in = {k: v for k, v in _L0_ffn_all.items() if k in ('ln1_weight', 'ln1_bias', 'ln2_weight', 'ln2_bias', 'qkv_weight', 'proj_weight', 'router_weight', 'moe_w1', 'moe_w2')}
    del _L0_ffn_all
    return {'x': x, 'L0_tok_W': _L0_tok_in['W'], 'L0_attn_Win_f': _L0_attn_in['Win_f'], 'L0_attn_convw_f': _L0_attn_in['convw_f'], 'L0_attn_convb_f': _L0_attn_in['convb_f'], 'L0_attn_Wx_f': _L0_attn_in['Wx_f'], 'L0_attn_Wdt_f': _L0_attn_in['Wdt_f'], 'L0_attn_bdt_f': _L0_attn_in['bdt_f'], 'L0_attn_Alog_f': _L0_attn_in['Alog_f'], 'L0_attn_Dp_f': _L0_attn_in['Dp_f'], 'L0_attn_Wout_f': _L0_attn_in['Wout_f'], 'L0_attn_ln_g_f': _L0_attn_in['ln_g_f'], 'L0_attn_ln_b_f': _L0_attn_in['ln_b_f'], 'L0_attn_Win_b': _L0_attn_in['Win_b'], 'L0_attn_convw_b': _L0_attn_in['convw_b'], 'L0_attn_convb_b': _L0_attn_in['convb_b'], 'L0_attn_Wx_b': _L0_attn_in['Wx_b'], 'L0_attn_Wdt_b': _L0_attn_in['Wdt_b'], 'L0_attn_bdt_b': _L0_attn_in['bdt_b'], 'L0_attn_Alog_b': _L0_attn_in['Alog_b'], 'L0_attn_Dp_b': _L0_attn_in['Dp_b'], 'L0_attn_Wout_b': _L0_attn_in['Wout_b'], 'L0_attn_ln_g_b': _L0_attn_in['ln_g_b'], 'L0_attn_ln_b_b': _L0_attn_in['ln_b_b'], 'L0_attn_Wfuse': _L0_attn_in['Wfuse'], 'L0_attn_bfuse': _L0_attn_in['bfuse'], 'L0_ffn_ln1_weight': _L0_ffn_in['ln1_weight'], 'L0_ffn_ln1_bias': _L0_ffn_in['ln1_bias'], 'L0_ffn_ln2_weight': _L0_ffn_in['ln2_weight'], 'L0_ffn_ln2_bias': _L0_ffn_in['ln2_bias'], 'L0_ffn_qkv_weight': _L0_ffn_in['qkv_weight'], 'L0_ffn_proj_weight': _L0_ffn_in['proj_weight'], 'L0_ffn_router_weight': _L0_ffn_in['router_weight'], 'L0_ffn_moe_w1': _L0_ffn_in['moe_w1'], 'L0_ffn_moe_w2': _L0_ffn_in['moe_w2']}

def reference(x, L0_tok_W, L0_attn_Win_f, L0_attn_convw_f, L0_attn_convb_f, L0_attn_Wx_f, L0_attn_Wdt_f, L0_attn_bdt_f, L0_attn_Alog_f, L0_attn_Dp_f, L0_attn_Wout_f, L0_attn_ln_g_f, L0_attn_ln_b_f, L0_attn_Win_b, L0_attn_convw_b, L0_attn_convb_b, L0_attn_Wx_b, L0_attn_Wdt_b, L0_attn_bdt_b, L0_attn_Alog_b, L0_attn_Dp_b, L0_attn_Wout_b, L0_attn_ln_g_b, L0_attn_ln_b_b, L0_attn_Wfuse, L0_attn_bfuse, L0_ffn_ln1_weight, L0_ffn_ln1_bias, L0_ffn_ln2_weight, L0_ffn_ln2_bias, L0_ffn_qkv_weight, L0_ffn_proj_weight, L0_ffn_router_weight, L0_ffn_moe_w1, L0_ffn_moe_w2):
    import jax
    import jax.numpy as jnp

    def _L0_tok_ref(x, W):
        import jax, jax.numpy as jnp
        import numpy as np
        TOKENS = 50257
        DIMS = 256
        BATCH = 4
        SEQ = 1024
        return jnp.take(W.T, x, axis=0)

    def _L0_attn_ref(x, Win_f, convw_f, convb_f, Wx_f, Wdt_f, bdt_f, Alog_f, Dp_f, Wout_f, ln_g_f, ln_b_f, Win_b, convw_b, convb_b, Wx_b, Wdt_b, bdt_b, Alog_b, Dp_b, Wout_b, ln_g_b, ln_b_b, Wfuse, bfuse):
        import jax, jax.numpy as jnp
        import numpy as np
        D_MODEL = 256
        D_STATE = 32
        D_CONV = 4
        EXPAND = 2
        D_INNER = EXPAND * D_MODEL
        DT_RANK = D_MODEL // 16
        BATCH = 8
        SEQ = 256

        def _silu(x):
            return x * jax.nn.sigmoid(x)

        def _layernorm(x, g, b, eps=1e-05):
            m = x.mean(-1, keepdims=True)
            v = x.var(-1, keepdims=True)
            return (x - m) / jnp.sqrt(v + eps) * g + b

        def _mamba(x, Win, convw, convb, Wx, Wdt, bdt, Alog, Dp, Wout):
            Bn, Ln, _ = x.shape
            xz = jnp.einsum('bld,ed->ble', x, Win)
            u, z = jnp.split(xz, 2, axis=-1)
            up = jnp.pad(u, ((0, 0), (D_CONV - 1, 0), (0, 0)))
            uc = convb
            for k in range(D_CONV):
                uc = uc + up[:, k:k + Ln, :] * convw[:, k]
            uc = _silu(uc)
            x_dbl = jnp.einsum('bld,ed->ble', uc, Wx)
            dt = jax.nn.softplus(jnp.einsum('blr,dr->bld', x_dbl[..., :DT_RANK], Wdt) + bdt)
            Bv = x_dbl[..., DT_RANK:DT_RANK + D_STATE]
            Cv = x_dbl[..., DT_RANK + D_STATE:]
            A = -jnp.exp(Alog)

            def step(h, ins):
                dt_t, B_t, C_t, u_t = ins
                dA = jnp.exp(dt_t[..., None] * A)
                h = dA * h + (dt_t * u_t)[..., None] * B_t[:, None, :]
                y = jnp.einsum('bdn,bn->bd', h, C_t)
                return (h, y)
            h0 = jnp.zeros((Bn, D_INNER, D_STATE), x.dtype)
            xs = (dt.transpose(1, 0, 2), Bv.transpose(1, 0, 2), Cv.transpose(1, 0, 2), uc.transpose(1, 0, 2))
            _, ys = jax.lax.scan(step, h0, xs)
            y = ys.transpose(1, 0, 2) + uc * Dp
            y = y * _silu(z)
            return jnp.einsum('bld,ed->ble', y, Wout)
        fo = _mamba(x, Win_f, convw_f, convb_f, Wx_f, Wdt_f, bdt_f, Alog_f, Dp_f, Wout_f)
        fo = _layernorm(fo, ln_g_f, ln_b_f)
        xr = x[:, ::-1, :]
        bo = _mamba(xr, Win_b, convw_b, convb_b, Wx_b, Wdt_b, bdt_b, Alog_b, Dp_b, Wout_b)
        bo = _layernorm(bo[:, ::-1, :], ln_g_b, ln_b_b)
        combined = jnp.concatenate([fo, bo], axis=-1)
        return jnp.einsum('ble,de->bld', combined, Wfuse) + bfuse

    def _L0_ffn_ref(hidden_states, ln1_weight, ln1_bias, ln2_weight, ln2_bias, qkv_weight, proj_weight, router_weight, moe_w1, moe_w2):
        import jax, jax.numpy as jnp
        import numpy as np
        NH, NKV, E, K = (16, 4, 8, 2)
        CAP_FACTOR = 1.25
        LN_EPS = 1e-05

        def _layer_norm(x, w, b):
            mu = jnp.mean(x, axis=-1, keepdims=True)
            var = jnp.mean(jnp.square(x - mu), axis=-1, keepdims=True)
            return (x - mu) * jax.lax.rsqrt(var + LN_EPS) * w + b
        S, B, H = hidden_states.shape
        HD = H // NH
        q_per_kv = NH // NKV
        ln1 = _layer_norm(hidden_states, ln1_weight, ln1_bias)
        qkv = jnp.einsum('sbh,oh->sbo', ln1, qkv_weight)
        qkv = qkv.reshape(S, B, NKV, (q_per_kv + 2) * HD)
        q = qkv[..., :q_per_kv * HD].reshape(S, B, NH, HD)
        k = qkv[..., q_per_kv * HD:(q_per_kv + 1) * HD]
        v = qkv[..., (q_per_kv + 1) * HD:]
        qb = jnp.transpose(q, (1, 2, 0, 3)).reshape(B, NKV, q_per_kv, S, HD)
        kb = jnp.transpose(k, (1, 2, 0, 3))
        vb = jnp.transpose(v, (1, 2, 0, 3))
        scale = 1.0 / np.sqrt(HD).astype(np.float32)
        scores = jnp.einsum('bgqsd,bgtd->bgqst', qb, kb) * scale
        causal = jnp.tril(jnp.ones((S, S), bool))
        scores = jnp.where(causal, scores, jnp.finfo(scores.dtype).min)
        attn = jax.nn.softmax(scores, axis=-1)
        ao = jnp.einsum('bgqst,bgtd->bgqsd', attn, vb)
        ao = ao.reshape(B, NH, S, HD)
        ao = jnp.transpose(ao, (2, 0, 1, 3)).reshape(S, B, H)
        proj = jnp.einsum('sbh,oh->sbo', ao, proj_weight)
        h1 = hidden_states + proj
        ln2 = _layer_norm(h1, ln2_weight, ln2_bias)
        x = ln2.reshape(-1, H)
        N = x.shape[0]
        logits = x @ router_weight
        probs = jax.nn.softmax(logits, axis=-1)
        top_p, top_i = jax.lax.top_k(probs, K)
        top_p = top_p / jnp.sum(top_p, axis=-1, keepdims=True)
        exp_idx = top_i.reshape(-1)
        exp_p = top_p.reshape(-1)
        order = jnp.argsort(exp_idx, stable=True)
        sorted_exp = exp_idx[order]
        counts = jnp.bincount(exp_idx, length=E)
        offsets = jnp.concatenate([jnp.zeros((1,), counts.dtype), jnp.cumsum(counts)[:-1]])
        within = jnp.arange(N * K) - offsets[sorted_exp]
        cap = int(np.ceil(N * K / E * CAP_FACTOR))
        T = E * cap
        valid = within < cap
        dst = jnp.where(valid, sorted_exp * cap + within, T)
        padded_tokens = jnp.zeros((T, H), x.dtype).at[dst].set(x[order // K], mode='drop')
        padded_probs = jnp.zeros((T,), exp_p.dtype).at[dst].set(exp_p[order], mode='drop')
        padded_tid = jnp.zeros((T,), jnp.int32).at[dst].set((order // K).astype(jnp.int32), mode='drop')
        xt = padded_tokens.reshape(E, cap, H)
        fc1 = jax.nn.gelu(jnp.einsum('ech,ehf->ecf', xt, moe_w1))
        fc2 = jnp.einsum('ecf,efh->ech', fc1, moe_w2).reshape(T, H)
        weighted = fc2 * padded_probs[:, None]
        moe_out = jnp.zeros((N, H), hidden_states.dtype).at[padded_tid].add(weighted)
        return h1 + moe_out.reshape(S, B, H)
    h = _L0_tok_ref(x, L0_tok_W)
    h = h + _L0_attn_ref(_layernorm(h, axis=-1), L0_attn_Win_f, L0_attn_convw_f, L0_attn_convb_f, L0_attn_Wx_f, L0_attn_Wdt_f, L0_attn_bdt_f, L0_attn_Alog_f, L0_attn_Dp_f, L0_attn_Wout_f, L0_attn_ln_g_f, L0_attn_ln_b_f, L0_attn_Win_b, L0_attn_convw_b, L0_attn_convb_b, L0_attn_Wx_b, L0_attn_Wdt_b, L0_attn_bdt_b, L0_attn_Alog_b, L0_attn_Dp_b, L0_attn_Wout_b, L0_attn_ln_g_b, L0_attn_ln_b_b, L0_attn_Wfuse, L0_attn_bfuse)
    h = h + _L0_ffn_ref(_layernorm(h, axis=-1), L0_ffn_ln1_weight, L0_ffn_ln1_bias, L0_ffn_ln2_weight, L0_ffn_ln2_bias, L0_ffn_qkv_weight, L0_ffn_proj_weight, L0_ffn_router_weight, L0_ffn_moe_w1, L0_ffn_moe_w2)
    return h

_drawn_inputs = setup_inputs


def setup_inputs(seed=0):
    import zlib

    import numpy as np

    out = dict(_drawn_inputs(seed))
    spreads = {'L0_attn_convb_f': (0.0, 0.1),
     'L0_attn_Dp_f': (1.0, 0.2),
     'L0_attn_ln_g_f': (1.0, 0.2),
     'L0_attn_ln_b_f': (0.0, 0.1),
     'L0_attn_convb_b': (0.0, 0.1),
     'L0_attn_Dp_b': (1.0, 0.2),
     'L0_attn_ln_g_b': (1.0, 0.2),
     'L0_attn_ln_b_b': (0.0, 0.1),
     'L0_attn_bfuse': (0.0, 0.1),
     'L0_ffn_ln1_weight': (1.0, 0.6),
     'L0_ffn_ln1_bias': (0.0, 0.8),
     'L0_ffn_ln2_weight': (1.0, 0.6),
     'L0_ffn_ln2_bias': (0.0, 0.498)}
    factors = {'L0_attn_Wx_f': 8.0,
     'L0_attn_Wdt_f': 23.465,
     'L0_attn_bdt_f': 8.0,
     'L0_attn_Alog_f': 64.0,
     'L0_attn_Wx_b': 8.0,
     'L0_attn_Wdt_b': 45.556,
     'L0_attn_bdt_b': 8.0,
     'L0_attn_Alog_b': 63.559}
    for name, (base, spread) in spreads.items():
        noise = np.random.default_rng([zlib.crc32(name.encode()), seed]).standard_normal(out[name].shape)
        drawn = base * np.exp(spread * noise) if base else spread * noise
        out[name] = jnp.asarray(drawn.astype(out[name].dtype))
    for name, factor in factors.items():
        out[name] = (out[name] * factor).astype(out[name].dtype)
    return out
```

```python
import numpy as np

from contextlib import ExitStack

import concourse.bass as bass
from concourse import mybir

F32 = mybir.dt.float32
I32 = mybir.dt.int32
U32 = mybir.dt.uint32
ALU = mybir.AluOpType
ACT = mybir.ActivationFunctionType
AX_X = mybir.AxisListType.X

P = 128
DM = 256
KD = DM // P
DI = 512
MD = DI // P
NS = 32
RK = 16
NX = 2 * NS + RK
TAPS = 4
SEQ = 512
NSEQ = 32
TT = SEQ // P
PAD = TAPS - 1
EPS = 1e-5
DIRS = 2
LN2 = 0.6931471805599453
DEAD_LOG = 5.5
ALOG_TOP = 80.0
EXP_TOP = 40.0


def mamba_stage(nc, tok_ids, table, w, h1_dram):
    ctx = ExitStack()
    with ctx:
        def sb(name, shape, dt=F32):
            return ctx.enter_context(nc.sbuf_tensor(name, shape, dt))

        def sem(name):
            return ctx.enter_context(nc.semaphore(name))

        win = [sb(f"win{d}", [P, KD, 2 * DI]) for d in range(DIRS)]
        wx = [sb(f"wx{d}", [P, MD, NX]) for d in range(DIRS)]
        wdt = [sb(f"wdt{d}", [P, DI]) for d in range(DIRS)]
        wdta = [sb(f"wdta{d}", [P, DI]) for d in range(DIRS)]
        wout = [sb(f"wout{d}", [P, MD, DM]) for d in range(DIRS)]
        wfus = [sb(f"wfus{d}", [P, KD, DM]) for d in range(DIRS)]
        convw = [sb(f"convw{d}", [P, MD, TAPS]) for d in range(DIRS)]
        convb = [sb(f"convb{d}", [P, MD]) for d in range(DIRS)]
        bdt = [sb(f"bdt{d}", [P, MD]) for d in range(DIRS)]
        dp = [sb(f"dp{d}", [P, MD]) for d in range(DIRS)]
        amat = [sb(f"amat{d}", [P, MD, NS]) for d in range(DIRS)]
        almin = [sb(f"almin{d}", [P, MD]) for d in range(DIRS)]
        alok = [sb(f"alok{d}", [P, MD]) for d in range(DIRS)]
        alb = [sb(f"alb{d}", [P, MD]) for d in range(DIRS)]
        lng = [sb(f"lng{d}", [P, KD]) for d in range(DIRS)]
        lnb = [sb(f"lnb{d}", [P, KD]) for d in range(DIRS)]
        bfus = sb("bfus", [1, DM])
        wmean = sb("wmean", [P, DIRS, MD])
        cvec = sb("cvec", [P, DM])
        ident = sb("ident", [P, P])
        ones = sb("ones", [P, P])
        neg_half = sb("neg_half", [P, TT])
        smask0 = sb("smask0", [NS, P])

        ids = sb("ids", [P, (NSEQ + 2) * TT], I32)
        idc = sb("idc", [P, TT], I32)
        g = sb("g", [P, TT, DM])
        stats = sb("stats", [P, TT, 6])
        mv = sb("mv", [P, TT, 2])
        rstd = sb("rstd", [P, TT])
        xn = sb("xn", [P, TT, DM])
        xt = sb("xt", [P, KD, SEQ])
        h0c = sb("h0c", [P, TT, DM])
        h1a = sb("h1a", [P, TT, DM])
        h1o = sb("h1o", [P, TT, DM])
        u = sb("u", [P, MD, SEQ + 2 * PAD])
        uc = [sb(f"uc{d}", [P, MD, SEQ]) for d in range(DIRS)]
        zs = [sb(f"zs{d}", [P, MD, SEQ]) for d in range(DIRS)]
        xd = [sb(f"xd{d}", [P, SEQ]) for d in range(DIRS)]
        bcp = sb("bcp", [NS, SEQ])
        bb = [sb(f"bb{d}", [P, 2, SEQ]) for d in range(DIRS)]
        v = sb("v", [P, MD, SEQ])
        y = sb("y", [P, MD, SEQ])
        lg = sb("lg", [P, MD, SEQ])
        wk = sb("wk", [P, MD, SEQ])
        yz = sb("yz", [P, MD, SEQ])
        qq = sb("qq", [P, MD, SEQ])
        tp = sb("tp", [P, MD, SEQ])
        fo = sb("fo", [P, KD, SEQ])
        sq = sb("sq", [P, KD, SEQ])
        r2 = sb("r2", [P, TT])
        r3 = sb("r3", [P, TT])
        xmax = sb("xmax", [P, 1])
        dgt = sb("dgt", [P, MD])
        dct = sb("dct", [P, 1])
        dall = sb("dall", [P, 1])
        live = sb("live", [P, DIRS], I32)
        smask = sb("smask", [NS, P])
        eb = sb("eb", [P, 2, SEQ])
        eda = sb("eda", [P, SEQ])
        eh = sb("eh", [P, SEQ])

        pj = [ctx.enter_context(nc.psum_tensor(f"pj{i}", [P, SEQ], F32)) for i in range(2)]
        px = ctx.enter_context(nc.psum_tensor("px", [P, SEQ], F32))
        pss = [ctx.enter_context(nc.psum_tensor(f"pss{i}", [P, SEQ], F32)) for i in range(DIRS)]
        po = [ctx.enter_context(nc.psum_tensor(f"po{i}", [P, SEQ], F32)) for i in range(3)]

        bc_dram = [nc.dram_tensor(f"bc{d}", [2 * NS, SEQ], F32).ap() for d in range(DIRS)]

        names = """c_tab cv ld_w ld_ids prep_a prep_w prep_v idc_ok gath st_ok lnv_ok lnr_ok xn_ok xt_ps xt_ok h0_ok
          u_ps u_ok a_ok z_ps z_ok uc_ok xd_ps xd_ok bc_ok bcast xd_st dt_ps v_ok vc_ok y_ok l_ok w_ok g_ok
          d0_ok dt_ok dtu_ok tp_ok da_ok h_ok hc_ok q_ok q2_ok yv_ok yz_ok xm_ok qd_ps gt_ok ct_ok cnt_ps
          fl_ok s_ps o_ps fo_ok sq_ok ss_ps rv_ok rr_ok f_ps fin_ok h1_st gt2 e_bc e_da e_tp e_h e_hc e_y""".split()
        S = {n: sem("m_" + n) for n in names}

        block = ctx.enter_context(nc.Block())

        def wait_apart(eng, semaphore, value):
            value = value if isinstance(value, int) else eng.to_reg(value)
            eng.wait_ge(S["c_tab"], 1)
            eng.wait_ge(semaphore, value)

        def xd_rows(d):
            return xd[d][2 * NS:NX, :]

        @block.sync
        def _(sp):
            for d in range(DIRS):
                k = w[d]
                sp.dma_start(win[d][:], k["Win"].rearrange("(k p) e -> p k e", p=P)).then_inc(S["ld_w"], 16)
                sp.dma_start(wx[d][:], k["Wx"].rearrange("(m p) e -> p m e", p=P)).then_inc(S["ld_w"], 16)
                sp.dma_start(wdt[d][2 * NS:NX, :], k["Wdt"]).then_inc(S["ld_w"], 16)
                sp.dma_start(wout[d][:], k["Wout"].rearrange("(m p) e -> p m e", p=P)).then_inc(S["ld_w"], 16)
                sp.dma_start(wfus[d][:], k["Wfuse"].rearrange("(k p) e -> p k e", p=P)).then_inc(S["ld_w"], 16)
                sp.dma_start(convw[d][:], k["convw"].rearrange("(m p) e -> p m e", p=P)).then_inc(S["ld_w"], 16)
                sp.dma_start(amat[d][:], k["Alog"].rearrange("(m p) e -> p m e", p=P)).then_inc(S["ld_w"], 16)
                for dst, name in ((convb, "convb"), (bdt, "bdt"), (dp, "Dp"), (lng, "ln_g"), (lnb, "ln_b")):
                    sp.dma_start(dst[d][:], k[name]).then_inc(S["ld_w"], 16)
                if d == 0:
                    sp.dma_start(bfus[:], k["bfuse"]).then_inc(S["ld_w"], 16)
            sp.dma_start(ids[:], tok_ids).then_inc(S["ld_ids"], 16)

            def broadcast(t, d):
                if not (isinstance(t, int) and t < 2):
                    wait_apart(sp, S["hc_ok"], MD * (t - 1))
                wait_apart(sp, S["xd_ok"], t + 1)
                sp.dma_start(bc_dram[d], xd[d][0:2 * NS, :]).then_inc(S["xd_st"], 16)
                sp.wait_ge(S["xd_st"], 16 * (t + 1))
                sp.dma_start(bb[d][:], bc_dram[d][0:2 * NS:NS, :].partition_broadcast(P)).then_inc(S["bcast"], 16)

            def store(s):
                sp.wait_ge(S["fin_ok"], TT * (2 * s + 2))
                dst = h1_dram[bass.ds(s * SEQ, SEQ), :].rearrange("(j p) c -> p j c", p=P)
                sp.dma_start(dst, h1o[:]).then_inc(S["h1_st"], 16)

            def more_states(t, d):
                wait_apart(sp, S["fl_ok"], 4 * t + 3)
                go = sp.value_load(live[0:1, d:d + 1], min_val=0, max_val=1)
                with sp.If(go > 0):
                    with sp.Fori(1, NS) as n:
                        c = sp.snap(sp_count)
                        wait_apart(sp, S["e_y"], c * MD)
                        for i in range(2):
                            row = bc_dram[d][bass.ds(n + NS * i, 1), :].squeeze(0)
                            sp.dma_start(eb[:, i, :], row.partition_broadcast(P)).then_inc(S["e_bc"], 16)
                        sp.reg_add(sp_count, sp_count, 1)
                with sp.Else():
                    sp.nop()

            sp_count = sp.alloc_register("sp_states")
            sp.reg_mov(sp_count, 0)
            broadcast(0, 0)

            def slots(s, first):
                for d in range(DIRS):
                    t = 2 * s + d
                    more_states(t, d)
                    broadcast(t + 1, 1 - d)
                    if d == 0 and not first:
                        store(s - 1)

            slots(0, True)
            with sp.Fori(1, NSEQ) as s:
                slots(s, False)
            store(NSEQ - 1)
            sp.wait_ge(S["h1_st"], 16 * NSEQ)
            sp.wait_ge(S["bcast"], 16 * (2 * NSEQ + 1))

        @block.gpsimd
        def _(pool):
            pool.memset(ones[:], 1.0).then_inc(S["c_tab"], 1)
            pool.wait_ge(S["c_tab"], 1)
            pool.memset(neg_half[:], -0.5).then_inc(S["c_tab"], 1)
            pool.wait_ge(S["c_tab"], 2)
            pool.memset(u[:, :, 0:PAD], 0.0).then_inc(S["c_tab"], 1)
            pool.wait_ge(S["c_tab"], 3)
            pool.memset(u[:, :, PAD + SEQ:], 0.0).then_inc(S["c_tab"], 1)
            pool.wait_ge(S["c_tab"], 4)
            pool.memset(ident[:], 0.0).then_inc(S["c_tab"], 1)
            pool.wait_ge(S["c_tab"], 5)
            pool.affine_select(out=ident[:], in_=ident[:], compare_op=ALU.not_equal, fill=1.0, base=0,
                               pattern=[[-1, P]], channel_multiplier=1).then_inc(S["c_tab"], 1)
            pool.wait_ge(S["c_tab"], 6)
            pool.affine_select(out=smask0[:], in_=ones[0:NS, :], compare_op=ALU.is_gt, fill=0.0, base=0,
                               pattern=[[0, P]], channel_multiplier=1).then_inc(S["c_tab"], 1)
            pool.wait_ge(S["c_tab"], 7)
            pool.wait_ge(S["ld_ids"], 16)

            def gather(s):
                if not (isinstance(s, int) and s == 0):
                    pool.wait_ge(S["gath"], 16 * TT * s)
                    pool.wait_ge(S["xn_ok"], TT * s)
                    pool.wait_ge(S["h0_ok"], s)
                pool.tensor_copy(idc[:], ids[:, bass.ds(s * TT, TT)]).then_inc(S["idc_ok"], 1)
                wait_apart(pool, S["idc_ok"], s + 1)
                for j in range(TT):
                    pool.indirect_dma_start(out=g[:, j, :], out_offset=None, in_=table,
                                            in_offset=bass.IndirectOffsetOnAxis(ap=idc[:, j:j + 1].bitcast(U32), axis=0)
                                            ).then_inc(S["gath"], 16)

            def ln_scale(s):
                wait_apart(pool, S["st_ok"], s + 1)
                pool.tensor_scalar(r3[:], mv[:, :, 1], 1.0, EPS, ALU.mult, ALU.add).then_inc(S["lnv_ok"], 1)
                pool.wait_ge(S["lnv_ok"], s + 1)
                pool.tensor_tensor(rstd[:], r3[:], neg_half[:], ALU.pow).then_inc(S["lnr_ok"], 1)

            def keep_residual(s):
                if not (isinstance(s, int) and s == 0):
                    pool.wait_ge(S["fin_ok"], TT * (2 * s - 1))
                pool.wait_ge(S["prep_v"], 3 * DIRS + 2)
                pool.wait_ge(S["gath"], 16 * TT * (s + 1))
                pool.tensor_tensor(h0c[:], g[:], cvec[:].unsqueeze(1).to_broadcast([P, TT, DM]), ALU.add
                                   ).then_inc(S["h0_ok"], 1)

            def clamp(t):
                for m in range(MD):
                    wait_apart(pool, S["v_ok"], MD * t + m + 1)
                    if not (isinstance(t, int) and t == 0):
                        wait_apart(pool, S["g_ok"], MD * (t - 1) + m + 1)
                    pool.tensor_scalar(lg[:, m, :], v[:, m, :], EXP_TOP, -3.0e38, ALU.min, ALU.max
                                       ).then_inc(S["vc_ok"], 1)

            def scan_inputs(t, d):
                pool.wait_ge(S["bcast"], 16 * (t + 1))
                for m in range(MD):
                    pool.wait_ge(S["dt_ok"], MD * t + m + 1)
                    pool.tensor_tensor(wk[:, m, :], v[:, m, :], uc[d][:, m, :], ALU.mult).then_inc(S["dtu_ok"], 1)
                    pool.wait_ge(S["dtu_ok"], MD * t + m + 1)
                    if not (isinstance(t, int) and t == 0):
                        pool.wait_ge(S["yv_ok"], MD * (t - 1) + m + 1)
                    pool.tensor_tensor(tp[:, m, :], wk[:, m, :], bb[d][:, 0, :], ALU.mult).then_inc(S["tp_ok"], 1)

            def gate(t, d):
                for m in range(MD):
                    pool.wait_ge(S["yv_ok"], MD * t + m + 1)
                    if not (isinstance(t, int) and t == 0):
                        pool.wait_ge(S["o_ps"], KD * t)
                    pool.tensor_tensor(yz[:, m, :], tp[:, m, :], zs[d][:, m, :], ALU.mult).then_inc(S["yz_ok"], 1)

            def row_scale(t):
                pool.wait_ge(S["ss_ps"], t + 1)
                pool.wait_ge(S["rv_ok"], t + 1)
                if not (isinstance(t, int) and t == 0):
                    pool.wait_ge(S["fin_ok"], TT * t)
                pool.tensor_tensor(r2[:], r2[:], neg_half[:], ALU.pow).then_inc(S["rr_ok"], 1)

            gather(0)
            ln_scale(0)
            keep_residual(0)
            gather(1)
            clamp(0)

            def slots(s, first):
                for d in range(DIRS):
                    t = 2 * s + d
                    scan_inputs(t, d)
                    if not (first and d == 0):
                        row_scale(t - 1)
                    if d == 0:
                        ln_scale(s + 1)
                    clamp(t + 1)
                    gate(t, d)
                    if d == 1:
                        keep_residual(s + 1)
                        gather(s + 2)

            slots(0, True)
            with pool.Fori(1, NSEQ) as s:
                slots(s, False)
            row_scale(2 * NSEQ - 1)
            pool.wait_ge(S["gath"], 16 * TT * (NSEQ + 2))

        @block.scalar
        def _(act):
            act.wait_ge(S["ld_w"], 16 * (12 * DIRS + 1))
            for d in range(DIRS):
                act.activation(wdta[d][2 * NS:NX, :], wdt[d][2 * NS:NX, :], ACT.Abs).then_inc(S["prep_a"], 1)
            act.wait_ge(S["prep_v"], 2 * DIRS)
            for d in range(DIRS):
                act.activation(amat[d][:], amat[d][:], ACT.Exp).then_inc(S["prep_a"], 1)
            act.wait_ge(S["prep_a"], 2 * DIRS)
            for d in range(DIRS):
                act.activation(amat[d][:], amat[d][:], ACT.Copy, scale=-1.0).then_inc(S["prep_a"], 1)
            act.wait_ge(S["prep_a"], 3 * DIRS)

            def xt_copy(s):
                for k in range(KD):
                    act.wait_ge(S["xt_ps"], KD * s + k + 1)
                    act.activation(xt[:, k, :], pj[k][:], ACT.Copy).then_inc(S["xt_ok"], 1)

            def u_copy(t, d):
                act.wait_ge(S["c_tab"], 4)
                tap = TAPS - 1
                for m in range(MD):
                    act.wait_ge(S["u_ps"], MD * t + m + 1)
                    if not (isinstance(t, int) and t == 0):
                        act.wait_ge(S["cv"], PAD * MD * t - MD + m + 1)
                    act.activation(u[:, m, PAD:PAD + SEQ], pj[m % 2][:], ACT.Copy).then_inc(S["u_ok"], 1)
                    if not (isinstance(t, int) and t < 2):
                        act.wait_ge(S["q2_ok"], MD * (t - 2) + m + 1)
                    act.activation(uc[d][:, m, :], pj[m % 2][:], ACT.Identity, bias=convb[d][:, m:m + 1],
                                   scale=convw[d][:, m, tap:tap + 1]).then_inc(S["a_ok"], 1)

            def z_silu(t, d):
                for m in range(MD):
                    act.wait_ge(S["z_ps"], MD * t + m + 1)
                    if not (isinstance(t, int) and t < 2):
                        act.wait_ge(S["yz_ok"], MD * (t - 2) + m + 1)
                    act.activation(zs[d][:, m, :], pj[m % 2][:], ACT.Silu).then_inc(S["z_ok"], 1)

            def uc_silu(t, d):
                for m in range(MD):
                    act.wait_ge(S["cv"], PAD * MD * t + 2 * MD + m + 1)
                    act.activation(uc[d][:, m, :], uc[d][:, m, :], ACT.Silu).then_inc(S["uc_ok"], 1)

            def xd_copy(t, d):
                act.wait_ge(S["xd_ps"], t + 1)
                if not (isinstance(t, int) and t < 2):
                    act.wait_ge(S["xd_st"], 16 * (t - 1))
                act.activation(xd[d][0:NX, :], px[0:NX, :], ACT.Copy).then_inc(S["xd_ok"], 1)

            def softplus_logs(t, d):
                for m in range(MD):
                    act.wait_ge(S["dt_ps"], MD * t + m + 1)
                    if not (isinstance(t, int) and t == 0):
                        act.wait_ge(S["q_ok"], MD * (t - 1) + m + 1)
                        act.wait_ge(S["dtu_ok"], MD * (t - 1) + m + 1)
                        act.wait_ge(S["da_ok"], MD * (t - 1) + m + 1)
                    act.activation(v[:, m, :], pj[m % 2][:], ACT.Identity, bias=bdt[d][:, m:m + 1]
                                   ).then_inc(S["v_ok"], 1)
                act.preload_act_table_set("natural_log_exp_and_others")
                for m in range(MD):
                    act.wait_ge(S["vc_ok"], MD * t + m + 1)
                    if not (isinstance(t, int) and t == 0):
                        act.wait_ge(S["h_ok"], MD * (t - 1) + m + 1)
                    act.activation(y[:, m, :], lg[:, m, :], ACT.Exp).then_inc(S["y_ok"], 1)
                for m in range(MD):
                    act.wait_ge(S["y_ok"], MD * t + m + 1)
                    act.activation(lg[:, m, :], y[:, m, :], ACT.Ln, bias=1.0).then_inc(S["l_ok"], 1)

            def decays(t, d):
                for m in range(MD):
                    act.wait_ge(S["dt_ok"], MD * t + m + 1)
                    act.activation(y[:, m, :], v[:, m, :], ACT.Exp, scale=amat[d][:, m, 0:1]).then_inc(S["da_ok"], 1)

            def project_copies(t):
                for k in range(KD):
                    act.wait_ge(S["o_ps"], KD * t + k + 1)
                    if not (isinstance(t, int) and t == 0):
                        act.wait_ge(S["f_ps"], 2 * t)
                    act.activation(sq[:, k, :], po[k][:], ACT.Square).then_inc(S["sq_ok"], 1)
                    act.activation(fo[:, k, :], po[k][:], ACT.Copy).then_inc(S["fo_ok"], 1)

            def more_states(t, d):
                wait_apart(act, S["fl_ok"], 4 * t + 3)
                go = act.value_load(live[0:1, d:d + 1], min_val=0, max_val=1)
                with act.If(go > 0):
                    with act.Fori(1, NS) as n:
                        c = act.snap(act_count)
                        for m in range(MD):
                            act.wait_ge(S["e_h"], c * MD + m)
                            act.activation(eda[:], v[:, m, :], ACT.Exp, scale=amat[d][:, m, bass.ds(n, 1)]
                                           ).then_inc(S["e_da"], 1)
                        act.reg_add(act_count, act_count, 1)
                with act.Else():
                    act.nop()

            act_count = act.alloc_register("act_states")
            act.reg_mov(act_count, 0)

            def front(t, d):
                uc_silu(t, d)
                xd_copy(t, d)
                softplus_logs(t, d)

            xt_copy(0)
            u_copy(0, 0)
            z_silu(0, 0)
            front(0, 0)

            def slots(s, first):
                for d in range(DIRS):
                    t = 2 * s + d
                    u_copy(t + 1, 1 - d)
                    decays(t, d)
                    more_states(t, d)
                    z_silu(t + 1, 1 - d)
                    if not (first and d == 0):
                        project_copies(t - 1)
                    front(t + 1, 1 - d)
                    if d == 0:
                        xt_copy(s + 1)

            slots(0, True)
            with act.Fori(1, NSEQ) as s:
                slots(s, False)
            project_copies(2 * NSEQ - 1)

        @block.tensor
        def _(pe):
            mm = nc.tensor.matmul
            pe.wait_ge(S["c_tab"], 6)
            pe.wait_ge(S["ld_w"], 16 * (12 * DIRS + 1))
            pe.wait_ge(S["prep_w"], 1)
            for d in range(DIRS):
                for k in range(KD):
                    mm(po[0][:, 0:DM], fo[:, 0, (d * KD + k) * P:(d * KD + k + 1) * P], wfus[d][:, k, :],
                       start=(d == 0 and k == 0), stop=False)
            mm(po[0][:, 0:DM], ones[0:1, :], bfus[:], start=False, stop=True).then_inc(S["ct_ok"], 1)
            pe.wait_ge(S["prep_w"], 2)

            def turn_x(s):
                pe.wait_ge(S["xn_ok"], TT * (s + 1))
                for k in range(KD):
                    if not (isinstance(s, int) and s == 0):
                        pe.wait_ge(S["v_ok"], MD * (2 * s - 1) + 2 + k + 1)
                    for j in range(TT):
                        i = nc.tensor.transpose(pj[k][:, j * P:(j + 1) * P], xn[:, j, k * P:(k + 1) * P], ident[:])
                    i.then_inc(S["xt_ps"], 1)

            def in_proj(t, d, s_of):
                pe.wait_ge(S["xt_ok"], KD * (s_of + 1))
                if not (isinstance(t, int) and t == 0):
                    pe.wait_ge(S["v_ok"], MD * t)
                for half, ps, ok in ((0, "u_ps", "a_ok"), (1, "z_ps", "z_ok")):
                    for m in range(MD):
                        if half == 1 or m >= 2:
                            prev = "a_ok" if half == 0 or m < 2 else "z_ok"
                            pe.wait_ge(S[prev], MD * t + (m - 2) % MD + 1)
                        for k in range(KD):
                            c = half * DI + m * P
                            i = mm(pj[m % 2][:], win[d][:, k, c:c + P], xt[:, k, :], start=(k == 0), stop=(k == KD - 1))
                        i.then_inc(S[ps], 1)

            def x_dbl(t, d):
                if not (isinstance(t, int) and t == 0):
                    pe.wait_ge(S["fl_ok"], 4 * t)
                for m in range(MD):
                    pe.wait_ge(S["uc_ok"], MD * t + m + 1)
                    i = mm(px[0:NX, :], wx[d][:, m, :], uc[d][:, m, :], start=(m == 0), stop=(m == MD - 1))
                i.then_inc(S["xd_ps"], 1)

            def dt_proj(t, d):
                pe.wait_ge(S["xd_ok"], t + 1)
                for m in range(MD):
                    if m < 2:
                        pe.wait_ge(S["z_ok"], MD * t + m + 3)
                    else:
                        pe.wait_ge(S["v_ok"], MD * t + m - 1)
                    mm(pj[m % 2][:], wdt[d][2 * NS:NX, m * P:(m + 1) * P], xd_rows(d), start=True, stop=True
                       ).then_inc(S["dt_ps"], 1)

            def dead_sums(t, d):
                pe.wait_ge(S["xm_ok"], t + 1)
                for m in range(MD):
                    i = mm(px[:, m:m + 1], wdta[d][2 * NS:NX, m * P:(m + 1) * P], xmax[2 * NS:NX, :],
                           start=True, stop=True)
                i.then_inc(S["qd_ps"], 1)
                pe.wait_ge(S["gt_ok"], 2 * t + 2)
                mm(px[:, 8:8 + MD], ones[:], dgt[:], start=True, stop=True).then_inc(S["cnt_ps"], 1)

            def state_sum(t, d):
                pe.wait_ge(S["fl_ok"], 4 * t + 4)
                pe.wait_ge(S["bc_ok"], t + 1)
                if not (isinstance(t, int) and t < 2):
                    pe.wait_ge(S["q_ok"], MD * (t - 1))
                mm(pss[d][:], smask[:], bcp[:], start=True, stop=True).then_inc(S["s_ps"], 1)

            def out_proj(t, d):
                for k in range(KD):
                    if not (isinstance(t, int) and t == 0):
                        pe.wait_ge(S["fin_ok"], TT * t)
                    for m in range(MD):
                        pe.wait_ge(S["yz_ok"], MD * t + m + 1)
                        i = mm(po[k][:], wout[d][:, m, k * P:(k + 1) * P], yz[:, m, :], start=(m == 0), stop=(m == MD - 1))
                    i.then_inc(S["o_ps"], 1)

            def fusion(t, d):
                pe.wait_ge(S["sq_ok"], KD * (t + 1))
                pe.wait_ge(S["fo_ok"], KD * (t + 1))
                for j in range(TT):
                    for k in range(KD):
                        i = mm(po[1][:, j:j + 1], sq[:, k, j * P:(j + 1) * P], ones[:, 0:1],
                               start=(k == 0), stop=(k == KD - 1))
                i.then_inc(S["ss_ps"], 1)
                for h in range(2):
                    bank = po[2] if h == 0 else po[0]
                    for jj in range(2):
                        j = 2 * h + jj
                        for k in range(KD):
                            i = mm(bank[:, jj * DM:(jj + 1) * DM], fo[:, k, j * P:(j + 1) * P], wfus[d][:, k, :],
                                   start=(k == 0), stop=(k == KD - 1))
                    i.then_inc(S["f_ps"], 1)

            def front_tail(t, d):
                dt_proj(t, d)
                dead_sums(t, d)
                state_sum(t, d)

            turn_x(0)
            in_proj(0, 0, 0)
            x_dbl(0, 0)
            front_tail(0, 0)

            def slots(s, first):
                for d in range(DIRS):
                    t = 2 * s + d
                    in_proj(t + 1, 1 - d, s + d)
                    if not (first and d == 0):
                        out_proj(t - 1, 1 - d)
                    x_dbl(t + 1, 1 - d)
                    if not (first and d == 0):
                        fusion(t - 1, 1 - d)
                    front_tail(t + 1, 1 - d)
                    if d == 0:
                        turn_x(s + 1)

            slots(0, True)
            with pe.Fori(1, NSEQ) as s:
                slots(s, False)
            out_proj(2 * NSEQ - 1, 1)
            fusion(2 * NSEQ - 1, 1)

        @block.vector
        def _(dve):
            tt, ts, stt = nc.vector.tensor_tensor, nc.vector.tensor_scalar, nc.vector.scalar_tensor_tensor
            dve.wait_ge(S["ld_w"], 16 * (12 * DIRS + 1))
            dve.wait_ge(S["c_tab"], 7)
            for d in range(DIRS):
                for k in range(KD):
                    c = d * KD + k
                    i = ts(fo[:, 0, c * P:(c + 1) * P], ones[:], lnb[d][:, k:k + 1], None, ALU.mult)
            i.then_inc(S["prep_w"], 1)
            for d in range(DIRS):
                nc.vector.tensor_reduce(almin[d][:], amat[d][:, :, 1:NS], AX_X, ALU.min).then_inc(S["prep_v"], 1)
                dve.wait_ge(S["prep_v"], 2 * d + 1)
                ts(amat[d][:], amat[d][:], ALOG_TOP, None, ALU.min).then_inc(S["prep_v"], 1)
            for d in range(DIRS):
                nc.vector.tensor_reduce(wmean[:, d, :], wout[d][:], AX_X, ALU.add).then_inc(S["prep_v"], 1)
            dve.wait_ge(S["prep_v"], 3 * DIRS)
            ts(wmean[:], wmean[:], 1.0 / DM, None, ALU.mult).then_inc(S["prep_v"], 1)
            dve.wait_ge(S["prep_v"], 3 * DIRS + 1)
            dve.wait_ge(S["ct_ok"], 1)
            nc.vector.tensor_copy(cvec[:], po[0][:, 0:DM]).then_inc(S["prep_v"], 1)
            for d in range(DIRS):
                for m in range(MD):
                    ts(wout[d][:, m, :], wout[d][:, m, :], wmean[:, d, m:m + 1], None, ALU.subtract)
                for k in range(KD):
                    ts(wfus[d][:, k, :], wfus[d][:, k, :], lng[d][:, k:k + 1], None, ALU.mult)
                tt(alb[d][:], almin[d][:], bdt[d][:], ALU.add)
                i = ts(alok[d][:], almin[d][:], DEAD_LOG, None, ALU.is_gt)
            i.then_inc(S["prep_w"], 1)

            def ln_stats(s):
                dve.wait_ge(S["gath"], 16 * TT * (s + 1))
                if not (isinstance(s, int) and s == 0):
                    dve.wait_ge(S["xn_ok"], TT * s)
                for j in range(TT):
                    i = nc.vector.bn_stats(stats[:, j, :], g[:, j, :])
                i.then_inc(S["gt2"], 1)
                wait_apart(dve, S["gt2"], s + 1)
                for j in range(TT):
                    i = nc.vector.bn_aggr(mv[:, j, :], stats[:, j, :])
                i.then_inc(S["st_ok"], 1)

            def ln_apply(s):
                dve.wait_ge(S["lnr_ok"], s + 1)
                if not (isinstance(s, int) and s == 0):
                    dve.wait_ge(S["xt_ps"], KD * s)
                for j in range(TT):
                    ts(xn[:, j, :], g[:, j, :], mv[:, j, 0:1], rstd[:, j:j + 1], ALU.subtract, ALU.mult
                       ).then_inc(S["xn_ok"], 1)

            def conv(t, d):
                dve.wait_ge(S["u_ok"], MD * (t + 1))
                for n in range(PAD):
                    tap = TAPS - 2 - n
                    shift = -(n + 1) if d == 0 else n + 1
                    for m in range(MD):
                        if n == 0:
                            dve.wait_ge(S["a_ok"], MD * t + m + 1)
                        else:
                            dve.wait_ge(S["cv"], PAD * MD * t + (n - 1) * MD + m + 1)
                        stt(uc[d][:, m, :], u[:, m, PAD + shift:PAD + shift + SEQ], convw[d][:, m, tap:tap + 1],
                            uc[d][:, m, :], ALU.mult, ALU.add).then_inc(S["cv"], 1)

            def bc_product(t, d):
                dve.wait_ge(S["xd_ok"], t + 1)
                if not (isinstance(t, int) and t == 0):
                    dve.wait_ge(S["s_ps"], t)
                    dve.wait_ge(S["qd_ps"], t)
                tt(bcp[:], px[NS:2 * NS, :], xd[d][0:NS, :], ALU.mult).then_inc(S["bc_ok"], 1)
                nc.vector.tensor_reduce(xmax[2 * NS:NX, :], xd_rows(d), AX_X, ALU.max,
                                        apply_absolute_value=True).then_inc(S["xm_ok"], 1)

            def dead_test(t, d):
                dve.wait_ge(S["qd_ps"], t + 1)
                if not (isinstance(t, int) and t == 0):
                    dve.wait_ge(S["cnt_ps"], t)
                tt(dgt[:], alb[d][:], px[:, 0:MD], ALU.subtract).then_inc(S["gt_ok"], 1)
                dve.wait_ge(S["gt_ok"], 2 * t + 1)
                stt(dgt[:], dgt[:], DEAD_LOG, alok[d][:], ALU.is_gt, ALU.mult).then_inc(S["gt_ok"], 1)

            def dead_mask(t, d):
                dve.wait_ge(S["cnt_ps"], t + 1)
                nc.vector.tensor_reduce(dct[:], px[:, 8:8 + MD], AX_X, ALU.add).then_inc(S["fl_ok"], 1)
                dve.wait_ge(S["fl_ok"], 4 * t + 1)
                ts(dall[:], dct[:], DI - 0.5, None, ALU.is_gt).then_inc(S["fl_ok"], 1)
                ts(live[0:1, d:d + 1], dct[0:1, :], DI - 0.5, None, ALU.is_le).then_inc(S["fl_ok"], 1)
                dve.wait_ge(S["fl_ok"], 4 * t + 2)
                ts(smask[:], smask0[:], dall[0:NS, :], None, ALU.mult).then_inc(S["fl_ok"], 1)

            def softplus(t, d):
                for m in range(MD):
                    dve.wait_ge(S["y_ok"], MD * t + m + 1)
                    ts(wk[:, m, :], y[:, m, :], 1.0, 1.0, ALU.min, ALU.add).then_inc(S["w_ok"], 1)
                for m in range(MD):
                    dve.wait_ge(S["w_ok"], MD * t + m + 1)
                    dve.wait_ge(S["l_ok"], MD * t + m + 1)
                    stt(wk[:, m, :], wk[:, m, :], 1.0, lg[:, m, :], ALU.subtract, ALU.subtract).then_inc(S["g_ok"], 1)
                for m in range(MD):
                    dve.wait_ge(S["g_ok"], MD * t + m + 1)
                    stt(wk[:, m, :], y[:, m, :], 1.0, wk[:, m, :], ALU.min, ALU.subtract).then_inc(S["d0_ok"], 1)
                for m in range(MD):
                    dve.wait_ge(S["d0_ok"], MD * t + m + 1)
                    tt(v[:, m, :], v[:, m, :], wk[:, m, :], ALU.max).then_inc(S["dt_ok"], 1)

            def scan(t, d):
                step = slice(None) if d == 0 else slice(None, None, -1)
                for m in range(MD):
                    dve.wait_ge(S["da_ok"], MD * t + m + 1)
                    dve.wait_ge(S["tp_ok"], MD * t + m + 1)
                    nc.vector.tensor_tensor_scan(tp[:, m, step], y[:, m, step], tp[:, m, step], 0.0, ALU.mult, ALU.add
                                                 ).then_inc(S["h_ok"], 1)

            def dead_part(t, d):
                dve.wait_ge(S["s_ps"], t + 1)
                for m in range(MD):
                    tt(qq[:, m, :], v[:, m, :], pss[d][:], ALU.mult).then_inc(S["q_ok"], 1)
                for m in range(MD):
                    dve.wait_ge(S["q_ok"], MD * t + m + 1)
                    stt(qq[:, m, :], qq[:, m, :], dp[d][:, m:m + 1], uc[d][:, m, :], ALU.add, ALU.mult
                        ).then_inc(S["q2_ok"], 1)

            def outputs(t, d):
                for m in range(MD):
                    dve.wait_ge(S["h_ok"], MD * t + m + 1)
                    tt(tp[:, m, :], tp[:, m, :], bb[d][:, 1, :], ALU.mult).then_inc(S["hc_ok"], 1)

            def more_states(t, d):
                wait_apart(dve, S["fl_ok"], 4 * t + 3)
                go = dve.value_load(live[0:1, d:d + 1], min_val=0, max_val=1)
                step = slice(None) if d == 0 else slice(None, None, -1)
                with dve.If(go > 0):
                    with dve.Fori(1, NS) as n:
                        c = dve.snap(dve_count)
                        dve.wait_ge(S["e_bc"], 32 * c + 32)
                        for m in range(MD):
                            at = MD * c + m + 1
                            dve.wait_ge(S["e_y"], at - 1)
                            tt(eh[:], wk[:, m, :], eb[:, 0, :], ALU.mult).then_inc(S["e_tp"], 1)
                            dve.wait_ge(S["e_tp"], at)
                            dve.wait_ge(S["e_da"], at)
                            nc.vector.tensor_tensor_scan(eh[:, step], eda[:, step], eh[:, step], 0.0, ALU.mult, ALU.add
                                                         ).then_inc(S["e_h"], 1)
                            dve.wait_ge(S["e_h"], at)
                            tt(eh[:], eh[:], eb[:, 1, :], ALU.mult).then_inc(S["e_hc"], 1)
                            dve.wait_ge(S["e_hc"], at)
                            dve.wait_ge(S["q2_ok"], MD * (t + 1))
                            tt(qq[:, m, :], qq[:, m, :], eh[:], ALU.add).then_inc(S["e_y"], 1)
                        dve.reg_add(dve_count, dve_count, 1)
                    wait_apart(dve, S["e_y"], dve.snap(dve_count) * MD)
                with dve.Else():
                    dve.nop()

            def sums(t):
                for m in range(MD):
                    dve.wait_ge(S["hc_ok"], MD * t + m + 1)
                    dve.wait_ge(S["q2_ok"], MD * t + m + 1)
                    tt(tp[:, m, :], tp[:, m, :], qq[:, m, :], ALU.add).then_inc(S["yv_ok"], 1)

            def row_var(t):
                dve.wait_ge(S["ss_ps"], t + 1)
                if not (isinstance(t, int) and t == 0):
                    dve.wait_ge(S["fin_ok"], TT * t)
                ts(r2[:], po[1][:, 0:TT], 1.0 / DM, EPS, ALU.mult, ALU.add).then_inc(S["rv_ok"], 1)

            def finish(t, d, s_of):
                dve.wait_ge(S["rr_ok"], t + 1)
                if d == 0:
                    dve.wait_ge(S["h0_ok"], s_of + 1)
                elif not (isinstance(s_of, int) and s_of == 0):
                    dve.wait_ge(S["h1_st"], 16 * s_of)
                if d == 1:
                    dve.wait_ge(S["fin_ok"], TT * t)
                for j in range(TT):
                    bank = po[2] if j < 2 else po[0]
                    dve.wait_ge(S["f_ps"], 2 * t + j // 2 + 1)
                    src, dst = (h0c, h1a) if d == 0 else (h1a, h1o)
                    stt(dst[:, j, :], bank[:, (j % 2) * DM:(j % 2 + 1) * DM], r2[:, j:j + 1], src[:, j, :],
                        ALU.mult, ALU.add).then_inc(S["fin_ok"], 1)

            dve_count = dve.alloc_register("dve_states")
            dve.reg_mov(dve_count, 0)

            ln_stats(0)
            ln_apply(0)
            conv(0, 0)
            bc_product(0, 0)
            dead_test(0, 0)
            dead_mask(0, 0)

            def slots(s, first):
                for d in range(DIRS):
                    t = 2 * s + d
                    softplus(t, d)
                    conv(t + 1, 1 - d)
                    dead_part(t, d)
                    scan(t, d)
                    outputs(t, d)
                    more_states(t, d)
                    if not (first and d == 0):
                        row_var(t - 1)
                    bc_product(t + 1, 1 - d)
                    sums(t)
                    dead_test(t + 1, 1 - d)
                    if not (first and d == 0):
                        finish(t - 1, 1 - d, s if d == 1 else s - 1)
                    if d == 0:
                        ln_stats(s + 1)
                    dead_mask(t + 1, 1 - d)
                    if d == 0:
                        ln_apply(s + 1)

            slots(0, True)
            with dve.Fori(1, NSEQ) as s:
                slots(s, False)
            row_var(2 * NSEQ - 1)
            finish(2 * NSEQ - 1, 1, NSEQ - 1)


NCH = 32
BB = 16
NG = 4
NQ = 4
HD = 16
S_A = 32
NE = 8
TABLES = 7 + NQ * (3 + NG)
NT = NSEQ * SEQ // P
MASKED = -3.0e38


def attention_stage(nc, w, h1_dram, base_dram, xc_dram, lg_all):
    ctx = ExitStack()
    with ctx:
        def sb(name, shape, dt=F32):
            return ctx.enter_context(nc.sbuf_tensor(name, shape, dt))

        wq = sb("a_wq", [P, KD, NQ + 1, P])
        wv = sb("a_wv", [P, KD, NG * HD])
        wp = sb("a_wp", [NG * HD, NQ, DM])
        wr = sb("a_wr", [P, KD, NE])
        lnw = sb("a_lnw", [P, 2, KD])
        lnb = sb("a_lnb", [P, 2, KD])
        ident = sb("a_ident", [P, P])
        cmask = sb("a_cmask", [P, S_A])
        vmask = sb("a_vmask", [P, NG * HD])
        nh = sb("a_nh", [P, TT])

        h1 = sb("a_h1", [P, TT, DM])
        stats = sb("a_stats", [P, TT, 6])
        mv = sb("a_mv", [P, TT, 2])
        ve = sb("a_ve", [P, TT])
        mean = sb("a_mean", [P, (NCH + 2) * TT])
        r1 = sb("a_r1", [P, (NCH + 2) * TT])
        r1s = sb("a_r1s", [P, TT])
        sc = sb("a_sc", [P, TT])
        core = sb("a_core", [P, TT, DM])
        lt = sb("a_lt", [P, KD, SEQ])
        qt = sb("a_qt", [P, BB, NQ, S_A])
        kt = sb("a_kt", [P, SEQ])
        vd = sb("a_vd", [P, TT, 4, NG * HD])
        spread = sb("a_spread", [P, P])
        bmask = sb("a_bmask", [P, 4])
        vb = sb("a_vb", [P, BB, NG * HD])
        ss = sb("a_ss", [P, BB, NG, S_A])
        mx = sb("a_mx", [P, NG, BB])
        sm = sb("a_sm", [P, NG, BB])
        rs = sb("a_rs", [P, NG, BB])
        pt = sb("a_pt", [P, BB, P])
        ao = sb("a_ao", [NG * HD, NQ, SEQ])
        hb = sb("a_hb", [P, TT, DM])
        fi = sb("a_fi", [P, TT, DM])
        hh = sb("a_hh", [P, TT, DM])
        bs = sb("a_bs", [P, TT, DM])
        st2 = sb("a_st2", [P, TT, 6])
        mv2 = sb("a_mv2", [P, TT, 2])
        ve2 = sb("a_ve2", [P, TT])
        rr2 = sb("a_rr2", [P, TT])
        x2 = sb("a_x2", [P, TT, DM])
        x2t = sb("a_x2t", [P, KD, SEQ])

        A = [ctx.enter_context(nc.psum_tensor(f"a_pa{i}", [P, SEQ], F32)) for i in range(4)]
        B = [ctx.enter_context(nc.psum_tensor(f"a_pb{i}", [P, SEQ], F32)) for i in range(4)]

        names = """vv vn_ps vd_ok c0 ld_w ld_h ld_hb bn1 st1 ve1 rq1 v2 sc1 core_ok t1_ps lt_ok qk_ps qk_ok v_ps v_ok s_ps s_ok mx_ok
          sub_ok ex_ok su_ok rc_ok p_ok pt_ps pt_ok av_ps ao_ok pr_ps fi_ok hh_ok bs_ok bn2 st2 ve2 rr2 x2_ok t2_ps x2t_ok
          lg_ps lg_ok st_b st_x""".split()
        S = {n: ctx.enter_context(nc.semaphore("a_" + n)) for n in names}
        block = ctx.enter_context(nc.Block())

        def wait_apart(eng, *waits):
            waits = [(s, v if isinstance(v, int) else eng.to_reg(v)) for s, v in waits]
            eng.wait_ge(S["c0"], 1)
            for semaphore, value in waits:
                if not (isinstance(value, int) and value <= 0):
                    eng.wait_ge(semaphore, value)

        def after(eng, name, value):
            if not (isinstance(value, int) and value <= 0):
                eng.wait_ge(S[name], value)

        h1_v = h1_dram.rearrange("(s b) c -> b s c", s=NSEQ)

        @block.sync
        def _(sp):
            for dst, name in ((wq, "wq"), (wv, "wv"), (wr, "wr")):
                src = w[name].rearrange("(k p) j e -> p k j e", p=P) if name == "wq" else \
                    w[name].rearrange("(k p) e -> p k e", p=P)
                sp.dma_start(dst[:], src).then_inc(S["ld_w"], 16)
            sp.dma_start(wp[:], w["wp"]).then_inc(S["ld_w"], 16)
            sp.dma_start(lnw[:], w["lnw"]).then_inc(S["ld_w"], 16)
            sp.dma_start(lnb[:], w["lnb"]).then_inc(S["ld_w"], 16)

            def load(dst, c, name):
                b0 = c * BB if isinstance(c, int) else (c * BB) % SEQ
                for j in range(TT):
                    sp.dma_start(dst[:, j, :], h1_v[bass.ds(b0 + 4 * j, 4), :, :]).then_inc(S[name], 16)

            load(h1, 0, "ld_h")
            sp.wait_ge(S["core_ok"], TT)
            load(h1, 1, "ld_h")

            def slot(c):
                after(sp, "bs_ok", c)
                load(hb, c, "ld_hb")
                sp.wait_ge(S["core_ok"], TT * (c + 2))
                load(h1, c + 2, "ld_h")
                sp.wait_ge(S["bs_ok"], c + 1)
                for dram, tile, name in ((base_dram, bs, "st_b"), (xc_dram, x2, "st_x")):
                    if name == "st_x":
                        sp.wait_ge(S["x2_ok"], TT * (c + 1))
                    dst = dram[:, bass.ds(c * TT, TT), :]
                    sp.dma_start(dst, tile[:]).then_inc(S[name], 16)

            slot(0)
            with sp.Fori(1, NCH - 1) as c:
                slot(c)
            slot_last = NCH - 1
            after(sp, "bs_ok", slot_last)
            load(hb, slot_last, "ld_hb")
            sp.wait_ge(S["core_ok"], TT * (slot_last + 2))
            load(h1, 1, "ld_h")
            sp.wait_ge(S["bs_ok"], NCH)
            sp.wait_ge(S["x2_ok"], TT * NCH)
            for dram, tile, name in ((base_dram, bs, "st_b"), (xc_dram, x2, "st_x")):
                dst = dram[:, slot_last * TT:NCH * TT, :]
                sp.dma_start(dst, tile[:]).then_inc(S[name], 16)
            sp.wait_ge(S["st_b"], 16 * NCH)
            sp.wait_ge(S["st_x"], 16 * NCH)
            sp.wait_ge(S["ld_h"], 16 * TT * (NCH + 2))

        @block.gpsimd
        def _(pool):
            pool.memset(nh[:], -0.5).then_inc(S["c0"], 1)
            pool.wait_ge(S["c0"], 1)
            done = 1
            for tile in (ident, cmask, vmask, bmask, spread):
                pool.memset(tile[:], 0.0).then_inc(S["c0"], 1)
                done += 1
                pool.wait_ge(S["c0"], done)
            pool.affine_select(out=ident[:], in_=ident[:], compare_op=ALU.not_equal, fill=1.0, base=0,
                               pattern=[[-1, P]], channel_multiplier=1).then_inc(S["c0"], 1)
            pool.wait_ge(S["c0"], done + 1)
            done += 1
            for q in range(NQ):
                rows = slice(S_A * q, S_A * (q + 1))
                pool.affine_select(out=cmask[rows, :], in_=cmask[rows, :], compare_op=ALU.is_ge, fill=MASKED, base=0,
                                   pattern=[[-1, S_A]], channel_multiplier=1).then_inc(S["c0"], 1)
                pool.wait_ge(S["c0"], done + 1)
                pool.memset(vmask[rows, HD * q:HD * (q + 1)], 1.0).then_inc(S["c0"], 1)
                pool.wait_ge(S["c0"], done + 2)
                pool.memset(bmask[rows, q:q + 1], 1.0).then_inc(S["c0"], 1)
                pool.wait_ge(S["c0"], done + 3)
                for n in range(NG):
                    pool.tensor_copy(spread[rows, S_A * n:S_A * (n + 1)], ident[rows, rows]).then_inc(S["c0"], 1)
                    pool.wait_ge(S["c0"], done + 4 + n)
                done += 3 + NG

            def scales1(c):
                wait_apart(pool, (S["st1"], c + 1), (S["core_ok"], TT * c))
                pool.tensor_scalar(ve[:], mv[:, :, 1], 1.0, EPS, ALU.mult, ALU.add).then_inc(S["ve1"], 1)
                pool.wait_ge(S["ve1"], c + 1)
                pool.tensor_tensor(r1s[:], ve[:], nh[:], ALU.pow).then_inc(S["rq1"], 1)

            def scales2(c):
                wait_apart(pool, (S["v2"], c + 1))
                pool.tensor_tensor(sc[:], sc[:], nh[:], ALU.pow).then_inc(S["sc1"], 1)

            def scales3(c):
                wait_apart(pool, (S["st2"], c + 1), (S["x2_ok"], TT * c))
                pool.tensor_scalar(ve2[:], mv2[:, :, 1], 1.0, EPS, ALU.mult, ALU.add).then_inc(S["ve2"], 1)
                pool.wait_ge(S["ve2"], c + 1)
                pool.tensor_tensor(rr2[:], ve2[:], nh[:], ALU.pow).then_inc(S["rr2"], 1)

            def subtract_max(c):
                for g in range(NG):
                    pool.wait_ge(S["mx_ok"], NG * c + g + 1)
                    pool.tensor_tensor(ss[:, :, g, :], ss[:, :, g, :], mx[:, g, :].unsqueeze(2).to_broadcast([P, BB, S_A]),
                                       ALU.subtract).then_inc(S["sub_ok"], 1)

            def normalise(c):
                for g in range(NG):
                    pool.wait_ge(S["rc_ok"], NG * c + g + 1)
                    pool.tensor_tensor(ss[:, :, g, :], ss[:, :, g, :], rs[:, g, :].unsqueeze(2).to_broadcast([P, BB, S_A]),
                                       ALU.mult).then_inc(S["p_ok"], 1)

            def base(c):
                pool.wait_ge(S["hh_ok"], 2 * (c + 1))
                after(pool, "st_b", 16 * c)
                pool.tensor_tensor(bs[:], hh[:], hb[:], ALU.add).then_inc(S["bs_ok"], 1)

            for c in range(2):
                scales1(c)
                scales2(c)

            def slot(c):
                subtract_max(c)
                normalise(c)
                scales1(c + 2)
                scales2(c + 2)
                base(c)
                scales3(c)

            slot(0)
            with pool.Fori(1, NCH) as c:
                slot(c)

        @block.scalar
        def _(act):
            act.wait_ge(S["ld_w"], 16 * 6)

            def lt_copy(c):
                for k in range(KD):
                    act.wait_ge(S["t1_ps"], KD * c + k + 1)
                    act.activation(lt[:, k, :], B[k][:], ACT.Identity, bias=lnb[:, 0, k:k + 1],
                                   scale=lnw[:, 0, k:k + 1]).then_inc(S["lt_ok"], 1)

            def qk_copy(c):
                for q in range(NQ + 1):
                    act.wait_ge(S["qk_ps"], (NQ + 1) * c + q + 1)
                    after(act, "s_ps", NG * c)
                    src = B[q % 2][:]
                    dst = kt[:] if q == NQ else qt[:, :, q, :]
                    act.activation(dst, src if q == NQ else src.rearrange("p (b s) -> p b s", b=BB), ACT.Copy
                                   ).then_inc(S["qk_ok"], 1)

            def exps(c):
                for g in range(NG):
                    act.wait_ge(S["sub_ok"], NG * c + g + 1)
                    act.activation(ss[:, :, g, :], ss[:, :, g, :], ACT.Exp, scale=HD ** -0.5).then_inc(S["ex_ok"], 1)

            def pt_copy(c):
                for i in range(4):
                    act.wait_ge(S["pt_ps"], 4 * c + i + 1)
                    after(act, "av_ps", 4 * c)
                    act.activation(pt[:, 4 * i:4 * i + 4, :], A[i][:].rearrange("p (b n) -> p b n", b=4), ACT.Copy
                                   ).then_inc(S["pt_ok"], 1)

            def ao_copy(c):
                for i in range(4):
                    act.wait_ge(S["av_ps"], 4 * c + i + 1)
                    after(act, "pr_ps", 2 * c)
                    src = B[i][0:NG * HD, :].rearrange("p (b q s) -> p b q s", b=4, q=NQ)
                    dst = ao[:, :, i * P:(i + 1) * P].rearrange("p q (b s) -> p b q s", b=4)
                    act.activation(dst, src, ACT.Copy).then_inc(S["ao_ok"], 1)

            def x2t_copy(c):
                for k in range(KD):
                    act.wait_ge(S["t2_ps"], KD * c + k + 1)
                    after(act, "lg_ps", c)
                    act.activation(x2t[:, k, :], A[2 + k][:], ACT.Identity, bias=lnb[:, 1, k:k + 1],
                                   scale=lnw[:, 1, k:k + 1]).then_inc(S["x2t_ok"], 1)

            lt_copy(0)
            qk_copy(0)
            act.wait_ge(S["v_ps"], 2)
            lt_copy(1)

            def slot(c):
                qk_copy(c + 1)
                exps(c)
                pt_copy(c)
                ao_copy(c)
                act.wait_ge(S["v_ps"], 2 * (c + 2))
                lt_copy(c + 2)
                x2t_copy(c)

            slot(0)
            with act.Fori(1, NCH) as c:
                slot(c)

        @block.tensor
        def _(pe):
            mm = nc.tensor.matmul
            pe.wait_ge(S["ld_w"], 16 * 6)
            pe.wait_ge(S["c0"], TABLES)

            def turn1(c):
                pe.wait_ge(S["core_ok"], TT * (c + 1))
                for k in range(KD):
                    if k == 0:
                        after(pe, "ao_ok", 4 * (c - 1))
                        after(pe, "qk_ok", (NQ + 1) * c)
                    for j in range(TT):
                        i = nc.tensor.transpose(B[k][:, j * P:(j + 1) * P], core[:, j, k * P:(k + 1) * P], ident[:])
                    i.then_inc(S["t1_ps"], 1)

            def qk(c):
                pe.wait_ge(S["lt_ok"], KD * (c + 1))
                for q in range(NQ + 1):
                    if q >= 2:
                        pe.wait_ge(S["qk_ok"], (NQ + 1) * c + q - 1)
                    elif q == 0:
                        after(pe, "lg_ok", c - 1)
                    for k in range(KD):
                        i = mm(B[q % 2][:], wq[:, k, q, :], lt[:, k, :], start=(k == 0), stop=(k == KD - 1))
                    i.then_inc(S["qk_ps"], 1)

            def values(c):
                after(pe, "pt_ok", 4 * c)
                for j in range(TT):
                    for k in range(KD):
                        n = mm(A[2][:, j * 64:(j + 1) * 64], lt[:, k, j * P:(j + 1) * P], wv[:, k, :],
                               start=(k == 0), stop=(k == KD - 1))
                n.then_inc(S["vn_ps"], 1)
                for i in range(2):
                    pe.wait_ge(S["vd_ok"], TT * c + 2 * i + 2)
                    for jj in range(2):
                        n = mm(A[i][:, jj * 256:(jj + 1) * 256], spread[:],
                               vd[:, 2 * i + jj, :, :].rearrange("p b n -> p (b n)"), start=True, stop=True)
                    n.then_inc(S["v_ps"], 1)

            def scores(c):
                pe.wait_ge(S["qk_ok"], (NQ + 1) * (c + 1))
                pe.wait_ge(S["v_ok"], 2 * (c + 1))
                after(pe, "x2t_ok", KD * c)
                for g in range(NG):
                    rows = slice(32 * g, 32 * g + HD)
                    for b in range(BB):
                        i = mm(A[g][:, b * S_A:(b + 1) * S_A], qt[rows, b, :, :].rearrange("p q s -> p (q s)"),
                               kt[rows, b * S_A:(b + 1) * S_A], start=True, stop=True)
                    i.then_inc(S["s_ps"], 1)

            def turn_p(c):
                pe.wait_ge(S["p_ok"], NG * (c + 1))
                for i in range(4):
                    for b in range(4):
                        n = nc.tensor.transpose(A[i][:, b * P:(b + 1) * P],
                                                ss[:, 4 * i + b, :, :].rearrange("p g t -> p (g t)"), ident[:])
                    n.then_inc(S["pt_ps"], 1)

            def products(c):
                for i in range(4):
                    pe.wait_ge(S["pt_ok"], 4 * c + i + 1)
                    if i < 2:
                        pe.wait_ge(S["qk_ok"], (NQ + 1) * (c + 2))
                    else:
                        after(pe, "hh_ok", 2 * c)
                    for b in range(4):
                        n = mm(B[i][0:NG * HD, b * P:(b + 1) * P], vb[:, 4 * i + b, :], pt[:, 4 * i + b, :],
                               start=True, stop=True)
                    n.then_inc(S["av_ps"], 1)

            def project(c):
                pe.wait_ge(S["ao_ok"], 4 * (c + 1))
                for i in range(2):
                    for jj in range(2):
                        j = 2 * i + jj
                        for q in range(NQ):
                            n = mm(B[2 + i][:, jj * DM:(jj + 1) * DM], ao[:, q, j * P:(j + 1) * P], wp[:, q, :],
                                   start=(q == 0), stop=(q == NQ - 1))
                    n.then_inc(S["pr_ps"], 1)

            def turn2(c):
                pe.wait_ge(S["x2_ok"], TT * (c + 1))
                pe.wait_ge(S["pt_ok"], 4 * (c + 1))
                for k in range(KD):
                    for j in range(TT):
                        i = nc.tensor.transpose(A[2 + k][:, j * P:(j + 1) * P], x2[:, j, k * P:(k + 1) * P], ident[:])
                    i.then_inc(S["t2_ps"], 1)

            def router(c):
                pe.wait_ge(S["x2t_ok"], KD * (c + 1))
                pe.wait_ge(S["lt_ok"], KD * (c + 3))
                for j in range(TT):
                    for k in range(KD):
                        i = mm(B[0][:, j * NE:(j + 1) * NE], x2t[:, k, j * P:(j + 1) * P], wr[:, k, :],
                               start=(k == 0), stop=(k == KD - 1))
                i.then_inc(S["lg_ps"], 1)

            turn1(0)
            qk(0)
            values(0)
            turn1(1)

            def slot(c):
                scores(c)
                qk(c + 1)
                turn_p(c)
                products(c)
                values(c + 1)
                project(c)
                turn1(c + 2)
                turn2(c)
                router(c)

            slot(0)
            with pe.Fori(1, NCH) as c:
                slot(c)

        @block.vector
        def _(dve):
            tt, ts, stt = nc.vector.tensor_tensor, nc.vector.tensor_scalar, nc.vector.scalar_tensor_tensor

            def front(c):
                dve.wait_ge(S["ld_h"], 16 * TT * (c + 1))
                for j in range(TT):
                    i = nc.vector.bn_stats(stats[:, j, :], h1[:, j, :])
                i.then_inc(S["bn1"], 1)
                wait_apart(dve, (S["bn1"], c + 1))
                for j in range(TT):
                    i = nc.vector.bn_aggr(mv[:, j, :], stats[:, j, :])
                i.then_inc(S["st1"], 1)
                dve.wait_ge(S["st1"], c + 1)
                cols = bass.ds(c * TT, TT)
                nc.vector.tensor_copy(mean[:, cols], mv[:, :, 0])
                dve.wait_ge(S["rq1"], c + 1)
                nc.vector.tensor_copy(r1[:, cols], r1s[:])
                tt(sc[:], mv[:, :, 1], r1s[:], ALU.mult).then_inc(S["vv"], 1)
                dve.wait_ge(S["vv"], 3 * c + 1)
                tt(sc[:], sc[:], r1s[:], ALU.mult).then_inc(S["vv"], 1)
                dve.wait_ge(S["vv"], 3 * c + 2)
                ts(sc[:], sc[:], EPS, None, ALU.add).then_inc(S["v2"], 1)
                dve.wait_ge(S["sc1"], c + 1)
                tt(sc[:], sc[:], r1s[:], ALU.mult).then_inc(S["vv"], 1)
                dve.wait_ge(S["vv"], 3 * c + 3)
                after(dve, "t1_ps", KD * c)
                for j in range(TT):
                    ts(core[:, j, :], h1[:, j, :], mv[:, j, 0:1], sc[:, j:j + 1], ALU.subtract, ALU.mult
                       ).then_inc(S["core_ok"], 1)

            def v_parts(c):
                dve.wait_ge(S["vn_ps"], c + 1)
                after(dve, "v_ps", 2 * c)
                for j in range(TT):
                    tt(vd[:, j, :, :], A[2][:, j * 64:(j + 1) * 64].unsqueeze(1).to_broadcast([P, 4, NG * HD]),
                       bmask[:].unsqueeze(2).to_broadcast([P, 4, NG * HD]), ALU.mult).then_inc(S["vd_ok"], 1)

            def v_copy(c):
                for i in range(2):
                    dve.wait_ge(S["v_ps"], 2 * c + i + 1)
                    after(dve, "av_ps", 4 * c)
                    tt(vb[:, 8 * i:8 * i + 8, :], A[i][:].rearrange("p (b n) -> p b n", b=8),
                       vmask[:].unsqueeze(1).to_broadcast([P, 8, NG * HD]), ALU.mult).then_inc(S["v_ok"], 1)

            def maxima(c):
                for g in range(NG):
                    dve.wait_ge(S["s_ps"], NG * c + g + 1)
                    after(dve, "pt_ps", 4 * c)
                    tt(ss[:, :, g, :], A[g][:].rearrange("p (b t) -> p b t", b=BB),
                       cmask[:].unsqueeze(1).to_broadcast([P, BB, S_A]), ALU.add).then_inc(S["s_ok"], 1)
                for g in range(NG):
                    dve.wait_ge(S["s_ok"], NG * c + g + 1)
                    nc.vector.tensor_reduce(mx[:, g, :], ss[:, :, g, :], AX_X, ALU.max).then_inc(S["mx_ok"], 1)

            def sums(c):
                for g in range(NG):
                    dve.wait_ge(S["ex_ok"], NG * c + g + 1)
                    nc.vector.tensor_reduce(sm[:, g, :], ss[:, :, g, :], AX_X, ALU.add).then_inc(S["su_ok"], 1)
                for g in range(NG):
                    dve.wait_ge(S["su_ok"], NG * c + g + 1)
                    nc.vector.reciprocal(rs[:, g, :], sm[:, g, :]).then_inc(S["rc_ok"], 1)

            def back(c):
                dve.wait_ge(S["ld_hb"], 16 * TT * (c + 1))
                cols = c * TT
                for j in range(TT):
                    ts(fi[:, j, :], hb[:, j, :], mean[:, bass.ds(cols + j, 1)], r1[:, bass.ds(cols + j, 1)],
                       ALU.subtract, ALU.mult).then_inc(S["fi_ok"], 1)
                for i in range(2):
                    dve.wait_ge(S["pr_ps"], 2 * c + i + 1)
                    dve.wait_ge(S["fi_ok"], TT * (c + 1))
                    after(dve, "bs_ok", c)
                    tt(hh[:, 2 * i:2 * i + 2, :], B[2 + i][:].rearrange("p (j e) -> p j e", j=2),
                       fi[:, 2 * i:2 * i + 2, :], ALU.add).then_inc(S["hh_ok"], 1)
                for j in range(TT):
                    dve.wait_ge(S["hh_ok"], 2 * c + j // 2 + 1)
                    i = nc.vector.bn_stats(st2[:, j, :], hh[:, j, :])
                i.then_inc(S["bn2"], 1)
                wait_apart(dve, (S["bn2"], c + 1))
                for j in range(TT):
                    i = nc.vector.bn_aggr(mv2[:, j, :], st2[:, j, :])
                i.then_inc(S["st2"], 1)
                dve.wait_ge(S["rr2"], c + 1)
                after(dve, "st_x", 16 * c)
                after(dve, "t2_ps", KD * c)
                for j in range(TT):
                    ts(x2[:, j, :], hh[:, j, :], mv2[:, j, 0:1], rr2[:, j:j + 1], ALU.subtract, ALU.mult
                       ).then_inc(S["x2_ok"], 1)

            def route(c):
                dve.wait_ge(S["lg_ps"], c + 1)
                nc.vector.tensor_copy(lg_all[:, bass.ds(c * TT, TT), :],
                                      B[0][:, 0:TT * NE].rearrange("p (j e) -> p j e", j=TT)).then_inc(S["lg_ok"], 1)

            dve.wait_ge(S["c0"], TABLES)
            front(0)
            v_parts(0)
            v_copy(0)
            front(1)

            def slot(c):
                maxima(c)
                if not (isinstance(c, int) and c == 0):
                    route(c - 1)
                sums(c)
                front(c + 2)
                v_parts(c + 1)
                v_copy(c + 1)
                back(c)

            slot(0)
            with dve.Fori(1, NCH) as c:
                slot(c)
            route(NCH - 1)


NTILE = NSEQ * SEQ // P
TOP = 2
FF = 512
MF = FF // P
CAP = -(-NSEQ * SEQ * TOP * 5 // (NE * 4))
HALF = 256
HT = HALF // P
PAIR = 2 * HALF
CAP_ROWS = CAP + PAIR
MAX_PAIRS = -(-CAP // PAIR)
NOWHERE = float(1 << 20)
GT = 4
NGT = NTILE // GT


def routing_stage(nc, lg_all, dst_row, src_row, prob, plan):
    ctx = ExitStack()
    with ctx:
        def sb(name, shape, dt=F32):
            return ctx.enter_context(nc.sbuf_tensor(name, shape, dt))

        block_shape = [P, NTILE, NE]
        ident = sb("r_ident", [P, P])
        same = sb("r_same", [P, P])
        later = sb("r_later", [P, P])
        below = sb("r_below", [P, P])
        ones = sb("r_ones", [P, P])
        expert = sb("r_expert", [P, NE])
        row0 = sb("r_row0", [P, NE])
        steps = sb("r_steps", [1, MAX_PAIRS - 1])
        m = sb("r_m", [P, TOP, NTILE])
        pick = sb("r_pick", [P, NTILE])
        flag = sb("r_flag", block_shape)
        rest = sb("r_rest", block_shape)
        hot = [sb(f"r_hot{k}", block_shape) for k in range(TOP)]
        both = sb("r_both", block_shape)
        rank = sb("r_rank", block_shape)
        total = sb("r_total", [P, NE])
        dst = sb("r_dst", [P, TOP, NTILE])
        keep = sb("r_keep", [P, TOP, NTILE])
        kdst = sb("r_kdst", [P, TOP, NTILE])
        ex = sb("r_ex", [P, NTILE])
        count = sb("r_count", [1, NE])
        over = sb("r_over", [1, NE, MAX_PAIRS - 1])
        planf = sb("r_planf", [1, 2, NE])
        ps_same = [ctx.enter_context(nc.psum_tensor(f"r_ps{i}", [P, SEQ], F32)) for i in range(2)]
        ps_part = [ctx.enter_context(nc.psum_tensor(f"r_pp{i}", [P, SEQ], F32)) for i in range(2)]
        ps_base = ctx.enter_context(nc.psum_tensor("r_pb", [P, 2, NE], F32))
        S = {n: ctx.enter_context(nc.semaphore("r_" + n)) for n in "tab seq both_ok tot_ok counted ex_ok".split()}
        block = ctx.enter_context(nc.Block())

        @block.gpsimd
        def _(pool):
            n = 0
            for tile, value in ((ident, 0.0), (same, 0.0), (later, 0.0), (below, 0.0), (ones, 1.0)):
                pool.memset(tile[:], value).then_inc(S["tab"], 1)
                n += 1
                pool.wait_ge(S["tab"], n)
            pool.affine_select(out=ident[:], in_=ident[:], compare_op=ALU.not_equal, fill=1.0, base=0,
                               pattern=[[-1, P]], channel_multiplier=1).then_inc(S["tab"], 1)
            n += 1
            pool.wait_ge(S["tab"], n)
            for q in range(4):
                rows = slice(S_A * q, S_A * (q + 1))
                for g in range(4):
                    cols = slice(S_A * g, S_A * (g + 1))
                    pool.tensor_copy(same[rows, cols], ident[rows, rows]).then_inc(S["tab"], 1)
                    n += 1
                    pool.wait_ge(S["tab"], n)
                    if q >= g:
                        pool.tensor_scalar(later[rows, cols], ident[rows, rows], -1.0, None, ALU.mult
                                           ).then_inc(S["tab"], 1)
                        n += 1
                        pool.wait_ge(S["tab"], n)
                    pool.affine_select(out=below[rows, cols], in_=ones[rows, cols], compare_op=ALU.is_gt, fill=0.0,
                                       base=0, pattern=[[1, S_A]], channel_multiplier=-1).then_inc(S["tab"], 1)
                    n += 1
                    pool.wait_ge(S["tab"], n)
            for e in range(NE):
                for tile, value in ((expert, e), (row0, e * CAP_ROWS)):
                    pool.memset(tile[:, e:e + 1], float(value)).then_inc(S["tab"], 1)
                    n += 1
                    pool.wait_ge(S["tab"], n)
            for i in range(MAX_PAIRS - 1):
                pool.memset(steps[:, i:i + 1], float(PAIR * (i + 1))).then_inc(S["tab"], 1)
                n += 1
                pool.wait_ge(S["tab"], n)
            assert n == TABLES_R

        @block.scalar
        def _(act):
            act.wait_ge(S["seq"], 11)
            act.activation(ex[:], ex[:], ACT.Exp).then_inc(S["ex_ok"], 1)

        @block.tensor
        def _(pe):
            pe.wait_ge(S["tab"], TABLES_R)
            pe.wait_ge(S["both_ok"], 1)
            flat = both[:].rearrange("p t e -> p (t e)")
            for i in range(2):
                cols = slice(SEQ * i, SEQ * (i + 1))
                nc.tensor.matmul(ps_same[i][:], same[:], flat[:, cols], start=True, stop=True)
                nc.tensor.matmul(ps_part[i][:], later[:], flat[:, cols], start=True, stop=True)
            pe.wait_ge(S["tot_ok"], 1)
            nc.tensor.matmul(ps_base[:, 0, :], below[:], total[:], start=True, stop=True)
            nc.tensor.matmul(ps_base[:, 1, :], ones[:], total[:], start=True, stop=True).then_inc(S["counted"], 1)

        @block.vector
        def _(dve):
            tt, ts, stt = nc.vector.tensor_tensor, nc.vector.tensor_scalar, nc.vector.scalar_tensor_tensor
            dve.wait_ge(S["tab"], TABLES_R)

            def per_expert(row):
                return row[:].unsqueeze(1).to_broadcast(block_shape)

            def per_token(col):
                return col.unsqueeze(2).to_broadcast(block_shape)

            n = 0
            for k in range(TOP):
                src = lg_all if k == 0 else rest
                nc.vector.tensor_reduce(m[:, k, :], src[:], AX_X, ALU.max).then_inc(S["seq"], 1)
                n += 1
                dve.wait_ge(S["seq"], n)
                tt(flag[:], src[:], per_token(m[:, k, :]), ALU.is_lt).then_inc(S["seq"], 1)
                n += 1
                dve.wait_ge(S["seq"], n)
                stt(flag[:], flag[:], float(NE), per_expert(expert), ALU.mult, ALU.add).then_inc(S["seq"], 1)
                n += 1
                dve.wait_ge(S["seq"], n)
                nc.vector.tensor_reduce(pick[:], flag[:], AX_X, ALU.min).then_inc(S["seq"], 1)
                n += 1
                dve.wait_ge(S["seq"], n)
                if k == 1:
                    tt(ex[:], m[:, 1, :], m[:, 0, :], ALU.subtract).then_inc(S["seq"], 1)
                    n += 1
                tt(hot[k][:], per_expert(expert), per_token(pick[:]), ALU.is_equal).then_inc(S["seq"], 1)
                n += 1
                dve.wait_ge(S["seq"], n)
                if k == 0:
                    stt(rest[:], hot[0][:], MASKED, lg_all[:], ALU.mult, ALU.add).then_inc(S["seq"], 1)
                    n += 1
                    dve.wait_ge(S["seq"], n)
            tt(both[:], hot[0][:], hot[1][:], ALU.add).then_inc(S["both_ok"], 1)
            dve.wait_ge(S["both_ok"], 1)
            nc.vector.tensor_reduce(total[:], both[:].rearrange("p t e -> p e t"), AX_X, ALU.add).then_inc(S["tot_ok"], 1)
            dve.wait_ge(S["ex_ok"], 1)
            ts(pick[:], ex[:], 1.0, None, ALU.add).then_inc(S["seq"], 1)
            n += 1
            dve.wait_ge(S["seq"], n)
            nc.vector.reciprocal(m[:, 0, :], pick[:]).then_inc(S["seq"], 1)
            n += 1
            dve.wait_ge(S["seq"], n)
            tt(m[:, 1, :], ex[:], m[:, 0, :], ALU.mult).then_inc(S["seq"], 1)
            n += 1

            dve.wait_ge(S["counted"], 1)
            half = NTILE // 2
            for i in range(2):
                same_v = ps_same[i][:].rearrange("p (t e) -> p t e", e=NE)
                for e in range(NE):
                    start = 0.0 if i == 0 else rank[:, half - 1, e:e + 1]
                    out = rank[:, half * i:half * (i + 1), e]
                    nc.vector.tensor_tensor_scan(out, ones[:, 0:half], same_v[:, :, e], start, ALU.mult, ALU.add
                                                 ).then_inc(S["seq"], 1)
                    n += 1
                dve.wait_ge(S["seq"], n)
            for i in range(2):
                part = ps_part[i][:].rearrange("p (t e) -> p t e", e=NE)
                rows = rank[:, half * i:half * (i + 1), :]
                tt(rows, rows, part, ALU.add).then_inc(S["seq"], 1)
                n += 1
            dve.wait_ge(S["seq"], n)
            tt(rank[:], rank[:], ps_base[:, 0, :].unsqueeze(1).to_broadcast(block_shape), ALU.add).then_inc(S["seq"], 1)
            n += 1
            dve.wait_ge(S["seq"], n)
            ts(flag[:], rank[:], CAP - 0.5, NOWHERE, ALU.is_gt, ALU.mult).then_inc(S["seq"], 1)
            n += 1
            dve.wait_ge(S["seq"], n)
            tt(rank[:], rank[:], flag[:], ALU.add).then_inc(S["seq"], 1)
            n += 1
            dve.wait_ge(S["seq"], n)
            tt(rank[:], rank[:], per_expert(row0), ALU.add).then_inc(S["seq"], 1)
            n += 1
            dve.wait_ge(S["seq"], n)
            for k in range(TOP):
                tt(hot[k][:], hot[k][:], rank[:], ALU.mult).then_inc(S["seq"], 1)
                n += 1
                dve.wait_ge(S["seq"], n)
                nc.vector.tensor_reduce(dst[:, k, :], hot[k][:], AX_X, ALU.add).then_inc(S["seq"], 1)
                n += 1
                dve.wait_ge(S["seq"], n)
            nc.vector.tensor_copy(dst_row[:], dst[:]).then_inc(S["seq"], 1)
            n += 1
            ts(keep[:], dst[:], NOWHERE - 0.5, None, ALU.is_lt).then_inc(S["seq"], 1)
            n += 1
            dve.wait_ge(S["seq"], n)
            tt(kdst[:], dst[:], keep[:], ALU.mult).then_inc(S["seq"], 1)
            n += 1
            dve.wait_ge(S["seq"], n)
            nc.vector.tensor_copy(src_row[:], kdst[:]).then_inc(S["seq"], 1)
            n += 1
            tt(prob[:], m[:], keep[:], ALU.mult).then_inc(S["seq"], 1)
            n += 1

            ts(count[:], ps_base[0:1, 1, :], float(CAP), None, ALU.min).then_inc(S["seq"], 1)
            n += 1
            dve.wait_ge(S["seq"], n)
            shape = [1, NE, MAX_PAIRS - 1]
            tt(over[:], count[:].unsqueeze(2).to_broadcast(shape), steps[:].unsqueeze(1).to_broadcast(shape), ALU.is_gt
               ).then_inc(S["seq"], 1)
            tt(planf[:, 1, :], count[:], row0[0:1, :], ALU.add).then_inc(S["seq"], 1)
            n += 2
            dve.wait_ge(S["seq"], n)
            nc.vector.tensor_reduce(planf[:, 0, :], over[:], AX_X, ALU.add).then_inc(S["seq"], 1)
            n += 1
            dve.wait_ge(S["seq"], n)
            ts(planf[:, 0, :], planf[:, 0, :], 1.0, None, ALU.add).then_inc(S["seq"], 1)
            n += 1
            dve.wait_ge(S["seq"], n)
            nc.vector.tensor_copy(plan[:], planf[:]).then_inc(S["seq"], 1)
            n += 1
            dve.wait_ge(S["seq"], n)


TABLES_R = 6 + 16 + 10 + 16 + 2 * NE + MAX_PAIRS - 1


def dispatch_stage(nc, xc_dram, xd_dram, dst_row, plan):
    ctx = ExitStack()
    with ctx:
        rows = [ctx.enter_context(nc.sbuf_tensor(f"d_rows{i}", [P, GT, DM], F32)) for i in range(2)]
        idx = [ctx.enter_context(nc.sbuf_tensor(f"d_idx{i}", [P, TOP, GT], I32)) for i in range(2)]
        zero = ctx.enter_context(nc.sbuf_tensor("d_zero", [P, PAIR // P, DM], F32))
        names = "ld0 ld1 idx_ok zeroed scat0 scat1 zst".split()
        S = {n: ctx.enter_context(nc.semaphore("d_" + n)) for n in names}
        block = ctx.enter_context(nc.Block())

        @block.sync
        def _(sp):
            def load(g, i):
                sp.dma_start(rows[i][:], xc_dram[:, bass.ds(g * GT, GT), :]).then_inc(S[f"ld{i}"], 16)

            for i in range(2):
                load(i, i)
            sp.wait_ge(S["zeroed"], 1)
            for e in range(NE):
                row = sp.value_load(plan[0:1, 1, e:e + 1], min_val=0, max_val=NE * CAP_ROWS - PAIR)
                sp.dma_start(xd_dram[bass.ds(row, PAIR), :].rearrange("(p j) c -> p j c", p=P), zero[:]
                             ).then_inc(S["zst"], 16)
            with sp.Fori(1, NGT // 2) as h:
                for i in range(2):
                    sp.wait_ge(S[f"scat{i}"], 16 * TOP * GT * h)
                    load(2 * h + i, i)
            sp.wait_ge(S["zst"], 16 * NE)

        @block.gpsimd
        def _(pool):
            pool.memset(zero[:], 0.0).then_inc(S["zeroed"], 1)
            pool.wait_ge(S["zeroed"], 1)

            def step(h, i):
                g = 2 * h + i
                if not isinstance(h, int):
                    pool.wait_ge(S[f"scat{i}"], 16 * TOP * GT * h)
                pool.tensor_copy(idx[i][:], dst_row[:, :, bass.ds(g * GT, GT)]).then_inc(S["idx_ok"], 1)
                pairs = [(S["idx_ok"], g + 1), (S[f"ld{i}"], 16 * (h + 1))]
                pairs = [(s, v if isinstance(v, int) else pool.to_reg(v)) for s, v in pairs]
                pool.wait_ge(S["zeroed"], 1)
                for s, v in pairs:
                    pool.wait_ge(s, v)
                for j in range(GT):
                    for k in range(TOP):
                        pool.indirect_dma_start(out=xd_dram, out_offset=bass.IndirectOffsetOnAxis(
                            ap=idx[i][:, k, j:j + 1].bitcast(U32), axis=0), in_=rows[i][:, j, :], in_offset=None,
                            bounds_check=NE * CAP_ROWS - 1, oob_is_err=False).then_inc(S[f"scat{i}"], 16)

            for i in range(2):
                step(0, i)
            with pool.Fori(1, NGT // 2) as h:
                for i in range(2):
                    step(h, i)
            for i in range(2):
                pool.wait_ge(S[f"scat{i}"], 16 * TOP * GT * NGT // 2)


def expert_stage(nc, w1_dram, w2_dram, lnw_dram, xd_dram, y_dram, plan):
    ctx = ExitStack()
    with ctx:
        def sb(name, shape, dt=F32):
            return ctx.enter_context(nc.sbuf_tensor(name, shape, dt))

        ident = sb("e_ident", [P, P])
        ln = sb("e_ln", [P, 2, KD])
        w1 = [sb(f"e_w1{i}", [P, KD, FF]) for i in range(2)]
        w2 = [sb(f"e_w2{i}", [P, MF, DM]) for i in range(2)]
        x = [sb(f"e_x{i}", [P, HT, DM]) for i in range(2)]
        xt = [sb(f"e_xt{i}", [P, KD, HALF]) for i in range(2)]
        a = [sb(f"e_a{i}", [P, MF, HALF]) for i in range(2)]
        y = [sb(f"e_y{i}", [P, HT, DM]) for i in range(2)]
        zero = sb("e_zero", [P, PAIR // P, DM])
        pt = [ctx.enter_context(nc.psum_tensor(f"e_pt{i}", [P, KD, HALF], F32)) for i in range(2)]
        p1 = [ctx.enter_context(nc.psum_tensor(f"e_p1{i}", [P, 2, HALF], F32)) for i in range(4)]
        p2 = [ctx.enter_context(nc.psum_tensor(f"e_p2{j}", [P, 2, DM], F32)) for j in range(HT)]
        names = "c0 zeroed zst ld_c ld_w0 ld_w1 ld_x0 ld_x1 t_ps xt_ok f1_ps a_ok f2_ps y_ok st0 st1".split()
        S = {n: ctx.enter_context(nc.semaphore("e_" + n)) for n in names}
        block = ctx.enter_context(nc.Block())

        def wait_apart(eng, *waits):
            waits = [(S[s], v if isinstance(v, int) else eng.to_reg(v)) for s, v in waits]
            eng.wait_ge(S["c0"], 1)
            for semaphore, value in waits:
                eng.wait_ge(semaphore, value)

        def experts(eng, name, turn, weights=None, rest=None):
            done = eng.alloc_register(name)
            eng.reg_mov(done, 0)
            with eng.Fori(0, NE // 2) as pair:
                for i in range(2):
                    e = 2 * pair + i
                    turns = eng.value_load(plan[0:1, 0, bass.ds(e, 1)], min_val=1, max_val=MAX_PAIRS)
                    if weights:
                        weights(pair, i, eng.snap(done))
                    with eng.Fori(0, turns) as c:
                        turn(pair, i, c, eng.snap(done))
                        eng.reg_add(done, done, 1)
                    if rest:
                        rest(pair, i, turns)
            return eng.snap(done)

        @block.sync
        def _(sp):
            sp.wait_ge(S["zeroed"], 1)

            def turn(pair, i, c, q):
                for n in range(2):
                    sp.wait_ge(S["t_ps"], 2 * q + n)
                    rows = xd_dram[bass.ds((2 * pair + i) * CAP_ROWS + c * PAIR + n * HALF, HALF), :]
                    sp.dma_start(x[n][:], rows.rearrange("(p j) c -> p j c", p=P)).then_inc(S[f"ld_x{n}"], 16)

            zeros = sp.alloc_register("e_zeros")
            sp.reg_mov(zeros, 0)

            def rest(pair, i, turns):
                with sp.Fori(turns, CAP_ROWS // PAIR) as c:
                    rows = y_dram[bass.ds((2 * pair + i) * CAP_ROWS + c * PAIR, PAIR), :]
                    sp.dma_start(rows.rearrange("(p j) c -> p j c", p=P), zero[:]).then_inc(S["zst"], 16)
                    sp.reg_add(zeros, zeros, 1)

            q = experts(sp, "e_sp", turn, rest=rest)
            sp.wait_ge(S["t_ps"], 2 * q)
            sp.dma_start(x[0][:], xd_dram[0:HALF, :].rearrange("(p j) c -> p j c", p=P)).then_inc(S["ld_x0"], 16)
            wait_apart(sp, ("ld_x0", 16 * q + 16), ("zst", 16 * sp.snap(zeros)))

        @block.gpsimd
        def _(pool):
            pool.memset(zero[:], 0.0).then_inc(S["zeroed"], 1)
            pool.wait_ge(S["zeroed"], 1)
            pool.memset(ident[:], 0.0).then_inc(S["c0"], 1)
            pool.wait_ge(S["c0"], 1)
            pool.affine_select(out=ident[:], in_=ident[:], compare_op=ALU.not_equal, fill=1.0, base=0,
                               pattern=[[-1, P]], channel_multiplier=1).then_inc(S["c0"], 1)
            pool.dma_start(ln[:], lnw_dram).then_inc(S["ld_c"], 16)

            def load_weights(e, i):
                pool.dma_start(w1[i][:], w1_dram[bass.ds(e * DM, DM), :].rearrange("(k p) f -> p k f", p=P)
                               ).then_inc(S[f"ld_w{i}"], 16)
                pool.dma_start(w2[i][:], w2_dram[bass.ds(e * FF, FF), :].rearrange("(m p) c -> p m c", p=P)
                               ).then_inc(S[f"ld_w{i}"], 16)

            load_weights(0, 0)

            def weights(pair, i, q):
                pool.wait_ge(S["f2_ps"], 2 * q)
                load_weights((2 * pair + i + 1) % NE, 1 - i)

            def turn(pair, i, c, q):
                for n in range(2):
                    pool.wait_ge(S["y_ok"], 2 * q + n + 1)
                    rows = y_dram[bass.ds((2 * pair + i) * CAP_ROWS + c * PAIR + n * HALF, HALF), :]
                    pool.dma_start(rows.rearrange("(p j) c -> p j c", p=P), y[n][:]).then_inc(S[f"st{n}"], 16)

            q = experts(pool, "e_pool", turn, weights)
            wait_apart(pool, ("st0", 16 * q), ("st1", 16 * q))
            pool.wait_ge(S["ld_w0"], 32 * (NE // 2 + 1))
            pool.wait_ge(S["ld_w1"], 32 * (NE // 2))

        @block.tensor
        def _(pe):
            mm = nc.tensor.matmul
            pe.nop().then_inc(S["t_ps"], 1)
            pe.wait_ge(S["c0"], 2)

            def turn_rows(q, n):
                pe.wait_ge(S[f"ld_x{n}"], 16 * q + 16)
                pe.wait_ge(S["xt_ok"], 2 * q + n)
                for k in range(KD):
                    for j in range(HT):
                        i = nc.tensor.transpose(pt[n][:, k, j * P:(j + 1) * P], x[n][:, j, k * P:(k + 1) * P], ident[:])
                i.then_inc(S["t_ps"], 1)

            pe.wait_ge(S["ld_x0"], 16)
            for k in range(KD):
                for j in range(HT):
                    i = nc.tensor.transpose(pt[0][:, k, j * P:(j + 1) * P], x[0][:, j, k * P:(k + 1) * P], ident[:])
            i.then_inc(S["t_ps"], 1)

            def turn(pair, i, c, q):
                pe.wait_ge(S[f"ld_w{i}"], 32 * pair + 32)
                for n in range(2):
                    pe.wait_ge(S["xt_ok"], 2 * q + n + 2)
                    for m in range(MF):
                        if m == 0:
                            pe.wait_ge(S["a_ok"], 4 * q + 2 * n)
                        bank = p1[2 * n + m // 2]
                        for k in range(KD):
                            o = mm(bank[:, m % 2, :], w1[i][:, k, m * P:(m + 1) * P], xt[n][:, k, :],
                                   start=(k == 0), stop=(k == KD - 1))
                        if m % 2:
                            o.then_inc(S["f1_ps"], 1)
                    turn_rows(q + n, 1 - n)
                    pe.wait_ge(S["y_ok"], 2 * q + n)
                    for m in range(MF):
                        if m % 2 == 0:
                            pe.wait_ge(S["a_ok"], 4 * q + 2 * n + m // 2 + 1)
                        for j in range(HT):
                            o = mm(p2[j][:, n, :], a[n][:, m, j * P:(j + 1) * P], w2[i][:, m, :],
                                   start=(m == 0), stop=(m == MF - 1))
                    o.then_inc(S["f2_ps"], 1)

            experts(pe, "e_pe", turn)

        @block.scalar
        def _(act):
            act.wait_ge(S["c0"], 1)

            def turn(pair, i, c, q):
                for n in range(2):
                    for b in range(2):
                        act.wait_ge(S["f1_ps"], 4 * q + 2 * n + b + 1)
                        act.wait_ge(S["f2_ps"], 2 * q + n)
                        act.activation(a[n][:, 2 * b:2 * b + 2, :], p1[2 * n + b][:], ACT.Gelu_apprx_tanh
                                       ).then_inc(S["a_ok"], 1)

            experts(act, "e_act", turn)

        @block.vector
        def _(dve):
            ts = nc.vector.tensor_scalar
            dve.wait_ge(S["ld_c"], 16)
            dve.wait_ge(S["c0"], 2)
            dve.nop().then_inc(S["xt_ok"], 1)

            def move(q, n, first=False):
                dve.wait_ge(S["t_ps"], 2 * q + n + 2)
                if not first:
                    dve.wait_ge(S["f1_ps"], 4 * q + 2 * n - 2)
                for k in range(KD):
                    o = ts(xt[n][:, k, :], pt[n][:, k, :], ln[:, 0, k:k + 1], ln[:, 1, k:k + 1], ALU.mult, ALU.add)
                o.then_inc(S["xt_ok"], 1)

            move(0, 0, True)

            def turn(pair, i, c, q):
                for n in range(2):
                    move(q + n, 1 - n)
                    dve.wait_ge(S["f2_ps"], 2 * q + n + 1)
                    dve.wait_ge(S[f"st{n}"], 16 * q)
                    for j in range(HT):
                        o = nc.vector.tensor_copy(y[n][:, j, :], p2[j][:, n, :])
                    o.then_inc(S["y_ok"], 1)

            experts(dve, "e_dve", turn)


def combine_stage(nc, base_dram, y_dram, out, src_row, prob):
    ctx = ExitStack()
    with ctx:
        def sb(name, shape, dt=F32):
            return [ctx.enter_context(nc.sbuf_tensor(f"{name}{i}", shape, dt)) for i in range(2)]

        b, idx, o = sb("o_b", [P, GT, DM]), sb("o_idx", [P, TOP, GT], I32), sb("o_o", [P, GT, DM])
        yr = sb("o_y", [P, TOP, GT, DM])
        names = "c0 ld0 ld1 idx_ok gath0 gath1 part sum st0 st1".split()
        S = {n: ctx.enter_context(nc.semaphore("o_" + n)) for n in names}
        block = ctx.enter_context(nc.Block())
        out_v = out.rearrange("(s b) c -> b s c", s=NSEQ)

        def steps(eng, step):
            for i in range(2):
                step(0, i)
            with eng.Fori(1, NGT // 2) as h:
                for i in range(2):
                    step(h, i)

        @block.sync
        def _(sp):
            def step(h, i):
                g = 2 * h + i
                if not isinstance(h, int):
                    sp.wait_ge(S["part"], GT * (g - 1))
                sp.dma_start(b[i][:], base_dram[:, bass.ds(g * GT, GT), :]).then_inc(S[f"ld{i}"], 16)

            steps(sp, step)
            for i in range(2):
                sp.wait_ge(S[f"ld{i}"], 16 * NGT // 2)

        @block.scalar
        def _(act):
            def step(h, i):
                g = 2 * h + i
                act.wait_ge(S["sum"], GT * (g + 1))
                for j in range(GT):
                    act.dma_start(out_v[bass.ds(g * 4 * GT + 4 * j, 4), :, :], o[i][:, j, :]).then_inc(S[f"st{i}"], 16)

            steps(act, step)
            for i in range(2):
                act.wait_ge(S[f"st{i}"], 16 * GT * NGT // 2)

        @block.gpsimd
        def _(pool):
            pool.nop().then_inc(S["c0"], 1)

            def step(h, i):
                g = 2 * h + i
                if not isinstance(h, int):
                    pool.wait_ge(S[f"gath{i}"], 16 * TOP * GT * h)
                pool.tensor_copy(idx[i][:], src_row[:, :, bass.ds(g * GT, GT)]).then_inc(S["idx_ok"], 1)
                pairs = [(S["idx_ok"], g + 1)] + ([] if isinstance(h, int) else [(S["sum"], GT * (g - 1))])
                pairs = [(s, v if isinstance(v, int) else pool.to_reg(v)) for s, v in pairs]
                pool.wait_ge(S["c0"], 1)
                for s, v in pairs:
                    pool.wait_ge(s, v)
                for j in range(GT):
                    for k in range(TOP):
                        pool.indirect_dma_start(out=yr[i][:, k, j, :], out_offset=None, in_=y_dram,
                                                in_offset=bass.IndirectOffsetOnAxis(
                                                    ap=idx[i][:, k, j:j + 1].bitcast(U32), axis=0)
                                                ).then_inc(S[f"gath{i}"], 16)

            steps(pool, step)

        @block.vector
        def _(dve):
            stt = nc.vector.scalar_tensor_tensor

            def step(h, i):
                g = 2 * h + i
                dve.wait_ge(S[f"ld{i}"], 16 * (h + 1))
                dve.wait_ge(S[f"gath{i}"], 16 * TOP * GT * (h + 1))
                if not isinstance(h, int):
                    dve.wait_ge(S[f"st{i}"], 16 * GT * h)
                for j in range(GT):
                    stt(yr[i][:, 0, j, :], yr[i][:, 0, j, :], prob[:, 0, bass.ds(g * GT + j, 1)], b[i][:, j, :],
                        ALU.mult, ALU.add).then_inc(S["part"], 1)
                for j in range(GT):
                    dve.wait_ge(S["part"], GT * g + j + 1)
                    stt(o[i][:, j, :], yr[i][:, 1, j, :], prob[:, 1, bass.ds(g * GT + j, 1)], yr[i][:, 0, j, :],
                        ALU.mult, ALU.add).then_inc(S["sum"], 1)

            steps(dve, step)


def build(nc, h, out):
    n_rows = NE * CAP_ROWS
    h1_dram = nc.dram_tensor("h1_rows", [NSEQ * SEQ, DM], F32).ap()
    base_dram = nc.dram_tensor("base_rows", [P, NTILE, DM], F32).ap()
    xc_dram = nc.dram_tensor("xc_rows", [P, NTILE, DM], F32).ap()
    xd_dram = nc.dram_tensor("expert_in", [n_rows, DM], F32).ap()
    y_dram = nc.dram_tensor("expert_out", [n_rows, DM], F32).ap()
    mamba_w = [{k[:-1]: v for k, v in h.items() if k.endswith(str(d))} for d in range(DIRS)]
    mamba_stage(nc, h["ids"], h["table"], mamba_w, h1_dram)
    with ExitStack() as ctx:
        dst_row = ctx.enter_context(nc.sbuf_tensor("dst_row", [P, TOP, NTILE], I32))
        src_row = ctx.enter_context(nc.sbuf_tensor("src_row", [P, TOP, NTILE], I32))
        prob = ctx.enter_context(nc.sbuf_tensor("prob", [P, TOP, NTILE], F32))
        plan = ctx.enter_context(nc.sbuf_tensor("plan", [1, 2, NE], I32))
        lg_all = ctx.enter_context(nc.sbuf_tensor("lg_all", [P, NTILE, NE], F32))
        attention_stage(nc, h, h1_dram, base_dram, xc_dram, lg_all)
        routing_stage(nc, lg_all, dst_row, src_row, prob, plan)
        dispatch_stage(nc, xc_dram, xd_dram, dst_row, plan)
        expert_stage(nc, h["moe_w1"], h["moe_w2"], h["ln2"], xd_dram, y_dram, plan)
        combine_stage(nc, base_dram, y_dram, out, src_row, prob)


def per_chunk(v):
    return v.reshape(-1, P).T


def mamba_layout(i):
    out = {}
    for d, suffix in enumerate("fb"):
        def g(name):
            return i[f"L0_attn_{name}_{suffix}"]
        wx = g("Wx")
        out[f"Win{d}"] = g("Win").T
        out[f"Wx{d}"] = np.concatenate([wx[RK:], wx[:RK]]).T
        out[f"Wdt{d}"] = g("Wdt").T
        out[f"Wout{d}"] = g("Wout").T
        out[f"Wfuse{d}"] = i["L0_attn_Wfuse"][:, DM * d:DM * (d + 1)].T
        out[f"convw{d}"] = g("convw")
        out[f"Alog{d}"] = g("Alog")
        for name in ("convb", "bdt", "Dp", "ln_g", "ln_b"):
            out[f"{name}{d}"] = per_chunk(g(name))
    out["bfuse0"] = i["L0_attn_bfuse"].reshape(1, DM)
    return out


def attention_layout(i):
    f = "L0_ffn_"
    w = i[f + "qkv_weight"].reshape(NG, NQ + 2, HD, DM)
    wq = np.zeros((DM, NQ + 1, NG, S_A), w.dtype)
    wq[..., :HD] = w[:, :NQ + 1].transpose(3, 1, 0, 2)
    ln = {n: np.stack([per_chunk(i[f + "ln1_" + n]), per_chunk(i[f + "ln2_" + n])], 1) for n in ("weight", "bias")}
    return dict(
        wq=wq.reshape(DM, NQ + 1, P),
        wv=w[:, NQ + 1].transpose(2, 0, 1).reshape(DM, NG * HD),
        wp=i[f + "proj_weight"].reshape(DM, NG, NQ, HD).transpose(1, 3, 2, 0).reshape(NG * HD, NQ, DM),
        wr=i[f + "router_weight"],
        lnw=ln["weight"],
        lnb=ln["bias"],
        ln2=np.stack([per_chunk(i[f + "ln2_weight"]), per_chunk(i[f + "ln2_bias"])], 1),
        moe_w1=i[f + "moe_w1"].reshape(NE * DM, FF),
        moe_w2=i[f + "moe_w2"].reshape(NE * FF, DM),
    )


def ids_layout(x):
    ids = x.reshape(NSEQ, TT, P).transpose(2, 0, 1).reshape(P, NSEQ * TT)
    return np.concatenate([ids, np.zeros((P, 2 * TT), ids.dtype)], 1)


def kernel(**inputs):
    import concourse.bacc as _bacc
    from concourse.bass_utils import run_bass_kernel_spmd as _run

    i = {k: np.asarray(v) for k, v in inputs.items()}
    arrays = {**mamba_layout(i), **attention_layout(i), "ids": ids_layout(i["x"]), "table": i["L0_tok_W"].T}
    arrays = {k: np.ascontiguousarray(v) for k, v in arrays.items()}
    nc = _bacc.Bacc("TRN2", target_bir_lowering=False, num_devices=1)
    handles = {k: nc.dram_tensor("in_" + k, v.shape, mybir.dt.from_np(v.dtype), kind="ExternalInput").ap()
               for k, v in arrays.items()}
    out = nc.dram_tensor("out", [NSEQ * SEQ, DM], F32, kind="ExternalOutput").ap()
    build(nc, handles, out)
    results = _run(nc, [{"in_" + k: v for k, v in arrays.items()}], core_ids=[0]).results
    return np.asarray(results[0]["out"]).reshape(NSEQ, SEQ, DM)
```

```python
import numpy as np

from contextlib import ExitStack

import concourse.bass as bass
from concourse import mybir

F32 = mybir.dt.float32
F32R = mybir.dt.float32r
I32 = mybir.dt.int32
U32 = mybir.dt.uint32
ALU = mybir.AluOpType
ACT = mybir.ActivationFunctionType
AX_X = mybir.AxisListType.X

P = 128
DM = 256
KD = DM // P
DI = 512
MD = DI // P
NS = 32
RK = 16
NX = 2 * NS + RK
TAPS = 4
SEQ = 512
NSEQ = 32
TT = SEQ // P
PAD = TAPS - 1
EPS = 1e-5
DIRS = 2
LN2 = 0.6931471805599453
PARTS = ((0, 0), (0, 1), (1, 0))
DEAD_LOG = 5.5
ALOG_TOP = 80.0


def mamba_stage(nc, tok_ids, table, w, h1_dram):
    ctx = ExitStack()
    with ctx:
        def sb(name, shape, dt=F32):
            return ctx.enter_context(nc.sbuf_tensor(name, shape, dt))

        def sem(name):
            return ctx.enter_context(nc.semaphore(name))

        win = [[sb(f"win{d}{h}", [P, KD, 2 * DI], F32R) for h in range(2)] for d in range(DIRS)]
        wx = [sb(f"wx{d}", [P, MD, NX]) for d in range(DIRS)]
        wdt = [sb(f"wdt{d}", [P, DI]) for d in range(DIRS)]
        wdta = [sb(f"wdta{d}", [P, DI]) for d in range(DIRS)]
        wout = [sb(f"wout{d}", [P, MD, DM]) for d in range(DIRS)]
        wfus = [sb(f"wfus{d}", [P, KD, DM]) for d in range(DIRS)]
        convw = [sb(f"convw{d}", [P, MD, TAPS]) for d in range(DIRS)]
        convb = [sb(f"convb{d}", [P, MD]) for d in range(DIRS)]
        bdt = [sb(f"bdt{d}", [P, MD]) for d in range(DIRS)]
        dp = [sb(f"dp{d}", [P, MD]) for d in range(DIRS)]
        amat = [sb(f"amat{d}", [P, MD, NS]) for d in range(DIRS)]
        almin = [sb(f"almin{d}", [P, MD]) for d in range(DIRS)]
        alok = [sb(f"alok{d}", [P, MD]) for d in range(DIRS)]
        alb = [sb(f"alb{d}", [P, MD]) for d in range(DIRS)]
        lng = [sb(f"lng{d}", [P, KD]) for d in range(DIRS)]
        lnb = [sb(f"lnb{d}", [P, KD]) for d in range(DIRS)]
        bfus = sb("bfus", [1, DM])
        wmean = sb("wmean", [P, DIRS, MD])
        cvec = sb("cvec", [P, DM])
        ident = sb("ident", [P, P])
        ones = sb("ones", [P, P])
        neg_half = sb("neg_half", [P, TT])
        smask0 = sb("smask0", [NS, P])

        ids = sb("ids", [P, (NSEQ + 2) * TT], I32)
        idc = sb("idc", [P, TT], I32)
        g = sb("g", [P, TT, DM])
        stats = sb("stats", [P, TT, 6])
        mv = sb("mv", [P, TT, 2])
        rstd = sb("rstd", [P, TT])
        xn = sb("xn", [P, TT, DM])
        xt = [sb(f"xt{h}", [P, KD, SEQ], F32R) for h in range(2)]
        h0c = sb("h0c", [P, 2, TT, DM])
        h1o = sb("h1o", [P, TT, DM])
        u = sb("u", [P, MD, SEQ + 2 * PAD])
        uc = [sb(f"uc{d}", [P, MD, SEQ]) for d in range(DIRS)]
        zs = [sb(f"zs{d}", [P, MD, SEQ]) for d in range(DIRS)]
        xd = [sb(f"xd{d}", [P, SEQ]) for d in range(DIRS)]
        bcp = sb("bcp", [NS, SEQ])
        bb = [sb(f"bb{d}", [P, 2, SEQ]) for d in range(DIRS)]
        v = sb("v", [P, MD, SEQ])
        y = sb("y", [P, MD, SEQ])
        lg = sb("lg", [P, MD, SEQ])
        wk = sb("wk", [P, MD, SEQ])
        yz = sb("yz", [P, MD, SEQ])
        qq = sb("qq", [P, MD, SEQ])
        tp = sb("tp", [P, MD, SEQ])
        fo = sb("fo", [P, KD, SEQ])
        sq = sb("sq", [P, KD, SEQ])
        r2 = sb("r2", [P, TT])
        r3 = sb("r3", [P, TT])
        xmax = sb("xmax", [P, 1])
        dgt = sb("dgt", [P, MD])
        dct = sb("dct", [P, 1])
        dall = sb("dall", [P, 1])
        live = sb("live", [P, DIRS], I32)
        smask = sb("smask", [NS, P])
        eh = sq[:, 0, :]

        pj = [ctx.enter_context(nc.psum_tensor(f"pj{i}", [P, SEQ], F32)) for i in range(2)]
        px = ctx.enter_context(nc.psum_tensor("px", [P, SEQ], F32))
        pss = [ctx.enter_context(nc.psum_tensor(f"pss{i}", [P, SEQ], F32)) for i in range(DIRS)]
        po = [ctx.enter_context(nc.psum_tensor(f"po{i}", [P, SEQ], F32)) for i in range(3)]

        bc_dram = [nc.dram_tensor(f"bc{d}", [2 * NS, SEQ], F32).ap() for d in range(DIRS)]

        names = """c_tab cv xl_ok ld_w ld_ids prep_a prep_w prep_v idc_ok gath st_ok lnv_ok lnr_ok xn_ok xt_ps xt_ok h0_ok
          u_ps u_ok a_ok z_ps z_ok uc_ok xd_ps xd_ok bc_ok bcast xd_st dt_ps v_ok vc_ok y_ok l_ok w_ok g_ok
          d0_ok dt_ok dtu_ok tp_ok da_ok h_ok hc_ok q_ok q2_ok yv_ok yz_ok xm_ok qd_ps gt_ok ct_ok cnt_ps
          fl_ok s_ps o_ps fo_ok sq_ok ss_ps rv_ok rr_ok f_ps fin_ok h1_st gt2 e_bc e_da e_tp e_h e_hc e_y""".split()
        S = {n: sem("m_" + n) for n in names}

        block = ctx.enter_context(nc.Block())

        def wait_apart(eng, semaphore, value):
            value = value if isinstance(value, int) else eng.to_reg(value)
            eng.wait_ge(S["c_tab"], 1)
            eng.wait_ge(semaphore, value)

        def last_tap(m):
            return 6 * (m // 2) + 5 + m % 2

        def xd_rows(d):
            return xd[d][2 * NS:NX, :]

        @block.sync
        def _(sp):
            for d in range(DIRS):
                k = w[d]
                stage = (v, lg)[d][:].rearrange("p m n -> p (m n)").rearrange("p (k e) -> p k e", k=KD)
                sp.dma_start(stage, k["Win"].rearrange("(k p) e -> p k e", p=P)).then_inc(S["ld_w"], 16)
                sp.dma_start(wx[d][:], k["Wx"].rearrange("(m p) e -> p m e", p=P)).then_inc(S["ld_w"], 16)
                sp.dma_start(wdt[d][2 * NS:NX, :], k["Wdt"]).then_inc(S["ld_w"], 16)
                sp.dma_start(wout[d][:], k["Wout"].rearrange("(m p) e -> p m e", p=P)).then_inc(S["ld_w"], 16)
                sp.dma_start(wfus[d][:], k["Wfuse"].rearrange("(k p) e -> p k e", p=P)).then_inc(S["ld_w"], 16)
                sp.dma_start(convw[d][:], k["convw"].rearrange("(m p) e -> p m e", p=P)).then_inc(S["ld_w"], 16)
                sp.dma_start(amat[d][:], k["Alog"].rearrange("(m p) e -> p m e", p=P)).then_inc(S["ld_w"], 16)
                for dst, name in ((convb, "convb"), (bdt, "bdt"), (dp, "Dp"), (lng, "ln_g"), (lnb, "ln_b")):
                    sp.dma_start(dst[d][:], k[name]).then_inc(S["ld_w"], 16)
                if d == 0:
                    sp.dma_start(bfus[:], k["bfuse"]).then_inc(S["ld_w"], 16)
            sp.dma_start(ids[:], tok_ids).then_inc(S["ld_ids"], 16)

            def broadcast(t, d):
                if not (isinstance(t, int) and t < 2):
                    wait_apart(sp, S["hc_ok"], MD * (t - 1))
                wait_apart(sp, S["xd_ok"], t + 1)
                sp.dma_start(bc_dram[d], xd[d][0:2 * NS, :]).then_inc(S["xd_st"], 16)
                sp.wait_ge(S["xd_st"], 16 * (t + 1))
                sp.dma_start(bb[d][:], bc_dram[d][0:2 * NS:NS, :].partition_broadcast(P)).then_inc(S["bcast"], 16)

            def store(s):
                sp.wait_ge(S["fin_ok"], TT * (2 * s + 2))
                dst = h1_dram[bass.ds(s * SEQ, SEQ), :].rearrange("(j p) c -> p j c", p=P)
                sp.dma_start(dst, h1o[:]).then_inc(S["h1_st"], 16)

            def more_states(t, d):
                wait_apart(sp, S["fl_ok"], 4 * t + 3)
                go = sp.value_load(live[0:1, d:d + 1], min_val=0, max_val=1)
                with sp.If(go > 0):
                    with sp.Fori(1, NS) as n:
                        c = sp.snap(sp_count)
                        if not (isinstance(t, int) and t == 0):
                            sp.wait_ge(S["hc_ok"], MD * t)
                        wait_apart(sp, S["e_y"], c * MD + 1)
                        for i in range(2):
                            row = bc_dram[d][bass.ds(n + NS * i, 1), :].squeeze(0)
                            sp.dma_start(bb[1 - d][:, i, :], row.partition_broadcast(P)).then_inc(S["e_bc"], 16)
                        sp.reg_add(sp_count, sp_count, 1)
                    wait_apart(sp, S["e_y"], sp.snap(sp_count) * MD + 1)
                with sp.Else():
                    sp.nop()

            sp_count = sp.alloc_register("sp_states")
            sp.reg_mov(sp_count, 0)
            broadcast(0, 0)

            def slots(s, first):
                for d in range(DIRS):
                    t = 2 * s + d
                    more_states(t, d)
                    broadcast(t + 1, 1 - d)
                    if d == 1 and not first:
                        store(s - 1)

            slots(0, True)
            with sp.Fori(1, NSEQ) as s:
                slots(s, False)
            store(NSEQ - 1)
            sp.wait_ge(S["h1_st"], 16 * NSEQ)
            sp.wait_ge(S["bcast"], 16 * (2 * NSEQ + 1))

        @block.gpsimd
        def _(pool):
            pool.memset(ones[:], 1.0).then_inc(S["c_tab"], 1)
            pool.wait_ge(S["c_tab"], 1)
            pool.memset(neg_half[:], -0.5).then_inc(S["c_tab"], 1)
            pool.wait_ge(S["c_tab"], 2)
            pool.memset(u[:, :, 0:PAD], 0.0).then_inc(S["c_tab"], 1)
            pool.wait_ge(S["c_tab"], 3)
            pool.memset(u[:, :, PAD + SEQ:], 0.0).then_inc(S["c_tab"], 1)
            pool.wait_ge(S["c_tab"], 4)
            pool.memset(ident[:], 0.0).then_inc(S["c_tab"], 1)
            pool.wait_ge(S["c_tab"], 5)
            pool.affine_select(out=ident[:], in_=ident[:], compare_op=ALU.not_equal, fill=1.0, base=0,
                               pattern=[[-1, P]], channel_multiplier=1).then_inc(S["c_tab"], 1)
            pool.wait_ge(S["c_tab"], 6)
            pool.affine_select(out=smask0[:], in_=ones[0:NS, :], compare_op=ALU.is_gt, fill=0.0, base=0,
                               pattern=[[0, P]], channel_multiplier=1).then_inc(S["c_tab"], 1)
            pool.wait_ge(S["c_tab"], 7)
            pool.wait_ge(S["ld_ids"], 16)

            def gather(s):
                if not (isinstance(s, int) and s == 0):
                    pool.wait_ge(S["gath"], 16 * TT * s)
                    pool.wait_ge(S["xn_ok"], TT * s)
                    pool.wait_ge(S["h0_ok"], s)
                pool.tensor_copy(idc[:], ids[:, bass.ds(s * TT, TT)]).then_inc(S["idc_ok"], 1)
                wait_apart(pool, S["idc_ok"], s + 1)
                for j in range(TT):
                    pool.indirect_dma_start(out=g[:, j, :], out_offset=None, in_=table,
                                            in_offset=bass.IndirectOffsetOnAxis(ap=idc[:, j:j + 1].bitcast(U32), axis=0)
                                            ).then_inc(S["gath"], 16)

            def ln_scale(s):
                wait_apart(pool, S["st_ok"], s + 1)
                pool.tensor_scalar(r3[:], mv[:, :, 1], 1.0, EPS, ALU.mult, ALU.add).then_inc(S["lnv_ok"], 1)
                pool.wait_ge(S["lnv_ok"], s + 1)
                pool.tensor_tensor(rstd[:], r3[:], neg_half[:], ALU.pow).then_inc(S["lnr_ok"], 1)

            def keep_residual(s):
                if not (isinstance(s, int) and s < 2):
                    pool.wait_ge(S["fin_ok"], TT * (2 * s - 2))
                pool.wait_ge(S["prep_v"], 3 * DIRS + 2)
                pool.wait_ge(S["gath"], 16 * TT * (s + 1))
                pool.tensor_tensor(h0c[:, bass.ds(s % 2, 1)].squeeze(1), g[:],
                                   cvec[:].unsqueeze(1).to_broadcast([P, TT, DM]), ALU.add).then_inc(S["h0_ok"], 1)

            def scan_inputs(t, d):
                pool.wait_ge(S["bcast"], 16 * (t + 1))
                for m in range(MD):
                    pool.wait_ge(S["dt_ok"], MD * t + m + 1)
                    pool.tensor_tensor(wk[:, m, :], v[:, m, :], uc[d][:, m, :], ALU.mult).then_inc(S["dtu_ok"], 1)
                    pool.wait_ge(S["dtu_ok"], MD * t + m + 1)
                    if not (isinstance(t, int) and t == 0):
                        pool.wait_ge(S["yv_ok"], MD * (t - 1) + m + 1)
                    pool.tensor_tensor(tp[:, m, :], wk[:, m, :], bb[d][:, 0, :], ALU.mult).then_inc(S["tp_ok"], 1)

            def gate(t, d):
                for m in range(MD):
                    pool.wait_ge(S["yv_ok"], MD * t + m + 1)
                    if not (isinstance(t, int) and t == 0):
                        pool.wait_ge(S["o_ps"], KD * t)
                    pool.tensor_tensor(yz[:, m, :], tp[:, m, :], zs[d][:, m, :], ALU.mult).then_inc(S["yz_ok"], 1)

            def row_scale(t):
                pool.wait_ge(S["ss_ps"], t + 1)
                pool.wait_ge(S["rv_ok"], t + 1)
                if not (isinstance(t, int) and t == 0):
                    pool.wait_ge(S["fin_ok"], TT * t)
                pool.tensor_tensor(r2[:], r2[:], neg_half[:], ALU.pow).then_inc(S["rr_ok"], 1)

            gather(0)
            ln_scale(0)
            keep_residual(0)
            gather(1)
            scan_inputs(0, 0)

            def slots(s, first):
                for d in range(DIRS):
                    t = 2 * s + d
                    if d == 0:
                        ln_scale(s + 1)
                    if not first:
                        row_scale(t - 2)
                    gate(t, d)
                    if d == 1:
                        keep_residual(s + 1)
                        gather(s + 2)
                    scan_inputs(t + 1, 1 - d)

            slots(0, True)
            with pool.Fori(1, NSEQ) as s:
                slots(s, False)
            row_scale(2 * NSEQ - 2)
            row_scale(2 * NSEQ - 1)
            pool.wait_ge(S["gath"], 16 * TT * (NSEQ + 2))

        @block.scalar
        def _(act):
            act.wait_ge(S["ld_w"], 16 * (12 * DIRS + 1))
            for d in range(DIRS):
                act.activation(wdta[d][2 * NS:NX, :], wdt[d][2 * NS:NX, :], ACT.Abs).then_inc(S["prep_a"], 1)
            act.wait_ge(S["prep_v"], 2 * DIRS)
            for d in range(DIRS):
                act.activation(amat[d][:], amat[d][:], ACT.Exp).then_inc(S["prep_a"], 1)
            act.wait_ge(S["prep_a"], 2 * DIRS)
            for d in range(DIRS):
                act.activation(amat[d][:], amat[d][:], ACT.Copy, scale=-1.0).then_inc(S["prep_a"], 1)
            act.wait_ge(S["prep_a"], 3 * DIRS)

            def xt_copy(s):
                for k in range(KD):
                    act.wait_ge(S["xt_ps"], KD * s + k + 1)
                    act.activation(xt[0][:, k, :], pj[k][:], ACT.Copy).then_inc(S["xt_ok"], 1)

            def u_copy(t, d, m):
                tap = TAPS - 1
                act.wait_ge(S["u_ps"], MD * t + m + 1)
                if not (isinstance(t, int) and t == 0):
                    act.wait_ge(S["cv"], PAD * MD * (t - 1) + last_tap(m))
                act.activation(u[:, m, PAD:PAD + SEQ], pj[m % 2][:], ACT.Copy).then_inc(S["u_ok"], 1)
                if not (isinstance(t, int) and t < 2):
                    act.wait_ge(S["q2_ok"], MD * (t - 2) + m + 1)
                    act.wait_ge(S["dtu_ok"], MD * (t - 2) + m + 1)
                act.activation(uc[d][:, m, :], pj[m % 2][:], ACT.Identity, bias=convb[d][:, m:m + 1],
                               scale=convw[d][:, m, tap:tap + 1]).then_inc(S["a_ok"], 1)

            def z_silu(t, d):
                for m in range(MD):
                    act.wait_ge(S["z_ps"], MD * t + m + 1)
                    if not (isinstance(t, int) and t < 2):
                        act.wait_ge(S["yz_ok"], MD * (t - 2) + m + 1)
                    act.activation(zs[d][:, m, :], pj[m % 2][:], ACT.Silu).then_inc(S["z_ok"], 1)

            def uc_silu(t, d):
                for m in range(MD):
                    act.wait_ge(S["cv"], PAD * MD * t + last_tap(m))
                    act.activation(uc[d][:, m, :], uc[d][:, m, :], ACT.Silu).then_inc(S["uc_ok"], 1)

            def xd_copy(t, d):
                act.wait_ge(S["xd_ps"], t + 1)
                if not (isinstance(t, int) and t < 2):
                    act.wait_ge(S["xd_st"], 16 * (t - 1))
                act.activation(xd[d][0:NX, :], px[0:NX, :], ACT.Copy).then_inc(S["xd_ok"], 1)

            def v_copy(t, d):
                for m in range(MD):
                    act.wait_ge(S["dt_ps"], MD * t + m + 1)
                    if not (isinstance(t, int) and t == 0):
                        act.wait_ge(S["q_ok"], MD * (t - 1) + m + 1)
                        act.wait_ge(S["dtu_ok"], MD * (t - 1) + m + 1)
                        act.wait_ge(S["da_ok"], MD * (t - 1) + m + 1)
                    act.activation(v[:, m, :], pj[m % 2][:], ACT.Identity, bias=bdt[d][:, m:m + 1]
                                   ).then_inc(S["v_ok"], 1)
                    if not (isinstance(t, int) and t == 0):
                        act.wait_ge(S["g_ok"], MD * (t - 1) + m + 1)
                    act.activation(lg[:, m, :], pj[m % 2][:], ACT.Abs, bias=bdt[d][:, m:m + 1]
                                   ).then_inc(S["vc_ok"], 1)

            def softplus_exp(t):
                for m in range(MD):
                    act.wait_ge(S["vc_ok"], MD * t + m + 1)
                    if not (isinstance(t, int) and t == 0):
                        act.wait_ge(S["h_ok"], MD * (t - 1) + m + 1)
                    act.activation(y[:, m, :], lg[:, m, :], ACT.Exp, scale=-1.0).then_inc(S["y_ok"], 1)

            def softplus_log(t, m):
                act.wait_ge(S["y_ok"], MD * t + m + 1)
                act.activation(lg[:, m, :], y[:, m, :], ACT.Ln, bias=1.0).then_inc(S["l_ok"], 1)

            def decays(t, d):
                for m in range(MD):
                    act.wait_ge(S["dt_ok"], MD * t + m + 1)
                    act.activation(y[:, m, :], v[:, m, :], ACT.Exp, scale=amat[d][:, m, 0:1]).then_inc(S["da_ok"], 1)

            def project_copies(t):
                for k in range(KD):
                    act.wait_ge(S["o_ps"], KD * t + k + 1)
                    if not (isinstance(t, int) and t == 0):
                        act.wait_ge(S["f_ps"], 2 * t)
                    act.activation(sq[:, k, :], po[k][:], ACT.Square).then_inc(S["sq_ok"], 1)
                    act.activation(fo[:, k, :], po[k][:], ACT.Copy).then_inc(S["fo_ok"], 1)

            def more_states(t, d):
                wait_apart(act, S["fl_ok"], 4 * t + 3)
                go = act.value_load(live[0:1, d:d + 1], min_val=0, max_val=1)
                with act.If(go > 0):
                    with act.Fori(1, NS) as n:
                        c = act.snap(act_count)
                        for m in range(MD):
                            act.wait_ge(S["e_h"], c * MD + m + 1)
                            act.wait_ge(S["h_ok"], MD * t + m + 1)
                            act.activation(y[:, m, :], v[:, m, :], ACT.Exp, scale=amat[d][:, m, bass.ds(n, 1)]
                                           ).then_inc(S["e_da"], 1)
                        act.reg_add(act_count, act_count, 1)
                    wait_apart(act, S["e_y"], act.snap(act_count) * MD + 1)
                with act.Else():
                    act.nop()

            act_count = act.alloc_register("act_states")
            act.reg_mov(act_count, 0)

            def front_rest(t, d, back):
                softplus_exp(t)
                for m in range(MD):
                    softplus_log(t, m)
                if back:
                    project_copies(t - 2)
                for m in range(MD):
                    u_copy(t + 1, 1 - d, m)
                decays(t, d)
                act.preload_act_table_set("silu_and_others")
                z_silu(t + 1, 1 - d)

            act.wait_ge(S["c_tab"], 4)
            xt_copy(0)
            for m in range(MD):
                u_copy(0, 0, m)
            z_silu(0, 0)
            uc_silu(0, 0)
            xd_copy(0, 0)
            act.preload_act_table_set("natural_log_exp_and_others")
            v_copy(0, 0)
            front_rest(0, 0, False)

            def slots(s, first):
                for d in range(DIRS):
                    t = 2 * s + d
                    uc_silu(t + 1, 1 - d)
                    act.preload_act_table_set("natural_log_exp_and_others")
                    xd_copy(t + 1, 1 - d)
                    more_states(t, d)
                    v_copy(t + 1, 1 - d)
                    if d == 0:
                        xt_copy(s + 1)
                    front_rest(t + 1, 1 - d, not (first and d == 0))

            slots(0, True)
            with act.Fori(1, NSEQ) as s:
                slots(s, False)
            project_copies(2 * NSEQ - 1)

        @block.tensor
        def _(pe):
            mm = nc.tensor.matmul
            pe.wait_ge(S["c_tab"], 6)
            pe.wait_ge(S["ld_w"], 16 * (12 * DIRS + 1))
            pe.wait_ge(S["prep_w"], 1)
            for d in range(DIRS):
                for k in range(KD):
                    mm(po[0][:, 0:DM], fo[:, 0, (d * KD + k) * P:(d * KD + k + 1) * P], wfus[d][:, k, :],
                       start=(d == 0 and k == 0), stop=False)
            mm(po[0][:, 0:DM], ones[0:1, :], bfus[:], start=False, stop=True).then_inc(S["ct_ok"], 1)
            pe.wait_ge(S["prep_w"], 2)

            def turn_x(s):
                pe.wait_ge(S["xn_ok"], TT * (s + 1))
                for k in range(KD):
                    if not (isinstance(s, int) and s == 0):
                        pe.wait_ge(S["vc_ok"], MD * (2 * s - 1) + 2 + k + 1)
                    for j in range(TT):
                        i = nc.tensor.transpose(pj[k][:, j * P:(j + 1) * P], xn[:, j, k * P:(k + 1) * P], ident[:])
                    i.then_inc(S["xt_ps"], 1)

            def in_proj(t, d, half, tiles):
                ps = ("u_ps", "z_ps")[half]
                for m in tiles:
                    if half == 1 or m >= 2:
                        prev = "a_ok" if half == 0 or m < 2 else "z_ok"
                        pe.wait_ge(S[prev], MD * t + (m - 2) % MD + 1)
                    c = half * DI + m * P
                    for k in range(KD):
                        for n, (wp, xp) in enumerate(PARTS):
                            i = mm(pj[m % 2][:], win[d][wp][:, k, c:c + P], xt[xp][:, k, :],
                                   start=(k == 0 and n == 0), stop=(k == KD - 1 and n == 2))
                    i.then_inc(S[ps], 1)

            def x_dbl(t, d):
                if not (isinstance(t, int) and t == 0):
                    pe.wait_ge(S["fl_ok"], 4 * t)
                for m in range(MD):
                    pe.wait_ge(S["uc_ok"], MD * t + m + 1)
                    i = mm(px[0:NX, :], wx[d][:, m, :], uc[d][:, m, :], start=(m == 0), stop=(m == MD - 1))
                i.then_inc(S["xd_ps"], 1)

            def dt_proj(t, d):
                pe.wait_ge(S["xd_ok"], t + 1)
                for m in range(MD):
                    if m < 2:
                        pe.wait_ge(S["z_ok"], MD * t + m + 3)
                    else:
                        pe.wait_ge(S["vc_ok"], MD * t + m - 1)
                    mm(pj[m % 2][:], wdt[d][2 * NS:NX, m * P:(m + 1) * P], xd_rows(d), start=True, stop=True
                       ).then_inc(S["dt_ps"], 1)

            def dead_sums(t, d):
                pe.wait_ge(S["xm_ok"], t + 1)
                for m in range(MD):
                    i = mm(px[:, m:m + 1], wdta[d][2 * NS:NX, m * P:(m + 1) * P], xmax[2 * NS:NX, :],
                           start=True, stop=True)
                i.then_inc(S["qd_ps"], 1)

            def dead_count(t):
                pe.wait_ge(S["gt_ok"], 2 * t + 2)
                mm(px[:, 8:8 + MD], ones[:], dgt[:], start=True, stop=True).then_inc(S["cnt_ps"], 1)

            def state_sum(t, d):
                pe.wait_ge(S["fl_ok"], 4 * t + 4)
                pe.wait_ge(S["bc_ok"], t + 1)
                if not (isinstance(t, int) and t < 2):
                    pe.wait_ge(S["q_ok"], MD * (t - 1))
                mm(pss[d][:], smask[:], bcp[:], start=True, stop=True).then_inc(S["s_ps"], 1)

            def out_proj(t, d):
                for k in range(KD):
                    if not (isinstance(t, int) and t == 0):
                        pe.wait_ge(S["fin_ok"], TT * t)
                    for m in range(MD):
                        pe.wait_ge(S["yz_ok"], MD * t + m + 1)
                        i = mm(po[k][:], wout[d][:, m, k * P:(k + 1) * P], yz[:, m, :], start=(m == 0), stop=(m == MD - 1))
                    i.then_inc(S["o_ps"], 1)

            def fusion(t, d):
                pe.wait_ge(S["sq_ok"], KD * (t + 1))
                pe.wait_ge(S["fo_ok"], KD * (t + 1))
                for j in range(TT):
                    for k in range(KD):
                        i = mm(po[1][:, j:j + 1], sq[:, k, j * P:(j + 1) * P], ones[:, 0:1],
                               start=(k == 0), stop=(k == KD - 1))
                i.then_inc(S["ss_ps"], 1)
                for h in range(2):
                    bank = po[2] if h == 0 else po[0]
                    for jj in range(2):
                        j = 2 * h + jj
                        for k in range(KD):
                            i = mm(bank[:, jj * DM:(jj + 1) * DM], fo[:, k, j * P:(j + 1) * P], wfus[d][:, k, :],
                                   start=(k == 0), stop=(k == KD - 1))
                    i.then_inc(S["f_ps"], 1)

            def front(t, d, s_next, turn, back):
                x_dbl(t, d)
                dt_proj(t, d)
                if turn:
                    turn_x(s_next)
                dead_sums(t, d)
                if back:
                    out_proj(t - 2, d)
                dead_count(t)
                pe.wait_ge(S["xl_ok"], KD * (s_next + 1))
                pe.wait_ge(S["vc_ok"], MD * (t + 1))
                in_proj(t + 1, 1 - d, 0, range(MD))
                if back:
                    fusion(t - 2, d)
                in_proj(t + 1, 1 - d, 1, range(MD))
                state_sum(t, d)

            turn_x(0)
            pe.wait_ge(S["xl_ok"], KD)
            for half in range(2):
                in_proj(0, 0, half, range(MD))
            front(0, 0, 0, False, False)

            def slots(s, first):
                for d in range(DIRS):
                    t = 2 * s + d
                    front(t + 1, 1 - d, s + 1, d == 0, not (first and d == 0))

            slots(0, True)
            with pe.Fori(1, NSEQ) as s:
                slots(s, False)
            out_proj(2 * NSEQ - 1, 1)
            fusion(2 * NSEQ - 1, 1)

        @block.vector
        def _(dve):
            tt, ts, stt = nc.vector.tensor_tensor, nc.vector.tensor_scalar, nc.vector.scalar_tensor_tensor
            dve.wait_ge(S["ld_w"], 16 * (12 * DIRS + 1))
            dve.wait_ge(S["c_tab"], 7)
            for d in range(DIRS):
                for k in range(KD):
                    c = d * KD + k
                    i = ts(fo[:, 0, c * P:(c + 1) * P], ones[:], lnb[d][:, k:k + 1], None, ALU.mult)
            i.then_inc(S["prep_w"], 1)
            for d in range(DIRS):
                nc.vector.tensor_reduce(almin[d][:], amat[d][:, :, 1:NS], AX_X, ALU.min).then_inc(S["prep_v"], 1)
                dve.wait_ge(S["prep_v"], 2 * d + 1)
                ts(amat[d][:], amat[d][:], ALOG_TOP, None, ALU.min).then_inc(S["prep_v"], 1)
            for d in range(DIRS):
                nc.vector.tensor_reduce(wmean[:, d, :], wout[d][:], AX_X, ALU.add).then_inc(S["prep_v"], 1)
            dve.wait_ge(S["prep_v"], 3 * DIRS)
            ts(wmean[:], wmean[:], 1.0 / DM, None, ALU.mult).then_inc(S["prep_v"], 1)
            dve.wait_ge(S["prep_v"], 3 * DIRS + 1)
            dve.wait_ge(S["ct_ok"], 1)
            nc.vector.tensor_copy(cvec[:], po[0][:, 0:DM]).then_inc(S["prep_v"], 1)
            for d in range(DIRS):
                stage = (v, lg)[d][:].rearrange("p m n -> p (m n)").rearrange("p (k e) -> p k e", k=KD)
                nc.vector.tensor_copy(win[d][0][:], stage).then_inc(S["prep_v"], 1)
                dve.wait_ge(S["prep_v"], 3 * DIRS + 3 + d)
                tt(win[d][1][:], stage, win[d][0][:].bitcast(F32), ALU.subtract)
                for m in range(MD):
                    ts(wout[d][:, m, :], wout[d][:, m, :], wmean[:, d, m:m + 1], None, ALU.subtract)
                for k in range(KD):
                    ts(wfus[d][:, k, :], wfus[d][:, k, :], lng[d][:, k:k + 1], None, ALU.mult)
                tt(alb[d][:], almin[d][:], bdt[d][:], ALU.add)
                i = ts(alok[d][:], almin[d][:], DEAD_LOG, None, ALU.is_gt)
            i.then_inc(S["prep_w"], 1)

            def ln_stats(s):
                dve.wait_ge(S["gath"], 16 * TT * (s + 1))
                if not (isinstance(s, int) and s == 0):
                    dve.wait_ge(S["xn_ok"], TT * s)
                for j in range(TT):
                    i = nc.vector.bn_stats(stats[:, j, :], g[:, j, :])
                i.then_inc(S["gt2"], 1)
                wait_apart(dve, S["gt2"], s + 1)
                for j in range(TT):
                    i = nc.vector.bn_aggr(mv[:, j, :], stats[:, j, :])
                i.then_inc(S["st_ok"], 1)

            def ln_apply(s):
                dve.wait_ge(S["lnr_ok"], s + 1)
                if not (isinstance(s, int) and s == 0):
                    dve.wait_ge(S["xt_ps"], KD * s)
                for j in range(TT):
                    ts(xn[:, j, :], g[:, j, :], mv[:, j, 0:1], rstd[:, j:j + 1], ALU.subtract, ALU.mult
                       ).then_inc(S["xn_ok"], 1)

            def xt_low(s):
                for k in range(KD):
                    dve.wait_ge(S["xt_ok"], KD * s + k + 1)
                    tt(xt[1][:, k, :], pj[k][:], xt[0][:, k, :].bitcast(F32), ALU.subtract).then_inc(S["xl_ok"], 1)

            def conv(t, d):
                for pair, n in ((0, 0), (0, 1), (0, 2), (1, 0), (1, 1), (1, 2)):
                    tap = TAPS - 2 - n
                    shift = -(n + 1) if d == 0 else n + 1
                    for m in (2 * pair, 2 * pair + 1):
                        if n == 0:
                            dve.wait_ge(S["u_ok"], MD * t + m + 1)
                            dve.wait_ge(S["a_ok"], MD * t + m + 1)
                        else:
                            dve.wait_ge(S["cv"], PAD * MD * t + 6 * pair + 2 * (n - 1) + m % 2 + 1)
                        stt(uc[d][:, m, :], u[:, m, PAD + shift:PAD + shift + SEQ], convw[d][:, m, tap:tap + 1],
                            uc[d][:, m, :], ALU.mult, ALU.add).then_inc(S["cv"], 1)

            def bc_product(t, d):
                dve.wait_ge(S["xd_ok"], t + 1)
                if not (isinstance(t, int) and t == 0):
                    dve.wait_ge(S["s_ps"], t)
                    dve.wait_ge(S["qd_ps"], t)
                tt(bcp[:], px[NS:2 * NS, :], xd[d][0:NS, :], ALU.mult).then_inc(S["bc_ok"], 1)
                nc.vector.tensor_reduce(xmax[2 * NS:NX, :], xd_rows(d), AX_X, ALU.max,
                                        apply_absolute_value=True).then_inc(S["xm_ok"], 1)

            def dead_test(t, d):
                dve.wait_ge(S["qd_ps"], t + 1)
                if not (isinstance(t, int) and t == 0):
                    dve.wait_ge(S["cnt_ps"], t)
                tt(dgt[:], alb[d][:], px[:, 0:MD], ALU.subtract).then_inc(S["gt_ok"], 1)
                dve.wait_ge(S["gt_ok"], 2 * t + 1)
                stt(dgt[:], dgt[:], DEAD_LOG, alok[d][:], ALU.is_gt, ALU.mult).then_inc(S["gt_ok"], 1)

            def dead_mask(t, d):
                dve.wait_ge(S["cnt_ps"], t + 1)
                nc.vector.tensor_reduce(dct[:], px[:, 8:8 + MD], AX_X, ALU.add).then_inc(S["fl_ok"], 1)
                dve.wait_ge(S["fl_ok"], 4 * t + 1)
                ts(dall[:], dct[:], DI - 0.5, None, ALU.is_gt).then_inc(S["fl_ok"], 1)
                ts(live[0:1, d:d + 1], dct[0:1, :], DI - 0.5, None, ALU.is_le).then_inc(S["fl_ok"], 1)
                dve.wait_ge(S["fl_ok"], 4 * t + 2)
                ts(smask[:], smask0[:], dall[0:NS, :], None, ALU.mult).then_inc(S["fl_ok"], 1)

            def softplus(t, tiles):
                for m in tiles:
                    dve.wait_ge(S["y_ok"], MD * t + m + 1)
                    ts(wk[:, m, :], y[:, m, :], 1.0, None, ALU.add).then_inc(S["w_ok"], 1)
                for m in tiles:
                    dve.wait_ge(S["w_ok"], MD * t + m + 1)
                    dve.wait_ge(S["l_ok"], MD * t + m + 1)
                    stt(wk[:, m, :], wk[:, m, :], 1.0, lg[:, m, :], ALU.subtract, ALU.subtract).then_inc(S["g_ok"], 1)
                for m in tiles:
                    dve.wait_ge(S["g_ok"], MD * t + m + 1)
                    tt(wk[:, m, :], y[:, m, :], wk[:, m, :], ALU.subtract).then_inc(S["d0_ok"], 1)
                for m in tiles:
                    dve.wait_ge(S["d0_ok"], MD * t + m + 1)
                    stt(v[:, m, :], v[:, m, :], 0.0, wk[:, m, :], ALU.max, ALU.add).then_inc(S["dt_ok"], 1)

            def scan(t, d):
                step = slice(None) if d == 0 else slice(None, None, -1)
                for m in range(MD):
                    dve.wait_ge(S["da_ok"], MD * t + m + 1)
                    dve.wait_ge(S["tp_ok"], MD * t + m + 1)
                    nc.vector.tensor_tensor_scan(tp[:, m, step], y[:, m, step], tp[:, m, step], 0.0, ALU.mult, ALU.add
                                                 ).then_inc(S["h_ok"], 1)

            def dead_part(t, d):
                dve.wait_ge(S["s_ps"], t + 1)
                for m in range(MD):
                    tt(qq[:, m, :], v[:, m, :], pss[d][:], ALU.mult).then_inc(S["q_ok"], 1)
                for m in range(MD):
                    dve.wait_ge(S["q_ok"], MD * t + m + 1)
                    stt(qq[:, m, :], qq[:, m, :], dp[d][:, m:m + 1], uc[d][:, m, :], ALU.add, ALU.mult
                        ).then_inc(S["q2_ok"], 1)

            def outputs(t, d):
                for m in range(MD):
                    dve.wait_ge(S["h_ok"], MD * t + m + 1)
                    tt(tp[:, m, :], tp[:, m, :], bb[d][:, 1, :], ALU.mult).then_inc(S["hc_ok"], 1)

            def more_states(t, d):
                wait_apart(dve, S["fl_ok"], 4 * t + 3)
                go = dve.value_load(live[0:1, d:d + 1], min_val=0, max_val=1)
                step = slice(None) if d == 0 else slice(None, None, -1)
                with dve.If(go > 0):
                    with dve.Fori(1, NS) as n:
                        c = dve.snap(dve_count)
                        if not (isinstance(t, int) and t < 2):
                            dve.wait_ge(S["ss_ps"], t - 1)
                        dve.wait_ge(S["e_bc"], 32 * c + 32)
                        for m in range(MD):
                            at = MD * c + m + 1
                            dve.wait_ge(S["e_y"], at)
                            tt(eh, wk[:, m, :], bb[1 - d][:, 0, :], ALU.mult).then_inc(S["e_tp"], 1)
                            dve.wait_ge(S["e_tp"], at)
                            dve.wait_ge(S["e_da"], at)
                            nc.vector.tensor_tensor_scan(sq[:, 0, step], y[:, m, step], sq[:, 0, step], 0.0, ALU.mult, ALU.add
                                                         ).then_inc(S["e_h"], 1)
                            dve.wait_ge(S["e_h"], at + 1)
                            tt(eh, eh, bb[1 - d][:, 1, :], ALU.mult).then_inc(S["e_hc"], 1)
                            dve.wait_ge(S["e_hc"], at)
                            dve.wait_ge(S["q2_ok"], MD * (t + 1))
                            tt(qq[:, m, :], qq[:, m, :], eh, ALU.add).then_inc(S["e_y"], 1)
                        dve.reg_add(dve_count, dve_count, 1)
                    wait_apart(dve, S["e_y"], dve.snap(dve_count) * MD + 1)
                with dve.Else():
                    dve.nop()

            def sums(t):
                for m in range(MD):
                    dve.wait_ge(S["hc_ok"], MD * t + m + 1)
                    dve.wait_ge(S["q2_ok"], MD * t + m + 1)
                    tt(tp[:, m, :], tp[:, m, :], qq[:, m, :], ALU.add).then_inc(S["yv_ok"], 1)

            def row_var(t):
                dve.wait_ge(S["ss_ps"], t + 1)
                if not (isinstance(t, int) and t == 0):
                    dve.wait_ge(S["fin_ok"], TT * t)
                ts(r2[:], po[1][:, 0:TT], 1.0 / DM, EPS, ALU.mult, ALU.add).then_inc(S["rv_ok"], 1)

            def finish(t, d, s_of):
                dve.wait_ge(S["rr_ok"], t + 1)
                if d == 0:
                    dve.wait_ge(S["h0_ok"], s_of + 1)
                elif not (isinstance(s_of, int) and s_of == 0):
                    dve.wait_ge(S["h1_st"], 16 * s_of)
                if d == 1:
                    dve.wait_ge(S["fin_ok"], TT * t)
                for j in range(TT):
                    bank = po[2] if j < 2 else po[0]
                    dve.wait_ge(S["f_ps"], 2 * t + j // 2 + 1)
                    src = h0c[:, bass.ds(s_of % 2, 1), j, :].squeeze(1)
                    dst = src if d == 0 else h1o[:, j, :]
                    stt(dst, bank[:, (j % 2) * DM:(j % 2 + 1) * DM], r2[:, j:j + 1], src,
                        ALU.mult, ALU.add).then_inc(S["fin_ok"], 1)

            dve_count = dve.alloc_register("dve_states")
            dve.reg_mov(dve_count, 0)
            dve.nop().then_inc(S["e_h"], 1)
            dve.nop().then_inc(S["e_y"], 1)

            ln_stats(0)
            ln_apply(0)
            xt_low(0)
            conv(0, 0)
            bc_product(0, 0)
            softplus(0, range(2))
            dead_test(0, 0)
            softplus(0, range(2, MD))
            dead_mask(0, 0)

            def slots(s, first):
                for d in range(DIRS):
                    t = 2 * s + d
                    conv(t + 1, 1 - d)
                    if not first:
                        row_var(t - 2)
                    if d == 0:
                        ln_stats(s + 1)
                    dead_part(t, d)
                    if not first:
                        finish(t - 2, d, s - 1)
                    if d == 0:
                        ln_apply(s + 1)
                    bc_product(t + 1, 1 - d)
                    scan(t, d)
                    more_states(t, d)
                    outputs(t, d)
                    sums(t)
                    if d == 0:
                        xt_low(s + 1)
                    dead_test(t + 1, 1 - d)
                    softplus(t + 1, range(MD))
                    dead_mask(t + 1, 1 - d)

            slots(0, True)
            with dve.Fori(1, NSEQ) as s:
                slots(s, False)
            row_var(2 * NSEQ - 2)
            finish(2 * NSEQ - 2, 0, NSEQ - 1)
            row_var(2 * NSEQ - 1)
            finish(2 * NSEQ - 1, 1, NSEQ - 1)


NCH = 32
BB = 16
NG = 4
NQ = 4
HD = 16
S_A = 32
NE = 8
QK = NQ + NG
BANKS = (2, 3, 0, 1)
V_BANK = (3, 1)
TABLES = 8 + NQ * (3 + NG)
NT = NSEQ * SEQ // P
MASKED = -3.0e38


def attention_stage(nc, w, h1_dram, base_dram, xc_dram, lg_all):
    ctx = ExitStack()
    with ctx:
        def sb(name, shape, dt=F32):
            return ctx.enter_context(nc.sbuf_tensor(name, shape, dt))

        wq = sb("a_wq", [P, KD, NQ + 1, P])
        wv = sb("a_wv", [P, KD, NG * HD])
        wp = sb("a_wp", [NG * HD, NQ, DM])
        wr = sb("a_wr", [P, KD, NE])
        lnw = sb("a_lnw", [P, 2, KD])
        lnb = sb("a_lnb", [P, 2, KD])
        ident = sb("a_ident", [P, P])
        cmask = sb("a_cmask", [P, S_A])
        vmask = sb("a_vmask", [P, NG * HD])
        nh = sb("a_nh", [P, TT])

        h1 = sb("a_h1", [P, TT, DM])
        stats = sb("a_stats", [P, TT, 6])
        mv = sb("a_mv", [P, TT, 2])
        ve = sb("a_ve", [P, 2, TT])
        rs1 = sb("a_rs1", [P, 2, TT])
        mean = sb("a_mean", [P, (NCH + 2) * TT])
        r1 = sb("a_r1", [P, (NCH + 2) * TT])
        core = sb("a_core", [P, TT, DM])
        lt = sb("a_lt", [P, KD, SEQ])
        qt = sb("a_qt", [P, BB, NQ, S_A])
        kb = sb("a_kb", [P, BB, NG, S_A])
        vd = sb("a_vd", [P, TT, 4, NG * HD])
        spread = sb("a_spread", [P, P])
        bmask = sb("a_bmask", [P, 4])
        vb = sb("a_vb", [P, BB, NG * HD])
        ss = sb("a_ss", [P, BB, NG, S_A])
        mx = sb("a_mx", [P, BB, NG])
        sm = sb("a_sm", [P, BB, NG])
        rs = sb("a_rs", [P, BB, NG])
        pt = sb("a_pt", [P, BB, P])
        ao = sb("a_ao", [NG * HD, NQ, SEQ])
        hb = sb("a_hb", [P, TT, DM])
        fi = sb("a_fi", [P, TT, DM])
        hh = sb("a_hh", [P, TT, DM])
        bs = sb("a_bs", [P, TT, DM])
        st2 = sb("a_st2", [P, TT, 6])
        mv2 = sb("a_mv2", [P, TT, 2])
        ve2 = sb("a_ve2", [P, TT])
        rr2 = sb("a_rr2", [P, TT])
        x2 = sb("a_x2", [P, TT, DM])
        x2t = sb("a_x2t", [P, KD, SEQ])

        A = [ctx.enter_context(nc.psum_tensor(f"a_pa{i}", [P, SEQ], F32)) for i in range(4)]
        B = [ctx.enter_context(nc.psum_tensor(f"a_pb{i}", [P, SEQ], F32)) for i in range(4)]

        names = """c0 ld_w ld_h ld_hb st1 rq1 core_ok t1_ps lt_ok qk_ps qk_ok vn_ps vd_ok v_ps v_ok s_ps s_ok mx_ok
          sub_ok ex_ok su_ok rc_ok p_ok pt_ps pt_ok av_ps ao_ok pr_ps fi_ok hh_ok bs_ok st2 ve2 rr2 x2_ok t2_ps x2t_ok
          lg_ps lg_ok st_b st_x""".split()
        S = {n: ctx.enter_context(nc.semaphore("a_" + n)) for n in names}
        block = ctx.enter_context(nc.Block())

        def wait_apart(eng, *waits):
            waits = [(s, v if isinstance(v, int) else eng.to_reg(v)) for s, v in waits]
            eng.wait_ge(S["c0"], 1)
            for semaphore, value in waits:
                if not (isinstance(value, int) and value <= 0):
                    eng.wait_ge(semaphore, value)

        def after(eng, name, value):
            if not (isinstance(value, int) and value <= 0):
                eng.wait_ge(S[name], value)

        h1_v = h1_dram.rearrange("(s b) c -> b s c", s=NSEQ)

        @block.sync
        def _(sp):
            for dst, name in ((wq, "wq"), (wv, "wv"), (wr, "wr")):
                src = w[name].rearrange("(k p) j e -> p k j e", p=P) if name == "wq" else \
                    w[name].rearrange("(k p) e -> p k e", p=P)
                sp.dma_start(dst[:], src).then_inc(S["ld_w"], 16)
            sp.dma_start(wp[:], w["wp"]).then_inc(S["ld_w"], 16)
            sp.dma_start(lnw[:], w["lnw"]).then_inc(S["ld_w"], 16)
            sp.dma_start(lnb[:], w["lnb"]).then_inc(S["ld_w"], 16)

            def load(dst, c, name):
                b0 = c * BB if isinstance(c, int) else (c * BB) % SEQ
                for j in range(TT):
                    sp.dma_start(dst[:, j, :], h1_v[bass.ds(b0 + 4 * j, 4), :, :]).then_inc(S[name], 16)

            load(h1, 0, "ld_h")
            sp.wait_ge(S["core_ok"], TT)
            load(h1, 1, "ld_h")

            def results(c):
                sp.wait_ge(S["bs_ok"], c + 1)
                sp.dma_start(base_dram[:, bass.ds(c * TT, TT), :], bs[:]).then_inc(S["st_b"], 16)
                sp.wait_ge(S["x2_ok"], TT * (c + 1))
                sp.dma_start(xc_dram[:, bass.ds(c * TT, TT), :], x2[:]).then_inc(S["st_x"], 16)

            def slot(c):
                sp.wait_ge(S["core_ok"], TT * (c + 2))
                load(h1, c + 2, "ld_h")
                after(sp, "bs_ok", c)
                load(hb, c, "ld_hb")
                if not (isinstance(c, int) and c == 0):
                    results(c - 1)

            slot(0)
            slot(1)
            with sp.Fori(2, NCH) as c:
                slot(c)
            results(NCH - 1)
            sp.wait_ge(S["st_b"], 16 * NCH)
            sp.wait_ge(S["st_x"], 16 * NCH)
            sp.wait_ge(S["ld_h"], 16 * TT * (NCH + 2))

        @block.gpsimd
        def _(pool):
            pool.memset(nh[:], -0.5).then_inc(S["c0"], 1)
            pool.wait_ge(S["c0"], 1)
            done = 1
            for tile in (ident, cmask, vmask, bmask, spread, kb):
                pool.memset(tile[:], 0.0).then_inc(S["c0"], 1)
                done += 1
                pool.wait_ge(S["c0"], done)
            pool.affine_select(out=ident[:], in_=ident[:], compare_op=ALU.not_equal, fill=1.0, base=0,
                               pattern=[[-1, P]], channel_multiplier=1).then_inc(S["c0"], 1)
            pool.wait_ge(S["c0"], done + 1)
            done += 1
            for q in range(NQ):
                rows = slice(S_A * q, S_A * (q + 1))
                pool.affine_select(out=cmask[rows, :], in_=cmask[rows, :], compare_op=ALU.is_ge, fill=MASKED, base=0,
                                   pattern=[[-1, S_A]], channel_multiplier=1).then_inc(S["c0"], 1)
                pool.wait_ge(S["c0"], done + 1)
                pool.memset(vmask[rows, HD * q:HD * (q + 1)], 1.0).then_inc(S["c0"], 1)
                pool.wait_ge(S["c0"], done + 2)
                pool.memset(bmask[rows, q:q + 1], 1.0).then_inc(S["c0"], 1)
                pool.wait_ge(S["c0"], done + 3)
                for n in range(NG):
                    pool.tensor_copy(spread[rows, S_A * n:S_A * (n + 1)], ident[rows, rows]).then_inc(S["c0"], 1)
                    pool.wait_ge(S["c0"], done + 4 + n)
                done += 3 + NG

            def scales1(c):
                wait_apart(pool, (S["st1"], 2 * c + 2), (S["core_ok"], TT * c))
                pool.tensor_scalar(ve[:, 0, :], mv[:, :, 1], 1.0, EPS, ALU.mult, ALU.add).then_inc(S["rq1"], 1)
                pool.tensor_scalar(ve[:, 1, :], mv[:, :, 1], 1.0 + EPS, EPS * EPS, ALU.mult, ALU.add
                                   ).then_inc(S["rq1"], 1)
                pool.wait_ge(S["rq1"], 3 * c + 2)
                pool.tensor_tensor(rs1[:], ve[:], nh[:].unsqueeze(1).to_broadcast([P, 2, TT]), ALU.pow
                                   ).then_inc(S["rq1"], 1)

            def scales2(c):
                wait_apart(pool, (S["st2"], 2 * c + 2), (S["x2_ok"], TT * c))
                pool.tensor_scalar(ve2[:], mv2[:, :, 1], 1.0, EPS, ALU.mult, ALU.add).then_inc(S["ve2"], 1)
                pool.wait_ge(S["ve2"], c + 1)
                pool.tensor_tensor(rr2[:], ve2[:], nh[:], ALU.pow).then_inc(S["rr2"], 1)

            def per_row(tile, i):
                return tile[:, 4 * i:4 * i + 4, :].unsqueeze(3).to_broadcast([P, 4, NG, S_A])

            def subtract_max(c):
                for n, i in enumerate(BANKS):
                    pool.wait_ge(S["mx_ok"], 4 * c + n + 1)
                    pool.tensor_tensor(ss[:, 4 * i:4 * i + 4], ss[:, 4 * i:4 * i + 4], per_row(mx, i),
                                       ALU.subtract).then_inc(S["sub_ok"], 1)

            def normalise(c):
                for n, i in enumerate(BANKS):
                    pool.wait_ge(S["rc_ok"], 4 * c + n + 1)
                    pool.tensor_tensor(ss[:, 4 * i:4 * i + 4], ss[:, 4 * i:4 * i + 4], per_row(rs, i),
                                       ALU.mult).then_inc(S["p_ok"], 1)

            def base(c):
                pool.wait_ge(S["hh_ok"], 2 * (c + 1))
                after(pool, "st_b", 16 * c)
                pool.tensor_tensor(bs[:], hh[:], hb[:], ALU.add).then_inc(S["bs_ok"], 1)

            scales1(0)
            scales1(1)

            def slot(c):
                subtract_max(c)
                if not (isinstance(c, int) and c == 0):
                    base(c - 1)
                    scales2(c - 1)
                normalise(c)
                scales1(c + 2)

            slot(0)
            slot(1)
            with pool.Fori(2, NCH) as c:
                slot(c)
            base(NCH - 1)
            scales2(NCH - 1)

        @block.scalar
        def _(act):
            act.wait_ge(S["ld_w"], 16 * 6)

            def lt_copy(c):
                for k in range(KD):
                    act.wait_ge(S["t1_ps"], KD * c + k + 1)
                    act.activation(lt[:, k, :], B[k][:], ACT.Identity, bias=lnb[:, 0, k:k + 1],
                                   scale=lnw[:, 0, k:k + 1]).then_inc(S["lt_ok"], 1)

            def q_copy(c, q):
                act.wait_ge(S["qk_ps"], (NQ + 1) * c + q + 1)
                after(act, "s_ps", 4 * c)
                act.activation(qt[:, :, q, :], B[q % 2][:].rearrange("p (b s) -> p b s", b=BB), ACT.Copy
                               ).then_inc(S["qk_ok"], 1)

            def k_copy(c):
                act.wait_ge(S["qk_ps"], (NQ + 1) * (c + 1))
                for g in range(NG):
                    rows = slice(32 * g, 32 * (g + 1))
                    act.activation(kb[rows, :, g, :], B[0][rows, :].rearrange("p (b s) -> p b s", b=BB), ACT.Copy
                                   ).then_inc(S["qk_ok"], 1)

            def exp(c, n):
                i = BANKS[n]
                act.wait_ge(S["sub_ok"], 4 * c + n + 1)
                act.activation(ss[:, 4 * i:4 * i + 4], ss[:, 4 * i:4 * i + 4], ACT.Exp, scale=HD ** -0.5
                               ).then_inc(S["ex_ok"], 1)

            def pt_copy(c):
                for n, i in enumerate(BANKS):
                    act.wait_ge(S["pt_ps"], 4 * c + n + 1)
                    after(act, "av_ps", 4 * c)
                    act.activation(pt[:, 4 * i:4 * i + 4, :], A[i][:].rearrange("p (b n) -> p b n", b=4), ACT.Copy
                                   ).then_inc(S["pt_ok"], 1)

            def ao_copy(c):
                for n, i in enumerate(BANKS):
                    act.wait_ge(S["av_ps"], 4 * c + n + 1)
                    after(act, "pr_ps", 2 * c)
                    src = B[i][0:NG * HD, :].rearrange("p (b q s) -> p b q s", b=4, q=NQ)
                    dst = ao[:, :, i * P:(i + 1) * P].rearrange("p q (b s) -> p b q s", b=4)
                    act.activation(dst, src, ACT.Copy).then_inc(S["ao_ok"], 1)

            def x2t_copy(c):
                for k in range(KD):
                    act.wait_ge(S["t2_ps"], KD * c + k + 1)
                    after(act, "lg_ps", c)
                    act.activation(x2t[:, k, :], A[k][:], ACT.Identity, bias=lnb[:, 1, k:k + 1],
                                   scale=lnw[:, 1, k:k + 1]).then_inc(S["x2t_ok"], 1)

            act.wait_ge(S["c0"], TABLES)
            lt_copy(0)
            for q in range(NQ):
                q_copy(0, q)
            k_copy(0)
            act.wait_ge(S["vn_ps"], 1)
            lt_copy(1)

            def slot(c):
                exp(c, 0)
                exp(c, 1)
                q_copy(c + 1, 0)
                exp(c, 2)
                q_copy(c + 1, 1)
                exp(c, 3)
                q_copy(c + 1, 2)
                q_copy(c + 1, 3)
                k_copy(c + 1)
                if not (isinstance(c, int) and c == 0):
                    x2t_copy(c - 1)
                pt_copy(c)
                ao_copy(c)
                act.wait_ge(S["vn_ps"], c + 2)
                lt_copy(c + 2)

            slot(0)
            slot(1)
            with act.Fori(2, NCH) as c:
                slot(c)
            x2t_copy(NCH - 1)

        @block.tensor
        def _(pe):
            mm = nc.tensor.matmul
            pe.wait_ge(S["ld_w"], 16 * 6)
            pe.wait_ge(S["c0"], TABLES)

            def turn1(c):
                pe.wait_ge(S["core_ok"], TT * (c + 1))
                for k in range(KD):
                    if k == 0:
                        after(pe, "ao_ok", 4 * (c - 1))
                        after(pe, "qk_ok", QK * c)
                    for j in range(TT):
                        i = nc.tensor.transpose(B[k][:, j * P:(j + 1) * P], core[:, j, k * P:(k + 1) * P], ident[:])
                    i.then_inc(S["t1_ps"], 1)

            def qk(c):
                pe.wait_ge(S["lt_ok"], KD * (c + 1))
                for q in range(NQ + 1):
                    if q >= 2:
                        pe.wait_ge(S["qk_ok"], QK * c + q - 1)
                    for k in range(KD):
                        i = mm(B[q % 2][:], wq[:, k, q, :], lt[:, k, :], start=(k == 0), stop=(k == KD - 1))
                    i.then_inc(S["qk_ps"], 1)

            def values(c):
                after(pe, "ao_ok", 4 * c)
                for j in range(TT):
                    for k in range(KD):
                        n = mm(B[2][:, j * 64:(j + 1) * 64], lt[:, k, j * P:(j + 1) * P], wv[:, k, :],
                               start=(k == 0), stop=(k == KD - 1))
                n.then_inc(S["vn_ps"], 1)

            def spread_values(c):
                after(pe, "ao_ok", 4 * c)
                pe.wait_ge(S["qk_ok"], QK * (c + 1) + NQ)
                for i in range(2):
                    pe.wait_ge(S["vd_ok"], TT * c + 2 * i + 2)
                    for jj in range(2):
                        n = mm(B[V_BANK[i]][:, jj * 256:(jj + 1) * 256], spread[:],
                               vd[:, 2 * i + jj, :, :].rearrange("p b n -> p (b n)"), start=True, stop=True)
                    n.then_inc(S["v_ps"], 1)

            def scores(c):
                pe.wait_ge(S["qk_ok"], QK * (c + 1))
                after(pe, "pt_ok", 4 * c)
                for n, i in enumerate(BANKS):
                    if n == 2:
                        after(pe, "hh_ok", 2 * c)
                    for b in range(4):
                        o = mm(A[i][:, b * P:(b + 1) * P], qt[:, 4 * i + b].rearrange("p q s -> p (q s)"),
                               kb[:, 4 * i + b].rearrange("p g t -> p (g t)"), start=True, stop=True)
                    o.then_inc(S["s_ps"], 1)

            def turn_p(c):
                for n, i in enumerate(BANKS):
                    pe.wait_ge(S["p_ok"], 4 * c + n + 1)
                    if n == 2:
                        after(pe, "x2t_ok", KD * c)
                    for b in range(4):
                        o = nc.tensor.transpose(A[i][:, b * P:(b + 1) * P],
                                                ss[:, 4 * i + b, :, :].rearrange("p g t -> p (g t)"), ident[:])
                    o.then_inc(S["pt_ps"], 1)

            def products(c):
                pe.wait_ge(S["qk_ok"], QK * (c + 2))
                pe.wait_ge(S["v_ok"], 2 * (c + 1))
                after(pe, "lg_ok", c)
                for n, i in enumerate(BANKS):
                    pe.wait_ge(S["pt_ok"], 4 * c + n + 1)
                    for b in range(4):
                        o = mm(B[i][0:NG * HD, b * P:(b + 1) * P], vb[:, 4 * i + b, :], pt[:, 4 * i + b, :],
                               start=True, stop=True)
                    o.then_inc(S["av_ps"], 1)

            def project(c):
                pe.wait_ge(S["ao_ok"], 4 * (c + 1))
                for i in range(2):
                    for jj in range(2):
                        j = 2 * i + jj
                        for q in range(NQ):
                            n = mm(A[i][:, jj * DM:(jj + 1) * DM], ao[:, q, j * P:(j + 1) * P], wp[:, q, :],
                                   start=(q == 0), stop=(q == NQ - 1))
                    n.then_inc(S["pr_ps"], 1)

            def turn2(c, last=False):
                pe.wait_ge(S["x2_ok"], TT * (c + 1))
                if last:
                    pe.wait_ge(S["hh_ok"], 2 * (c + 1))
                else:
                    pe.wait_ge(S["s_ok"], 4 * (c + 2))
                for k in range(KD):
                    for j in range(TT):
                        i = nc.tensor.transpose(A[k][:, j * P:(j + 1) * P], x2[:, j, k * P:(k + 1) * P], ident[:])
                    i.then_inc(S["t2_ps"], 1)

            def router(c):
                pe.wait_ge(S["x2t_ok"], KD * (c + 1))
                pe.wait_ge(S["vd_ok"], TT * (c + 2))
                for j in range(TT):
                    for k in range(KD):
                        i = mm(B[2][:, j * NE:(j + 1) * NE], x2t[:, k, j * P:(j + 1) * P], wr[:, k, :],
                               start=(k == 0), stop=(k == KD - 1))
                i.then_inc(S["lg_ps"], 1)

            turn1(0)
            qk(0)
            values(0)
            turn1(1)

            def slot(c):
                scores(c)
                qk(c + 1)
                if not (isinstance(c, int) and c == 0):
                    turn2(c - 1)
                    spread_values(c)
                    router(c - 1)
                else:
                    spread_values(c)
                turn_p(c)
                products(c)
                project(c)
                values(c + 1)
                turn1(c + 2)

            slot(0)
            slot(1)
            with pe.Fori(2, NCH) as c:
                slot(c)
            turn2(NCH - 1, True)
            router(NCH - 1)

        @block.vector
        def _(dve):
            tt, ts, stt = nc.vector.tensor_tensor, nc.vector.tensor_scalar, nc.vector.scalar_tensor_tensor

            def stats1(c):
                dve.wait_ge(S["ld_h"], 16 * TT * (c + 1))
                for j in range(TT):
                    i = nc.vector.bn_stats(stats[:, j, :], h1[:, j, :])
                i.then_inc(S["st1"], 1)
                wait_apart(dve, (S["st1"], 2 * c + 1))
                for j in range(TT):
                    i = nc.vector.bn_aggr(mv[:, j, :], stats[:, j, :])
                i.then_inc(S["st1"], 1)

            def normalise(c):
                dve.wait_ge(S["st1"], 2 * c + 2)
                cols = bass.ds(c * TT, TT)
                nc.vector.tensor_copy(mean[:, cols], mv[:, :, 0])
                dve.wait_ge(S["rq1"], 3 * c + 3)
                nc.vector.tensor_copy(r1[:, cols], rs1[:, 0, :])
                after(dve, "t1_ps", KD * c)
                for j in range(TT):
                    ts(core[:, j, :], h1[:, j, :], mv[:, j, 0:1], rs1[:, 1, j:j + 1], ALU.subtract, ALU.mult
                       ).then_inc(S["core_ok"], 1)

            def v_parts(c):
                dve.wait_ge(S["vn_ps"], c + 1)
                after(dve, "v_ps", 2 * c)
                for j in range(TT):
                    tt(vd[:, j, :, :], B[2][:, j * 64:(j + 1) * 64].unsqueeze(1).to_broadcast([P, 4, NG * HD]),
                       bmask[:].unsqueeze(2).to_broadcast([P, 4, NG * HD]), ALU.mult).then_inc(S["vd_ok"], 1)

            def v_copy(c):
                for i in range(2):
                    dve.wait_ge(S["v_ps"], 2 * c + i + 1)
                    after(dve, "av_ps", 4 * c)
                    tt(vb[:, 8 * i:8 * i + 8, :], B[V_BANK[i]][:].rearrange("p (b n) -> p b n", b=8),
                       vmask[:].unsqueeze(1).to_broadcast([P, 8, NG * HD]), ALU.mult).then_inc(S["v_ok"], 1)

            def maxima(c):
                for n, i in enumerate(BANKS):
                    part = ss[:, 4 * i:4 * i + 4]
                    dve.wait_ge(S["s_ps"], 4 * c + n + 1)
                    after(dve, "pt_ps", 4 * c)
                    tt(part, A[i][:].rearrange("p (b g t) -> p b g t", b=4, g=NG),
                       cmask[:].unsqueeze(1).unsqueeze(1).to_broadcast([P, 4, NG, S_A]), ALU.add
                       ).then_inc(S["s_ok"], 1)
                    dve.wait_ge(S["s_ok"], 4 * c + n + 1)
                    nc.vector.tensor_reduce(mx[:, 4 * i:4 * i + 4, :], part, AX_X, ALU.max).then_inc(S["mx_ok"], 1)

            def sums(c):
                for n, i in enumerate(BANKS):
                    dve.wait_ge(S["ex_ok"], 4 * c + n + 1)
                    nc.vector.tensor_reduce(sm[:, 4 * i:4 * i + 4, :], ss[:, 4 * i:4 * i + 4], AX_X, ALU.add
                                            ).then_inc(S["su_ok"], 1)
                    dve.wait_ge(S["su_ok"], 4 * c + n + 1)
                    nc.vector.reciprocal(rs[:, 4 * i:4 * i + 4, :], sm[:, 4 * i:4 * i + 4, :]).then_inc(S["rc_ok"], 1)

            def first_input(c):
                dve.wait_ge(S["ld_hb"], 16 * TT * (c + 1))
                cols = c * TT
                for j in range(TT):
                    ts(fi[:, j, :], hb[:, j, :], mean[:, bass.ds(cols + j, 1)], r1[:, bass.ds(cols + j, 1)],
                       ALU.subtract, ALU.mult).then_inc(S["fi_ok"], 1)

            def add_projection(c):
                for i in range(2):
                    dve.wait_ge(S["pr_ps"], 2 * c + i + 1)
                    dve.wait_ge(S["fi_ok"], TT * (c + 1))
                    after(dve, "bs_ok", c)
                    tt(hh[:, 2 * i:2 * i + 2, :], A[i][:].rearrange("p (j e) -> p j e", j=2),
                       fi[:, 2 * i:2 * i + 2, :], ALU.add).then_inc(S["hh_ok"], 1)

            def stats2(c):
                for j in range(TT):
                    dve.wait_ge(S["hh_ok"], 2 * c + j // 2 + 1)
                    i = nc.vector.bn_stats(st2[:, j, :], hh[:, j, :])
                i.then_inc(S["st2"], 1)
                wait_apart(dve, (S["st2"], 2 * c + 1))
                for j in range(TT):
                    i = nc.vector.bn_aggr(mv2[:, j, :], st2[:, j, :])
                i.then_inc(S["st2"], 1)

            def normalise2(c):
                dve.wait_ge(S["rr2"], c + 1)
                after(dve, "st_x", 16 * c)
                after(dve, "t2_ps", KD * c)
                for j in range(TT):
                    ts(x2[:, j, :], hh[:, j, :], mv2[:, j, 0:1], rr2[:, j:j + 1], ALU.subtract, ALU.mult
                       ).then_inc(S["x2_ok"], 1)

            def keep_logits(c):
                dve.wait_ge(S["lg_ps"], c + 1)
                nc.vector.tensor_copy(lg_all[:, bass.ds(c * TT, TT), :],
                                      B[2][:, 0:TT * NE].rearrange("p (j e) -> p j e", j=TT)).then_inc(S["lg_ok"], 1)

            dve.wait_ge(S["c0"], TABLES)
            stats1(0)
            normalise(0)
            v_parts(0)
            stats1(1)
            normalise(1)

            def slot(c):
                first = isinstance(c, int) and c == 0
                if not first:
                    add_projection(c - 1)
                maxima(c)
                if not first:
                    stats2(c - 1)
                sums(c)
                if not first:
                    normalise2(c - 1)
                stats1(c + 2)
                v_copy(c)
                normalise(c + 2)
                if not first:
                    keep_logits(c - 1)
                first_input(c)
                v_parts(c + 1)

            slot(0)
            slot(1)
            with dve.Fori(2, NCH) as c:
                slot(c)
            add_projection(NCH - 1)
            stats2(NCH - 1)
            normalise2(NCH - 1)
            keep_logits(NCH - 1)
            dve.wait_ge(S["lg_ok"], NCH)


NTILE = NSEQ * SEQ // P
TOP = 2
FF = 512
MF = FF // P
CAP = -(-NSEQ * SEQ * TOP * 5 // (NE * 4))
HALF = 256
HT = HALF // P
PAIR = 2 * HALF
CAP_ROWS = CAP + PAIR
MAX_PAIRS = -(-CAP // PAIR)
NOWHERE = float(1 << 20)
GT = 4
NGT = NTILE // GT


def routing_stage(nc, lg_all, dst_row, src_row, prob, plan):
    ctx = ExitStack()
    with ctx:
        def sb(name, shape, dt=F32):
            return ctx.enter_context(nc.sbuf_tensor(name, shape, dt))

        block_shape = [P, NTILE, NE]
        ident = sb("r_ident", [P, P])
        same = sb("r_same", [P, P])
        later = sb("r_later", [P, P])
        below = sb("r_below", [P, P])
        ones = sb("r_ones", [P, P])
        expert = sb("r_expert", [P, NE])
        row0 = sb("r_row0", [P, NE])
        steps = sb("r_steps", [1, MAX_PAIRS - 1])
        m = sb("r_m", [P, TOP, NTILE])
        pick = sb("r_pick", [P, NTILE])
        flag = sb("r_flag", block_shape)
        rest = sb("r_rest", block_shape)
        hot = [sb(f"r_hot{k}", block_shape) for k in range(TOP)]
        both = sb("r_both", block_shape)
        rank = sb("r_rank", block_shape)
        total = sb("r_total", [P, NE])
        dst = sb("r_dst", [P, TOP, NTILE])
        keep = sb("r_keep", [P, TOP, NTILE])
        kdst = sb("r_kdst", [P, TOP, NTILE])
        ex = sb("r_ex", [P, NTILE])
        count = sb("r_count", [1, NE])
        over = sb("r_over", [1, NE, MAX_PAIRS - 1])
        planf = sb("r_planf", [1, 2, NE])
        ps_same = [ctx.enter_context(nc.psum_tensor(f"r_ps{i}", [P, SEQ], F32)) for i in range(2)]
        ps_part = [ctx.enter_context(nc.psum_tensor(f"r_pp{i}", [P, SEQ], F32)) for i in range(2)]
        ps_base = ctx.enter_context(nc.psum_tensor("r_pb", [P, 2, NE], F32))
        S = {n: ctx.enter_context(nc.semaphore("r_" + n)) for n in "tab seq both_ok tot_ok counted ex_ok".split()}
        block = ctx.enter_context(nc.Block())

        @block.gpsimd
        def _(pool):
            n = 0
            for tile, value in ((ident, 0.0), (same, 0.0), (later, 0.0), (below, 0.0), (ones, 1.0)):
                pool.memset(tile[:], value).then_inc(S["tab"], 1)
                n += 1
                pool.wait_ge(S["tab"], n)
            pool.affine_select(out=ident[:], in_=ident[:], compare_op=ALU.not_equal, fill=1.0, base=0,
                               pattern=[[-1, P]], channel_multiplier=1).then_inc(S["tab"], 1)
            n += 1
            pool.wait_ge(S["tab"], n)
            for q in range(4):
                rows = slice(S_A * q, S_A * (q + 1))
                for g in range(4):
                    cols = slice(S_A * g, S_A * (g + 1))
                    pool.tensor_copy(same[rows, cols], ident[rows, rows]).then_inc(S["tab"], 1)
                    n += 1
                    pool.wait_ge(S["tab"], n)
                    if q >= g:
                        pool.tensor_scalar(later[rows, cols], ident[rows, rows], -1.0, None, ALU.mult
                                           ).then_inc(S["tab"], 1)
                        n += 1
                        pool.wait_ge(S["tab"], n)
                    pool.affine_select(out=below[rows, cols], in_=ones[rows, cols], compare_op=ALU.is_gt, fill=0.0,
                                       base=0, pattern=[[1, S_A]], channel_multiplier=-1).then_inc(S["tab"], 1)
                    n += 1
                    pool.wait_ge(S["tab"], n)
            for e in range(NE):
                for tile, value in ((expert, e), (row0, e * CAP_ROWS)):
                    pool.memset(tile[:, e:e + 1], float(value)).then_inc(S["tab"], 1)
                    n += 1
                    pool.wait_ge(S["tab"], n)
            for i in range(MAX_PAIRS - 1):
                pool.memset(steps[:, i:i + 1], float(PAIR * (i + 1))).then_inc(S["tab"], 1)
                n += 1
                pool.wait_ge(S["tab"], n)
            assert n == TABLES_R

        @block.scalar
        def _(act):
            act.wait_ge(S["seq"], 11)
            act.activation(ex[:], ex[:], ACT.Exp).then_inc(S["ex_ok"], 1)

        @block.tensor
        def _(pe):
            pe.wait_ge(S["tab"], TABLES_R)
            pe.wait_ge(S["both_ok"], 1)
            flat = both[:].rearrange("p t e -> p (t e)")
            for i in range(2):
                cols = slice(SEQ * i, SEQ * (i + 1))
                nc.tensor.matmul(ps_same[i][:], same[:], flat[:, cols], start=True, stop=True)
                nc.tensor.matmul(ps_part[i][:], later[:], flat[:, cols], start=True, stop=True)
            pe.wait_ge(S["tot_ok"], 1)
            nc.tensor.matmul(ps_base[:, 0, :], below[:], total[:], start=True, stop=True)
            nc.tensor.matmul(ps_base[:, 1, :], ones[:], total[:], start=True, stop=True).then_inc(S["counted"], 1)

        @block.vector
        def _(dve):
            tt, ts, stt = nc.vector.tensor_tensor, nc.vector.tensor_scalar, nc.vector.scalar_tensor_tensor
            dve.wait_ge(S["tab"], TABLES_R)

            def per_expert(row):
                return row[:].unsqueeze(1).to_broadcast(block_shape)

            def per_token(col):
                return col.unsqueeze(2).to_broadcast(block_shape)

            n = 0
            for k in range(TOP):
                src = lg_all if k == 0 else rest
                nc.vector.tensor_reduce(m[:, k, :], src[:], AX_X, ALU.max).then_inc(S["seq"], 1)
                n += 1
                dve.wait_ge(S["seq"], n)
                tt(flag[:], src[:], per_token(m[:, k, :]), ALU.is_lt).then_inc(S["seq"], 1)
                n += 1
                dve.wait_ge(S["seq"], n)
                stt(flag[:], flag[:], float(NE), per_expert(expert), ALU.mult, ALU.add).then_inc(S["seq"], 1)
                n += 1
                dve.wait_ge(S["seq"], n)
                nc.vector.tensor_reduce(pick[:], flag[:], AX_X, ALU.min).then_inc(S["seq"], 1)
                n += 1
                dve.wait_ge(S["seq"], n)
                if k == 1:
                    tt(ex[:], m[:, 1, :], m[:, 0, :], ALU.subtract).then_inc(S["seq"], 1)
                    n += 1
                tt(hot[k][:], per_expert(expert), per_token(pick[:]), ALU.is_equal).then_inc(S["seq"], 1)
                n += 1
                dve.wait_ge(S["seq"], n)
                if k == 0:
                    stt(rest[:], hot[0][:], MASKED, lg_all[:], ALU.mult, ALU.add).then_inc(S["seq"], 1)
                    n += 1
                    dve.wait_ge(S["seq"], n)
            tt(both[:], hot[0][:], hot[1][:], ALU.add).then_inc(S["both_ok"], 1)
            dve.wait_ge(S["both_ok"], 1)
            nc.vector.tensor_reduce(total[:], both[:].rearrange("p t e -> p e t"), AX_X, ALU.add).then_inc(S["tot_ok"], 1)
            dve.wait_ge(S["ex_ok"], 1)
            ts(pick[:], ex[:], 1.0, None, ALU.add).then_inc(S["seq"], 1)
            n += 1
            dve.wait_ge(S["seq"], n)
            nc.vector.reciprocal(m[:, 0, :], pick[:]).then_inc(S["seq"], 1)
            n += 1
            dve.wait_ge(S["seq"], n)
            tt(m[:, 1, :], ex[:], m[:, 0, :], ALU.mult).then_inc(S["seq"], 1)
            n += 1

            dve.wait_ge(S["counted"], 1)
            half = NTILE // 2
            for i in range(2):
                same_v = ps_same[i][:].rearrange("p (t e) -> p t e", e=NE)
                for e in range(NE):
                    start = 0.0 if i == 0 else rank[:, half - 1, e:e + 1]
                    out = rank[:, half * i:half * (i + 1), e]
                    nc.vector.tensor_tensor_scan(out, ones[:, 0:half], same_v[:, :, e], start, ALU.mult, ALU.add
                                                 ).then_inc(S["seq"], 1)
                    n += 1
                dve.wait_ge(S["seq"], n)
            for i in range(2):
                part = ps_part[i][:].rearrange("p (t e) -> p t e", e=NE)
                rows = rank[:, half * i:half * (i + 1), :]
                tt(rows, rows, part, ALU.add).then_inc(S["seq"], 1)
                n += 1
            dve.wait_ge(S["seq"], n)
            tt(rank[:], rank[:], ps_base[:, 0, :].unsqueeze(1).to_broadcast(block_shape), ALU.add).then_inc(S["seq"], 1)
            n += 1
            dve.wait_ge(S["seq"], n)
            ts(flag[:], rank[:], CAP - 0.5, NOWHERE, ALU.is_gt, ALU.mult).then_inc(S["seq"], 1)
            n += 1
            dve.wait_ge(S["seq"], n)
            tt(rank[:], rank[:], flag[:], ALU.add).then_inc(S["seq"], 1)
            n += 1
            dve.wait_ge(S["seq"], n)
            tt(rank[:], rank[:], per_expert(row0), ALU.add).then_inc(S["seq"], 1)
            n += 1
            dve.wait_ge(S["seq"], n)
            for k in range(TOP):
                tt(hot[k][:], hot[k][:], rank[:], ALU.mult).then_inc(S["seq"], 1)
                n += 1
                dve.wait_ge(S["seq"], n)
                nc.vector.tensor_reduce(dst[:, k, :], hot[k][:], AX_X, ALU.add).then_inc(S["seq"], 1)
                n += 1
                dve.wait_ge(S["seq"], n)
            nc.vector.tensor_copy(dst_row[:], dst[:]).then_inc(S["seq"], 1)
            n += 1
            ts(keep[:], dst[:], NOWHERE - 0.5, None, ALU.is_lt).then_inc(S["seq"], 1)
            n += 1
            dve.wait_ge(S["seq"], n)
            tt(kdst[:], dst[:], keep[:], ALU.mult).then_inc(S["seq"], 1)
            n += 1
            dve.wait_ge(S["seq"], n)
            nc.vector.tensor_copy(src_row[:], kdst[:]).then_inc(S["seq"], 1)
            n += 1
            tt(prob[:], m[:], keep[:], ALU.mult).then_inc(S["seq"], 1)
            n += 1

            ts(count[:], ps_base[0:1, 1, :], float(CAP), None, ALU.min).then_inc(S["seq"], 1)
            n += 1
            dve.wait_ge(S["seq"], n)
            shape = [1, NE, MAX_PAIRS - 1]
            tt(over[:], count[:].unsqueeze(2).to_broadcast(shape), steps[:].unsqueeze(1).to_broadcast(shape), ALU.is_gt
               ).then_inc(S["seq"], 1)
            tt(planf[:, 1, :], count[:], row0[0:1, :], ALU.add).then_inc(S["seq"], 1)
            n += 2
            dve.wait_ge(S["seq"], n)
            nc.vector.tensor_reduce(planf[:, 0, :], over[:], AX_X, ALU.add).then_inc(S["seq"], 1)
            n += 1
            dve.wait_ge(S["seq"], n)
            ts(planf[:, 0, :], planf[:, 0, :], 1.0, None, ALU.add).then_inc(S["seq"], 1)
            n += 1
            dve.wait_ge(S["seq"], n)
            nc.vector.tensor_copy(plan[:], planf[:]).then_inc(S["seq"], 1)
            n += 1
            dve.wait_ge(S["seq"], n)


TABLES_R = 6 + 16 + 10 + 16 + 2 * NE + MAX_PAIRS - 1


def dispatch_stage(nc, xc_dram, xd_dram, dst_row, plan):
    ctx = ExitStack()
    with ctx:
        rows = [ctx.enter_context(nc.sbuf_tensor(f"d_rows{i}", [P, GT, DM], F32)) for i in range(2)]
        idx = [ctx.enter_context(nc.sbuf_tensor(f"d_idx{i}", [P, TOP, GT], I32)) for i in range(2)]
        zero = ctx.enter_context(nc.sbuf_tensor("d_zero", [P, PAIR // P, DM], F32))
        names = "ld0 ld1 idx_ok zeroed scat0 scat1 zst".split()
        S = {n: ctx.enter_context(nc.semaphore("d_" + n)) for n in names}
        block = ctx.enter_context(nc.Block())

        @block.sync
        def _(sp):
            def load(g, i):
                sp.dma_start(rows[i][:], xc_dram[:, bass.ds(g * GT, GT), :]).then_inc(S[f"ld{i}"], 16)

            for i in range(2):
                load(i, i)
            sp.wait_ge(S["zeroed"], 1)
            for e in range(NE):
                row = sp.value_load(plan[0:1, 1, e:e + 1], min_val=0, max_val=NE * CAP_ROWS - PAIR)
                sp.dma_start(xd_dram[bass.ds(row, PAIR), :].rearrange("(p j) c -> p j c", p=P), zero[:]
                             ).then_inc(S["zst"], 16)
            with sp.Fori(1, NGT // 2) as h:
                for i in range(2):
                    sp.wait_ge(S[f"scat{i}"], 16 * TOP * GT * h)
                    load(2 * h + i, i)
            sp.wait_ge(S["zst"], 16 * NE)

        @block.gpsimd
        def _(pool):
            pool.memset(zero[:], 0.0).then_inc(S["zeroed"], 1)
            pool.wait_ge(S["zeroed"], 1)

            def step(h, i):
                g = 2 * h + i
                if not isinstance(h, int):
                    pool.wait_ge(S[f"scat{i}"], 16 * TOP * GT * h)
                pool.tensor_copy(idx[i][:], dst_row[:, :, bass.ds(g * GT, GT)]).then_inc(S["idx_ok"], 1)
                pairs = [(S["idx_ok"], g + 1), (S[f"ld{i}"], 16 * (h + 1))]
                pairs = [(s, v if isinstance(v, int) else pool.to_reg(v)) for s, v in pairs]
                pool.wait_ge(S["zeroed"], 1)
                for s, v in pairs:
                    pool.wait_ge(s, v)
                for j in range(GT):
                    for k in range(TOP):
                        pool.indirect_dma_start(out=xd_dram, out_offset=bass.IndirectOffsetOnAxis(
                            ap=idx[i][:, k, j:j + 1].bitcast(U32), axis=0), in_=rows[i][:, j, :], in_offset=None,
                            bounds_check=NE * CAP_ROWS - 1, oob_is_err=False).then_inc(S[f"scat{i}"], 16)

            for i in range(2):
                step(0, i)
            with pool.Fori(1, NGT // 2) as h:
                for i in range(2):
                    step(h, i)
            for i in range(2):
                pool.wait_ge(S[f"scat{i}"], 16 * TOP * GT * NGT // 2)


def expert_stage(nc, w1_dram, w2_dram, lnw_dram, xd_dram, y_dram, plan):
    ctx = ExitStack()
    with ctx:
        def sb(name, shape, dt=F32):
            return ctx.enter_context(nc.sbuf_tensor(name, shape, dt))

        ident = sb("e_ident", [P, P])
        ln = sb("e_ln", [P, 2, KD])
        w1 = [sb(f"e_w1{i}", [P, KD, FF]) for i in range(2)]
        w2 = [sb(f"e_w2{i}", [P, MF, DM]) for i in range(2)]
        x = [sb(f"e_x{i}", [P, HT, DM]) for i in range(2)]
        xt = [sb(f"e_xt{i}", [P, KD, HALF]) for i in range(2)]
        a = [sb(f"e_a{i}", [P, MF, HALF]) for i in range(2)]
        y = [sb(f"e_y{i}", [P, HT, DM]) for i in range(2)]
        zero = sb("e_zero", [P, PAIR // P, DM])
        pt = [ctx.enter_context(nc.psum_tensor(f"e_pt{i}", [P, KD, HALF], F32)) for i in range(2)]
        p1 = [ctx.enter_context(nc.psum_tensor(f"e_p1{i}", [P, 2, HALF], F32)) for i in range(4)]
        p2 = [ctx.enter_context(nc.psum_tensor(f"e_p2{j}", [P, 2, DM], F32)) for j in range(HT)]
        names = "c0 zeroed zst ld_w0 ld_w1 ld_x0 ld_x1 t_ps xt_ok f1_ps a_ok f2_ps y_ok st0 st1".split()
        S = {n: ctx.enter_context(nc.semaphore("e_" + n)) for n in names}
        block = ctx.enter_context(nc.Block())

        def wait_apart(eng, *waits):
            waits = [(S[s], v if isinstance(v, int) else eng.to_reg(v)) for s, v in waits]
            eng.wait_ge(S["c0"], 1)
            for semaphore, value in waits:
                eng.wait_ge(semaphore, value)

        def experts(eng, name, turn, weights=None, rest=None):
            done = eng.alloc_register(name)
            eng.reg_mov(done, 0)
            with eng.Fori(0, NE // 2) as pair:
                for i in range(2):
                    e = 2 * pair + i
                    turns = eng.value_load(plan[0:1, 0, bass.ds(e, 1)], min_val=1, max_val=MAX_PAIRS)
                    if weights:
                        weights(pair, i, eng.snap(done))
                    with eng.Fori(0, turns) as c:
                        turn(pair, i, c, eng.snap(done))
                        eng.reg_add(done, done, 1)
                    if rest:
                        rest(pair, i, turns)
            return eng.snap(done)

        @block.sync
        def _(sp):
            sp.wait_ge(S["zeroed"], 1)

            def turn(pair, i, c, q):
                for n in range(2):
                    sp.wait_ge(S["t_ps"], 2 * q + n + 1)
                    rows = xd_dram[bass.ds((2 * pair + i) * CAP_ROWS + c * PAIR + n * HALF, HALF), :]
                    sp.dma_start(x[n][:], rows.rearrange("(p j) c -> p j c", p=P)).then_inc(S[f"ld_x{n}"], 16)

            zeros = sp.alloc_register("e_zeros")
            sp.reg_mov(zeros, 0)

            def rest(pair, i, turns):
                with sp.Fori(turns, CAP_ROWS // PAIR) as c:
                    rows = y_dram[bass.ds((2 * pair + i) * CAP_ROWS + c * PAIR, PAIR), :]
                    sp.dma_start(rows.rearrange("(p j) c -> p j c", p=P), zero[:]).then_inc(S["zst"], 16)
                    sp.reg_add(zeros, zeros, 1)

            q = experts(sp, "e_sp", turn, rest=rest)
            sp.wait_ge(S["t_ps"], 2 * q + 1)
            sp.dma_start(x[0][:], xd_dram[0:HALF, :].rearrange("(p j) c -> p j c", p=P)).then_inc(S["ld_x0"], 16)
            wait_apart(sp, ("ld_x0", 16 * q + 16), ("zst", 16 * sp.snap(zeros)))

        @block.gpsimd
        def _(pool):
            pool.memset(zero[:], 0.0).then_inc(S["zeroed"], 1)
            pool.wait_ge(S["zeroed"], 1)
            pool.memset(ident[:], 0.0).then_inc(S["c0"], 1)
            pool.wait_ge(S["c0"], 1)
            pool.affine_select(out=ident[:], in_=ident[:], compare_op=ALU.not_equal, fill=1.0, base=0,
                               pattern=[[-1, P]], channel_multiplier=1).then_inc(S["c0"], 1)
            for n in range(2):
                pool.dma_start(ln[:, n, :], lnw_dram[:, n, :]).then_inc(S[f"st{n}"], 16)

            def load_weights(e, i):
                pool.dma_start(w1[i][:], w1_dram[bass.ds(e * DM, DM), :].rearrange("(k p) f -> p k f", p=P)
                               ).then_inc(S[f"ld_w{i}"], 16)
                pool.dma_start(w2[i][:], w2_dram[bass.ds(e * FF, FF), :].rearrange("(m p) c -> p m c", p=P)
                               ).then_inc(S[f"ld_w{i}"], 16)

            load_weights(0, 0)

            def weights(pair, i, q):
                pool.wait_ge(S["f2_ps"], 2 * q + 1)
                load_weights((2 * pair + i + 1) % NE, 1 - i)

            def turn(pair, i, c, q):
                for n in range(2):
                    pool.wait_ge(S["y_ok"], 2 * q + n + 2)
                    rows = y_dram[bass.ds((2 * pair + i) * CAP_ROWS + c * PAIR + n * HALF, HALF), :]
                    pool.dma_start(rows.rearrange("(p j) c -> p j c", p=P), y[n][:]).then_inc(S[f"st{n}"], 16)

            q = experts(pool, "e_pool", turn, weights)
            wait_apart(pool, ("st0", 16 * q + 16), ("st1", 16 * q + 16))
            pool.wait_ge(S["ld_w0"], 32 * (NE // 2 + 1))
            pool.wait_ge(S["ld_w1"], 32 * (NE // 2))

        @block.tensor
        def _(pe):
            mm = nc.tensor.matmul
            pe.nop().then_inc(S["t_ps"], 2)
            pe.nop().then_inc(S["f1_ps"], 1)
            pe.nop().then_inc(S["f2_ps"], 1)
            pe.wait_ge(S["c0"], 2)

            def turn_rows(q, n):
                pe.wait_ge(S[f"ld_x{n}"], 16 * q + 16)
                pe.wait_ge(S["xt_ok"], 2 * q + n + 1)
                for k in range(KD):
                    for j in range(HT):
                        i = nc.tensor.transpose(pt[n][:, k, j * P:(j + 1) * P], x[n][:, j, k * P:(k + 1) * P], ident[:])
                i.then_inc(S["t_ps"], 1)

            pe.wait_ge(S["ld_x0"], 16)
            for k in range(KD):
                for j in range(HT):
                    i = nc.tensor.transpose(pt[0][:, k, j * P:(j + 1) * P], x[0][:, j, k * P:(k + 1) * P], ident[:])
            i.then_inc(S["t_ps"], 1)

            def turn(pair, i, c, q):
                pe.wait_ge(S[f"ld_w{i}"], 32 * pair + 32)
                for n in range(2):
                    pe.wait_ge(S["xt_ok"], 2 * q + n + 3)
                    for m in range(MF):
                        if m == 0:
                            pe.wait_ge(S["a_ok"], 4 * q + 2 * n + 1)
                        bank = p1[2 * n + m // 2]
                        for k in range(KD):
                            o = mm(bank[:, m % 2, :], w1[i][:, k, m * P:(m + 1) * P], xt[n][:, k, :],
                                   start=(k == 0), stop=(k == KD - 1))
                        if m % 2:
                            o.then_inc(S["f1_ps"], 1)
                    turn_rows(q + n, 1 - n)
                    pe.wait_ge(S["y_ok"], 2 * q + n + 1)
                    for m in range(MF):
                        if m % 2 == 0:
                            pe.wait_ge(S["a_ok"], 4 * q + 2 * n + m // 2 + 2)
                        for j in range(HT):
                            o = mm(p2[j][:, n, :], a[n][:, m, j * P:(j + 1) * P], w2[i][:, m, :],
                                   start=(m == 0), stop=(m == MF - 1))
                    o.then_inc(S["f2_ps"], 1)

            experts(pe, "e_pe", turn)

        @block.scalar
        def _(act):
            act.nop().then_inc(S["a_ok"], 1)

            def turn(pair, i, c, q):
                for n in range(2):
                    for b in range(2):
                        act.wait_ge(S["f1_ps"], 4 * q + 2 * n + b + 2)
                        act.wait_ge(S["f2_ps"], 2 * q + n + 1)
                        act.activation(a[n][:, 2 * b:2 * b + 2, :], p1[2 * n + b][:], ACT.Gelu_apprx_tanh
                                       ).then_inc(S["a_ok"], 1)

            experts(act, "e_act", turn)

        @block.vector
        def _(dve):
            ts = nc.vector.tensor_scalar
            for n in range(2):
                dve.wait_ge(S[f"st{n}"], 16)
            dve.wait_ge(S["c0"], 2)
            dve.nop().then_inc(S["xt_ok"], 2)
            dve.nop().then_inc(S["y_ok"], 1)

            def move(q, n, first=False):
                dve.wait_ge(S["t_ps"], 2 * q + n + 3)
                if not first:
                    dve.wait_ge(S["f1_ps"], 4 * q + 2 * n - 1)
                for k in range(KD):
                    o = ts(xt[n][:, k, :], pt[n][:, k, :], ln[:, 0, k:k + 1], ln[:, 1, k:k + 1], ALU.mult, ALU.add)
                o.then_inc(S["xt_ok"], 1)

            move(0, 0, True)

            def turn(pair, i, c, q):
                for n in range(2):
                    move(q + n, 1 - n)
                    dve.wait_ge(S["f2_ps"], 2 * q + n + 2)
                    dve.wait_ge(S[f"st{n}"], 16 * q + 16)
                    for j in range(HT):
                        o = nc.vector.tensor_copy(y[n][:, j, :], p2[j][:, n, :])
                    o.then_inc(S["y_ok"], 1)

            experts(dve, "e_dve", turn)


def combine_stage(nc, base_dram, y_dram, out, src_row, prob):
    ctx = ExitStack()
    with ctx:
        def sb(name, shape, dt=F32):
            return [ctx.enter_context(nc.sbuf_tensor(f"{name}{i}", shape, dt)) for i in range(2)]

        b, idx, o = sb("o_b", [P, GT, DM]), sb("o_idx", [P, TOP, GT], I32), sb("o_o", [P, GT, DM])
        yr = sb("o_y", [P, TOP, GT, DM])
        names = "c0 ld0 ld1 idx_ok gath0 gath1 part sum st0 st1".split()
        S = {n: ctx.enter_context(nc.semaphore("o_" + n)) for n in names}
        block = ctx.enter_context(nc.Block())
        out_v = out.rearrange("(s b) c -> b s c", s=NSEQ)

        def steps(eng, step):
            for i in range(2):
                step(0, i)
            with eng.Fori(1, NGT // 2) as h:
                for i in range(2):
                    step(h, i)

        @block.sync
        def _(sp):
            def step(h, i):
                g = 2 * h + i
                if not isinstance(h, int):
                    sp.wait_ge(S["part"], GT * (g - 1))
                sp.dma_start(b[i][:], base_dram[:, bass.ds(g * GT, GT), :]).then_inc(S[f"ld{i}"], 16)

            steps(sp, step)
            for i in range(2):
                sp.wait_ge(S[f"ld{i}"], 16 * NGT // 2)

        @block.scalar
        def _(act):
            def step(h, i):
                g = 2 * h + i
                act.wait_ge(S["sum"], GT * (g + 1))
                for j in range(GT):
                    act.dma_start(out_v[bass.ds(g * 4 * GT + 4 * j, 4), :, :], o[i][:, j, :]).then_inc(S[f"st{i}"], 16)

            steps(act, step)
            for i in range(2):
                act.wait_ge(S[f"st{i}"], 16 * GT * NGT // 2)

        @block.gpsimd
        def _(pool):
            pool.nop().then_inc(S["c0"], 1)

            def step(h, i):
                g = 2 * h + i
                if not isinstance(h, int):
                    pool.wait_ge(S[f"gath{i}"], 16 * TOP * GT * h)
                pool.tensor_copy(idx[i][:], src_row[:, :, bass.ds(g * GT, GT)]).then_inc(S["idx_ok"], 1)
                pairs = [(S["idx_ok"], g + 1)] + ([] if isinstance(h, int) else [(S["sum"], GT * (g - 1))])
                pairs = [(s, v if isinstance(v, int) else pool.to_reg(v)) for s, v in pairs]
                pool.wait_ge(S["c0"], 1)
                for s, v in pairs:
                    pool.wait_ge(s, v)
                for j in range(GT):
                    for k in range(TOP):
                        pool.indirect_dma_start(out=yr[i][:, k, j, :], out_offset=None, in_=y_dram,
                                                in_offset=bass.IndirectOffsetOnAxis(
                                                    ap=idx[i][:, k, j:j + 1].bitcast(U32), axis=0)
                                                ).then_inc(S[f"gath{i}"], 16)

            steps(pool, step)

        @block.vector
        def _(dve):
            stt = nc.vector.scalar_tensor_tensor

            def step(h, i):
                g = 2 * h + i
                dve.wait_ge(S[f"ld{i}"], 16 * (h + 1))
                dve.wait_ge(S[f"gath{i}"], 16 * TOP * GT * (h + 1))
                if not isinstance(h, int):
                    dve.wait_ge(S[f"st{i}"], 16 * GT * h)
                for j in range(GT):
                    stt(yr[i][:, 0, j, :], yr[i][:, 0, j, :], prob[:, 0, bass.ds(g * GT + j, 1)], b[i][:, j, :],
                        ALU.mult, ALU.add).then_inc(S["part"], 1)
                for j in range(GT):
                    dve.wait_ge(S["part"], GT * g + j + 1)
                    stt(o[i][:, j, :], yr[i][:, 1, j, :], prob[:, 1, bass.ds(g * GT + j, 1)], yr[i][:, 0, j, :],
                        ALU.mult, ALU.add).then_inc(S["sum"], 1)

            steps(dve, step)


def build(nc, h, out):
    n_rows = NE * CAP_ROWS
    h1_dram = nc.dram_tensor("h1_rows", [NSEQ * SEQ, DM], F32).ap()
    base_dram = nc.dram_tensor("base_rows", [P, NTILE, DM], F32).ap()
    xc_dram = nc.dram_tensor("xc_rows", [P, NTILE, DM], F32).ap()
    xd_dram = nc.dram_tensor("expert_in", [n_rows, DM], F32).ap()
    y_dram = nc.dram_tensor("expert_out", [n_rows, DM], F32).ap()
    mamba_w = [{k[:-1]: v for k, v in h.items() if k.endswith(str(d))} for d in range(DIRS)]
    mamba_stage(nc, h["ids"], h["table"], mamba_w, h1_dram)
    with ExitStack() as ctx:
        dst_row = ctx.enter_context(nc.sbuf_tensor("dst_row", [P, TOP, NTILE], I32))
        src_row = ctx.enter_context(nc.sbuf_tensor("src_row", [P, TOP, NTILE], I32))
        prob = ctx.enter_context(nc.sbuf_tensor("prob", [P, TOP, NTILE], F32))
        plan = ctx.enter_context(nc.sbuf_tensor("plan", [1, 2, NE], I32))
        lg_all = ctx.enter_context(nc.sbuf_tensor("lg_all", [P, NTILE, NE], F32))
        attention_stage(nc, h, h1_dram, base_dram, xc_dram, lg_all)
        routing_stage(nc, lg_all, dst_row, src_row, prob, plan)
        dispatch_stage(nc, xc_dram, xd_dram, dst_row, plan)
        expert_stage(nc, h["moe_w1"], h["moe_w2"], h["ln2"], xd_dram, y_dram, plan)
        combine_stage(nc, base_dram, y_dram, out, src_row, prob)


def per_chunk(v):
    return v.reshape(-1, P).T


def mamba_layout(i):
    out = {}
    for d, suffix in enumerate("fb"):
        def g(name):
            return i[f"L0_attn_{name}_{suffix}"]
        wx = g("Wx")
        out[f"Win{d}"] = g("Win").T
        out[f"Wx{d}"] = np.concatenate([wx[RK:], wx[:RK]]).T
        out[f"Wdt{d}"] = g("Wdt").T
        out[f"Wout{d}"] = g("Wout").T
        out[f"Wfuse{d}"] = i["L0_attn_Wfuse"][:, DM * d:DM * (d + 1)].T
        out[f"convw{d}"] = g("convw")
        out[f"Alog{d}"] = g("Alog")
        for name in ("convb", "bdt", "Dp", "ln_g", "ln_b"):
            out[f"{name}{d}"] = per_chunk(g(name))
    out["bfuse0"] = i["L0_attn_bfuse"].reshape(1, DM)
    return out


def attention_layout(i):
    f = "L0_ffn_"
    w = i[f + "qkv_weight"].reshape(NG, NQ + 2, HD, DM)
    wq = np.zeros((DM, NQ + 1, NG, S_A), w.dtype)
    wq[..., :HD] = w[:, :NQ + 1].transpose(3, 1, 0, 2)
    ln = {n: np.stack([per_chunk(i[f + "ln1_" + n]), per_chunk(i[f + "ln2_" + n])], 1) for n in ("weight", "bias")}
    return dict(
        wq=wq.reshape(DM, NQ + 1, P),
        wv=w[:, NQ + 1].transpose(2, 0, 1).reshape(DM, NG * HD),
        wp=i[f + "proj_weight"].reshape(DM, NG, NQ, HD).transpose(1, 3, 2, 0).reshape(NG * HD, NQ, DM),
        wr=i[f + "router_weight"],
        lnw=ln["weight"],
        lnb=ln["bias"],
        ln2=np.stack([per_chunk(i[f + "ln2_weight"]), per_chunk(i[f + "ln2_bias"])], 1),
        moe_w1=i[f + "moe_w1"].reshape(NE * DM, FF),
        moe_w2=i[f + "moe_w2"].reshape(NE * FF, DM),
    )


def ids_layout(x):
    ids = x.reshape(NSEQ, TT, P).transpose(2, 0, 1).reshape(P, NSEQ * TT)
    return np.concatenate([ids, np.zeros((P, 2 * TT), ids.dtype)], 1)


def kernel(**inputs):
    import concourse.bacc as _bacc
    from concourse.bass_utils import run_bass_kernel_spmd as _run

    i = {k: np.asarray(v) for k, v in inputs.items()}
    arrays = {**mamba_layout(i), **attention_layout(i), "ids": ids_layout(i["x"]), "table": i["L0_tok_W"].T}
    arrays = {k: np.ascontiguousarray(v) for k, v in arrays.items()}
    nc = _bacc.Bacc("TRN2", target_bir_lowering=False, num_devices=1)
    handles = {k: nc.dram_tensor("in_" + k, v.shape, mybir.dt.from_np(v.dtype), kind="ExternalInput").ap()
               for k, v in arrays.items()}
    out = nc.dram_tensor("out", [NSEQ * SEQ, DM], F32, kind="ExternalOutput").ap()
    build(nc, handles, out)
    results = _run(nc, [{"in_" + k: v for k, v in arrays.items()}], core_ids=[0]).results
    return np.asarray(results[0]["out"]).reshape(NSEQ, SEQ, DM)
```

```python
import numpy as np

from contextlib import ExitStack

import concourse.bass as bass
from concourse import mybir

F32 = mybir.dt.float32
F32R = mybir.dt.float32r
BF16 = mybir.dt.bfloat16
I32 = mybir.dt.int32
U32 = mybir.dt.uint32
ALU = mybir.AluOpType
ACT = mybir.ActivationFunctionType
AX_X = mybir.AxisListType.X

P = 128
DM = 256
KD = DM // P
DI = 512
MD = DI // P
NS = 32
RK = 16
NX = 2 * NS + RK
TAPS = 4
SEQ = 512
NSEQ = 32
TT = SEQ // P
PAD = TAPS - 1
EPS = 1e-5
DIRS = 2
LN2 = 0.6931471805599453
PARTS = ((0, 0), (0, 1), (1, 0))
DEAD_LOG = 5.5
ALOG_TOP = 80.0


def mamba_stage(nc, tok_ids, table, w, h1_dram):
    ctx = ExitStack()
    with ctx:
        def sb(name, shape, dt=F32):
            return ctx.enter_context(nc.sbuf_tensor(name, shape, dt))

        def sem(name):
            return ctx.enter_context(nc.semaphore(name))

        win = [[sb(f"win{d}{h}", [P, KD, 2 * DI], F32R) for h in range(2)] for d in range(DIRS)]
        wx = [sb(f"wx{d}", [P, MD, NX]) for d in range(DIRS)]
        wdt = [sb(f"wdt{d}", [P, DI]) for d in range(DIRS)]
        wdta = [sb(f"wdta{d}", [P, DI]) for d in range(DIRS)]
        wout = [sb(f"wout{d}", [P, MD, DM]) for d in range(DIRS)]
        wfus = [sb(f"wfus{d}", [P, KD, DM]) for d in range(DIRS)]
        convw = [sb(f"convw{d}", [P, MD, TAPS]) for d in range(DIRS)]
        convb = [sb(f"convb{d}", [P, MD]) for d in range(DIRS)]
        bdt = [sb(f"bdt{d}", [P, MD]) for d in range(DIRS)]
        dp = [sb(f"dp{d}", [P, MD]) for d in range(DIRS)]
        amat = [sb(f"amat{d}", [P, MD, NS]) for d in range(DIRS)]
        almin = [sb(f"almin{d}", [P, MD]) for d in range(DIRS)]
        alok = [sb(f"alok{d}", [P, MD]) for d in range(DIRS)]
        alb = [sb(f"alb{d}", [P, MD]) for d in range(DIRS)]
        lng = [sb(f"lng{d}", [P, KD]) for d in range(DIRS)]
        lnb = [sb(f"lnb{d}", [P, KD]) for d in range(DIRS)]
        bfus = sb("bfus", [1, DM])
        wmean = sb("wmean", [P, DIRS, MD])
        cvec = sb("cvec", [P, DM])
        ident = sb("ident", [P, P])
        ones = sb("ones", [P, P])
        neg_half = sb("neg_half", [P, TT])
        smask0 = sb("smask0", [NS, P])

        ids = sb("ids", [P, (NSEQ + 2) * TT], I32)
        idc = sb("idc", [P, TT], I32)
        g = sb("g", [P, TT, DM])
        stats = sb("stats", [P, TT, 6])
        mv = sb("mv", [P, TT, 2])
        rstd = sb("rstd", [P, TT])
        xn = sb("xn", [P, TT, DM])
        xt = [sb(f"xt{h}", [P, KD, SEQ], F32R) for h in range(2)]
        h0c = sb("h0c", [P, 2, TT, DM])
        h1o = sb("h1o", [P, TT, DM])
        u = sb("u", [P, MD, SEQ + 2 * PAD])
        uc = [sb(f"uc{d}", [P, MD, SEQ]) for d in range(DIRS)]
        zs = [sb(f"zs{d}", [P, MD, SEQ]) for d in range(DIRS)]
        xd = [sb(f"xd{d}", [P, SEQ]) for d in range(DIRS)]
        bcp = sb("bcp", [NS, SEQ])
        bb = [sb(f"bb{d}", [P, 2, SEQ]) for d in range(DIRS)]
        v = sb("v", [P, MD, SEQ])
        y = sb("y", [P, MD, SEQ])
        lg = sb("lg", [P, MD, SEQ])
        wk = sb("wk", [P, MD, SEQ])
        yz = sb("yz", [P, MD, SEQ])
        qq = sb("qq", [P, MD, SEQ])
        tp = sb("tp", [P, MD, SEQ])
        fo = sb("fo", [P, KD, SEQ])
        sq = sb("sq", [P, KD, SEQ])
        r2 = sb("r2", [P, TT])
        r3 = sb("r3", [P, TT])
        xmax = sb("xmax", [P, 1])
        dgt = sb("dgt", [P, MD])
        dct = sb("dct", [P, 1])
        dall = sb("dall", [P, 1])
        live = sb("live", [P, DIRS], I32)
        smask = sb("smask", [NS, P])
        eh = sq[:, 0, :]

        pj = [ctx.enter_context(nc.psum_tensor(f"pj{i}", [P, SEQ], F32)) for i in range(2)]
        px = ctx.enter_context(nc.psum_tensor("px", [P, SEQ], F32))
        pss = [ctx.enter_context(nc.psum_tensor(f"pss{i}", [P, SEQ], F32)) for i in range(DIRS)]
        po = [ctx.enter_context(nc.psum_tensor(f"po{i}", [P, SEQ], F32)) for i in range(3)]

        bc_dram = [nc.dram_tensor(f"bc{d}", [2 * NS, SEQ], F32).ap() for d in range(DIRS)]

        names = """c_tab cv xl_ok ld_w ld_ids prep_a prep_w prep_v idc_ok gath st_ok lnv_ok lnr_ok xn_ok xt_ps xt_ok h0_ok
          u_ps u_ok a_ok z_ps z_ok uc_ok xd_ps xd_ok bc_ok bcast xd_st dt_ps v_ok vc_ok y_ok l_ok w_ok g_ok
          d0_ok dt_ok dtu_ok tp_ok da_ok h_ok hc_ok q_ok q2_ok yv_ok yz_ok xm_ok qd_ps gt_ok ct_ok cnt_ps
          fl_ok s_ps o_ps fo_ok sq_ok ss_ps rv_ok rr_ok f_ps fin_ok h1_st gt2 e_bc e_da e_tp e_h e_hc e_y""".split()
        S = {n: sem("m_" + n) for n in names}

        block = ctx.enter_context(nc.Block())

        def wait_apart(eng, semaphore, value):
            value = value if isinstance(value, int) else eng.to_reg(value)
            eng.wait_ge(S["c_tab"], 1)
            eng.wait_ge(semaphore, value)

        def last_tap(m):
            return 6 * (m // 2) + 5 + m % 2

        def xd_rows(d):
            return xd[d][2 * NS:NX, :]

        @block.sync
        def _(sp):
            for d in range(DIRS):
                k = w[d]
                stage = (v, lg)[d][:].rearrange("p m n -> p (m n)").rearrange("p (k e) -> p k e", k=KD)
                sp.dma_start(stage, k["Win"].rearrange("(k p) e -> p k e", p=P)).then_inc(S["ld_w"], 16)
                sp.dma_start(wx[d][:], k["Wx"].rearrange("(m p) e -> p m e", p=P)).then_inc(S["ld_w"], 16)
                sp.dma_start(wdt[d][2 * NS:NX, :], k["Wdt"]).then_inc(S["ld_w"], 16)
                sp.dma_start(wout[d][:], k["Wout"].rearrange("(m p) e -> p m e", p=P)).then_inc(S["ld_w"], 16)
                sp.dma_start(wfus[d][:], k["Wfuse"].rearrange("(k p) e -> p k e", p=P)).then_inc(S["ld_w"], 16)
                sp.dma_start(convw[d][:], k["convw"].rearrange("(m p) e -> p m e", p=P)).then_inc(S["ld_w"], 16)
                sp.dma_start(amat[d][:], k["Alog"].rearrange("(m p) e -> p m e", p=P)).then_inc(S["ld_w"], 16)
                for dst, name in ((convb, "convb"), (bdt, "bdt"), (dp, "Dp"), (lng, "ln_g"), (lnb, "ln_b")):
                    sp.dma_start(dst[d][:], k[name]).then_inc(S["ld_w"], 16)
                if d == 0:
                    sp.dma_start(bfus[:], k["bfuse"]).then_inc(S["ld_w"], 16)
            sp.dma_start(ids[:], tok_ids).then_inc(S["ld_ids"], 16)

            def broadcast(t, d):
                if not (isinstance(t, int) and t < 2):
                    wait_apart(sp, S["hc_ok"], MD * (t - 1))
                wait_apart(sp, S["xd_ok"], t + 1)
                sp.dma_start(bc_dram[d], xd[d][0:2 * NS, :]).then_inc(S["xd_st"], 16)
                sp.wait_ge(S["xd_st"], 16 * (t + 1))
                sp.dma_start(bb[d][:], bc_dram[d][0:2 * NS:NS, :].partition_broadcast(P)).then_inc(S["bcast"], 16)

            def store(s):
                sp.wait_ge(S["fin_ok"], TT * (2 * s + 2))
                dst = h1_dram[bass.ds(s * SEQ, SEQ), :].rearrange("(j p) c -> p j c", p=P)
                sp.dma_start(dst, h1o[:]).then_inc(S["h1_st"], 16)

            def more_states(t, d):
                wait_apart(sp, S["fl_ok"], 4 * t + 3)
                go = sp.value_load(live[0:1, d:d + 1], min_val=0, max_val=1)
                with sp.If(go > 0):
                    with sp.Fori(1, NS) as n:
                        c = sp.snap(sp_count)
                        if not (isinstance(t, int) and t == 0):
                            sp.wait_ge(S["hc_ok"], MD * t)
                        wait_apart(sp, S["e_y"], c * MD + 1)
                        for i in range(2):
                            row = bc_dram[d][bass.ds(n + NS * i, 1), :].squeeze(0)
                            sp.dma_start(bb[1 - d][:, i, :], row.partition_broadcast(P)).then_inc(S["e_bc"], 16)
                        sp.reg_add(sp_count, sp_count, 1)
                    wait_apart(sp, S["e_y"], sp.snap(sp_count) * MD + 1)
                with sp.Else():
                    sp.nop()

            sp_count = sp.alloc_register("sp_states")
            sp.reg_mov(sp_count, 0)
            broadcast(0, 0)

            def slots(s, first):
                for d in range(DIRS):
                    t = 2 * s + d
                    more_states(t, d)
                    broadcast(t + 1, 1 - d)
                    if d == 1 and not first:
                        store(s - 1)

            slots(0, True)
            with sp.Fori(1, NSEQ) as s:
                slots(s, False)
            store(NSEQ - 1)
            sp.wait_ge(S["h1_st"], 16 * NSEQ)
            sp.wait_ge(S["bcast"], 16 * (2 * NSEQ + 1))

        @block.gpsimd
        def _(pool):
            pool.memset(ones[:], 1.0).then_inc(S["c_tab"], 1)
            pool.wait_ge(S["c_tab"], 1)
            pool.memset(neg_half[:], -0.5).then_inc(S["c_tab"], 1)
            pool.wait_ge(S["c_tab"], 2)
            pool.memset(u[:, :, 0:PAD], 0.0).then_inc(S["c_tab"], 1)
            pool.wait_ge(S["c_tab"], 3)
            pool.memset(u[:, :, PAD + SEQ:], 0.0).then_inc(S["c_tab"], 1)
            pool.wait_ge(S["c_tab"], 4)
            pool.memset(ident[:], 0.0).then_inc(S["c_tab"], 1)
            pool.wait_ge(S["c_tab"], 5)
            pool.affine_select(out=ident[:], in_=ident[:], compare_op=ALU.not_equal, fill=1.0, base=0,
                               pattern=[[-1, P]], channel_multiplier=1).then_inc(S["c_tab"], 1)
            pool.wait_ge(S["c_tab"], 6)
            pool.affine_select(out=smask0[:], in_=ones[0:NS, :], compare_op=ALU.is_gt, fill=0.0, base=0,
                               pattern=[[0, P]], channel_multiplier=1).then_inc(S["c_tab"], 1)
            pool.wait_ge(S["c_tab"], 7)
            pool.wait_ge(S["ld_ids"], 16)

            def gather(s):
                if not (isinstance(s, int) and s == 0):
                    pool.wait_ge(S["gath"], 16 * TT * s)
                    pool.wait_ge(S["xn_ok"], TT * s)
                    pool.wait_ge(S["h0_ok"], s)
                pool.tensor_copy(idc[:], ids[:, bass.ds(s * TT, TT)]).then_inc(S["idc_ok"], 1)
                wait_apart(pool, S["idc_ok"], s + 1)
                for j in range(TT):
                    pool.indirect_dma_start(out=g[:, j, :], out_offset=None, in_=table,
                                            in_offset=bass.IndirectOffsetOnAxis(ap=idc[:, j:j + 1].bitcast(U32), axis=0)
                                            ).then_inc(S["gath"], 16)

            def ln_scale(s):
                wait_apart(pool, S["st_ok"], s + 1)
                pool.tensor_scalar(r3[:], mv[:, :, 1], 1.0, EPS, ALU.mult, ALU.add).then_inc(S["lnv_ok"], 1)
                pool.wait_ge(S["lnv_ok"], s + 1)
                pool.tensor_tensor(rstd[:], r3[:], neg_half[:], ALU.pow).then_inc(S["lnr_ok"], 1)

            def keep_residual(s):
                if not (isinstance(s, int) and s < 2):
                    pool.wait_ge(S["fin_ok"], TT * (2 * s - 2))
                pool.wait_ge(S["prep_v"], 3 * DIRS + 2)
                pool.wait_ge(S["gath"], 16 * TT * (s + 1))
                pool.tensor_tensor(h0c[:, bass.ds(s % 2, 1)].squeeze(1), g[:],
                                   cvec[:].unsqueeze(1).to_broadcast([P, TT, DM]), ALU.add).then_inc(S["h0_ok"], 1)

            def scan_inputs(t, d):
                pool.wait_ge(S["bcast"], 16 * (t + 1))
                for m in range(MD):
                    pool.wait_ge(S["dt_ok"], MD * t + m + 1)
                    pool.tensor_tensor(wk[:, m, :], v[:, m, :], uc[d][:, m, :], ALU.mult).then_inc(S["dtu_ok"], 1)
                    pool.wait_ge(S["dtu_ok"], MD * t + m + 1)
                    if not (isinstance(t, int) and t == 0):
                        pool.wait_ge(S["yv_ok"], MD * (t - 1) + m + 1)
                    pool.tensor_tensor(tp[:, m, :], wk[:, m, :], bb[d][:, 0, :], ALU.mult).then_inc(S["tp_ok"], 1)

            def gate(t, d):
                for m in range(MD):
                    pool.wait_ge(S["yv_ok"], MD * t + m + 1)
                    if not (isinstance(t, int) and t == 0):
                        pool.wait_ge(S["o_ps"], KD * t)
                    pool.tensor_tensor(yz[:, m, :], tp[:, m, :], zs[d][:, m, :], ALU.mult).then_inc(S["yz_ok"], 1)

            def row_scale(t):
                pool.wait_ge(S["ss_ps"], t + 1)
                pool.wait_ge(S["rv_ok"], t + 1)
                if not (isinstance(t, int) and t == 0):
                    pool.wait_ge(S["fin_ok"], TT * t)
                pool.tensor_tensor(r2[:], r2[:], neg_half[:], ALU.pow).then_inc(S["rr_ok"], 1)

            gather(0)
            ln_scale(0)
            keep_residual(0)
            gather(1)
            scan_inputs(0, 0)

            def slots(s, first):
                for d in range(DIRS):
                    t = 2 * s + d
                    if d == 0:
                        ln_scale(s + 1)
                    if not first:
                        row_scale(t - 2)
                    gate(t, d)
                    if d == 1:
                        keep_residual(s + 1)
                        gather(s + 2)
                    scan_inputs(t + 1, 1 - d)

            slots(0, True)
            with pool.Fori(1, NSEQ) as s:
                slots(s, False)
            row_scale(2 * NSEQ - 2)
            row_scale(2 * NSEQ - 1)
            pool.wait_ge(S["gath"], 16 * TT * (NSEQ + 2))

        @block.scalar
        def _(act):
            act.wait_ge(S["ld_w"], 16 * (12 * DIRS + 1))
            for d in range(DIRS):
                act.activation(wdta[d][2 * NS:NX, :], wdt[d][2 * NS:NX, :], ACT.Abs).then_inc(S["prep_a"], 1)
            act.wait_ge(S["prep_v"], 2 * DIRS)
            for d in range(DIRS):
                act.activation(amat[d][:], amat[d][:], ACT.Exp).then_inc(S["prep_a"], 1)
            act.wait_ge(S["prep_a"], 2 * DIRS)
            for d in range(DIRS):
                act.activation(amat[d][:], amat[d][:], ACT.Copy, scale=-1.0).then_inc(S["prep_a"], 1)
            act.wait_ge(S["prep_a"], 3 * DIRS)

            def xt_copy(s):
                for k in range(KD):
                    act.wait_ge(S["xt_ps"], KD * s + k + 1)
                    act.activation(xt[0][:, k, :], pj[k][:], ACT.Copy).then_inc(S["xt_ok"], 1)

            def u_copy(t, d, m):
                tap = TAPS - 1
                act.wait_ge(S["u_ps"], MD * t + m + 1)
                if not (isinstance(t, int) and t == 0):
                    act.wait_ge(S["cv"], PAD * MD * (t - 1) + last_tap(m))
                act.activation(u[:, m, PAD:PAD + SEQ], pj[m % 2][:], ACT.Copy).then_inc(S["u_ok"], 1)
                if not (isinstance(t, int) and t < 2):
                    act.wait_ge(S["q2_ok"], MD * (t - 2) + m + 1)
                    act.wait_ge(S["dtu_ok"], MD * (t - 2) + m + 1)
                act.activation(uc[d][:, m, :], pj[m % 2][:], ACT.Identity, bias=convb[d][:, m:m + 1],
                               scale=convw[d][:, m, tap:tap + 1]).then_inc(S["a_ok"], 1)

            def z_silu(t, d, tiles):
                for m in tiles:
                    act.wait_ge(S["z_ps"], MD * t + m + 1)
                    if not (isinstance(t, int) and t < 2):
                        act.wait_ge(S["yz_ok"], MD * (t - 2) + m + 1)
                    act.activation(zs[d][:, m, :], pj[m % 2][:], ACT.Silu).then_inc(S["z_ok"], 1)

            def uc_silu(t, d):
                for m in range(MD):
                    act.wait_ge(S["cv"], PAD * MD * t + last_tap(m))
                    act.activation(uc[d][:, m, :], uc[d][:, m, :], ACT.Silu).then_inc(S["uc_ok"], 1)

            def xd_copy(t, d):
                act.wait_ge(S["xd_ps"], t + 1)
                if not (isinstance(t, int) and t < 2):
                    act.wait_ge(S["xd_st"], 16 * (t - 1))
                act.activation(xd[d][0:NX, :], px[0:NX, :], ACT.Copy).then_inc(S["xd_ok"], 1)

            def v_copy(t, d):
                for m in range(MD):
                    act.wait_ge(S["dt_ps"], MD * t + m + 1)
                    if not (isinstance(t, int) and t == 0):
                        act.wait_ge(S["q_ok"], MD * (t - 1) + m + 1)
                        act.wait_ge(S["dtu_ok"], MD * (t - 1) + m + 1)
                        act.wait_ge(S["da_ok"], MD * (t - 1) + m + 1)
                    act.activation(v[:, m, :], pj[m % 2][:], ACT.Identity, bias=bdt[d][:, m:m + 1]
                                   ).then_inc(S["v_ok"], 1)
                    if not (isinstance(t, int) and t == 0):
                        act.wait_ge(S["g_ok"], MD * (t - 1) + m + 1)
                    act.activation(lg[:, m, :], pj[m % 2][:], ACT.Abs, bias=bdt[d][:, m:m + 1]
                                   ).then_inc(S["vc_ok"], 1)

            def softplus_exp(t):
                for m in range(MD):
                    act.wait_ge(S["vc_ok"], MD * t + m + 1)
                    if not (isinstance(t, int) and t == 0):
                        act.wait_ge(S["h_ok"], MD * (t - 1) + m + 1)
                    act.activation(y[:, m, :], lg[:, m, :], ACT.Exp, scale=-1.0).then_inc(S["y_ok"], 1)

            def softplus_log(t, m):
                act.wait_ge(S["y_ok"], MD * t + m + 1)
                act.activation(lg[:, m, :], y[:, m, :], ACT.Ln, bias=1.0).then_inc(S["l_ok"], 1)

            def decays(t, d):
                for m in range(MD):
                    act.wait_ge(S["dt_ok"], MD * t + m + 1)
                    act.activation(y[:, m, :], v[:, m, :], ACT.Exp, scale=amat[d][:, m, 0:1]).then_inc(S["da_ok"], 1)

            def project_copies(t):
                for k in range(KD):
                    act.wait_ge(S["o_ps"], KD * t + k + 1)
                    if not (isinstance(t, int) and t == 0):
                        act.wait_ge(S["f_ps"], 2 * t)
                    act.activation(sq[:, k, :], po[k][:], ACT.Square).then_inc(S["sq_ok"], 1)
                    act.activation(fo[:, k, :], po[k][:], ACT.Copy).then_inc(S["fo_ok"], 1)

            def more_states(t, d):
                wait_apart(act, S["fl_ok"], 4 * t + 3)
                go = act.value_load(live[0:1, d:d + 1], min_val=0, max_val=1)
                with act.If(go > 0):
                    with act.Fori(1, NS) as n:
                        c = act.snap(act_count)
                        for m in range(MD):
                            act.wait_ge(S["e_h"], c * MD + m + 1)
                            act.wait_ge(S["h_ok"], MD * t + m + 1)
                            act.activation(y[:, m, :], v[:, m, :], ACT.Exp, scale=amat[d][:, m, bass.ds(n, 1)]
                                           ).then_inc(S["e_da"], 1)
                        act.reg_add(act_count, act_count, 1)
                    wait_apart(act, S["e_y"], act.snap(act_count) * MD + 1)
                with act.Else():
                    act.nop()

            act_count = act.alloc_register("act_states")
            act.reg_mov(act_count, 0)

            def front_rest(t, d, back):
                softplus_exp(t)
                for m in range(MD):
                    softplus_log(t, m)
                if back:
                    project_copies(t - 2)
                for m in range(MD):
                    u_copy(t + 1, 1 - d, m)
                decays(t, d)
                act.preload_act_table_set("silu_and_others")
                z_silu(t + 1, 1 - d, range(2))

            act.wait_ge(S["c_tab"], 4)
            xt_copy(0)
            for m in range(MD):
                u_copy(0, 0, m)
            z_silu(0, 0, range(MD))
            uc_silu(0, 0)
            xd_copy(0, 0)
            act.preload_act_table_set("natural_log_exp_and_others")
            v_copy(0, 0)
            front_rest(0, 0, False)

            def slots(s, first):
                for d in range(DIRS):
                    t = 2 * s + d
                    uc_silu(t + 1, 1 - d)
                    z_silu(t + 1, 1 - d, range(2, MD))
                    act.preload_act_table_set("natural_log_exp_and_others")
                    xd_copy(t + 1, 1 - d)
                    more_states(t, d)
                    v_copy(t + 1, 1 - d)
                    if d == 0:
                        xt_copy(s + 1)
                    front_rest(t + 1, 1 - d, not (first and d == 0))

            slots(0, True)
            with act.Fori(1, NSEQ) as s:
                slots(s, False)
            project_copies(2 * NSEQ - 1)

        @block.tensor
        def _(pe):
            mm = nc.tensor.matmul
            pe.wait_ge(S["c_tab"], 6)
            pe.wait_ge(S["ld_w"], 16 * (12 * DIRS + 1))
            pe.wait_ge(S["prep_w"], 1)
            for d in range(DIRS):
                for k in range(KD):
                    mm(po[0][:, 0:DM], fo[:, 0, (d * KD + k) * P:(d * KD + k + 1) * P], wfus[d][:, k, :],
                       start=(d == 0 and k == 0), stop=False)
            mm(po[0][:, 0:DM], ones[0:1, :], bfus[:], start=False, stop=True).then_inc(S["ct_ok"], 1)
            pe.wait_ge(S["prep_w"], 2)

            def turn_x(s):
                pe.wait_ge(S["xn_ok"], TT * (s + 1))
                for k in range(KD):
                    if not (isinstance(s, int) and s == 0):
                        pe.wait_ge(S["vc_ok"], MD * (2 * s - 1) + 2 + k + 1)
                    for j in range(TT):
                        i = nc.tensor.transpose(pj[k][:, j * P:(j + 1) * P], xn[:, j, k * P:(k + 1) * P], ident[:])
                    i.then_inc(S["xt_ps"], 1)

            def in_proj(t, d, half, tiles):
                ps = ("u_ps", "z_ps")[half]
                for m in tiles:
                    if half == 1 or m >= 2:
                        prev = "a_ok" if half == 0 or m < 2 else "z_ok"
                        pe.wait_ge(S[prev], MD * t + (m - 2) % MD + 1)
                    c = half * DI + m * P
                    for k in range(KD):
                        for n, (wp, xp) in enumerate(PARTS):
                            i = mm(pj[m % 2][:], win[d][wp][:, k, c:c + P], xt[xp][:, k, :],
                                   start=(k == 0 and n == 0), stop=(k == KD - 1 and n == 2))
                    i.then_inc(S[ps], 1)

            def x_dbl(t, d):
                if not (isinstance(t, int) and t == 0):
                    pe.wait_ge(S["fl_ok"], 4 * t)
                for m in range(MD):
                    pe.wait_ge(S["uc_ok"], MD * t + m + 1)
                    i = mm(px[0:NX, :], wx[d][:, m, :], uc[d][:, m, :], start=(m == 0), stop=(m == MD - 1))
                i.then_inc(S["xd_ps"], 1)

            def dt_proj(t, d, tiles):
                pe.wait_ge(S["xd_ok"], t + 1)
                for m in tiles:
                    if m < 2:
                        pe.wait_ge(S["z_ok"], MD * t + m + 3)
                    else:
                        pe.wait_ge(S["vc_ok"], MD * t + m - 1)
                    mm(pj[m % 2][:], wdt[d][2 * NS:NX, m * P:(m + 1) * P], xd_rows(d), start=True, stop=True
                       ).then_inc(S["dt_ps"], 1)

            def dead_sums(t, d):
                pe.wait_ge(S["xm_ok"], t + 1)
                for m in range(MD):
                    i = mm(px[:, m:m + 1], wdta[d][2 * NS:NX, m * P:(m + 1) * P], xmax[2 * NS:NX, :],
                           start=True, stop=True)
                i.then_inc(S["qd_ps"], 1)

            def dead_count(t):
                pe.wait_ge(S["gt_ok"], 2 * t + 2)
                mm(px[:, 8:8 + MD], ones[:], dgt[:], start=True, stop=True).then_inc(S["cnt_ps"], 1)

            def state_sum(t, d):
                pe.wait_ge(S["fl_ok"], 4 * t + 4)
                pe.wait_ge(S["bc_ok"], t + 1)
                if not (isinstance(t, int) and t < 2):
                    pe.wait_ge(S["q_ok"], MD * (t - 1))
                mm(pss[d][:], smask[:], bcp[:], start=True, stop=True).then_inc(S["s_ps"], 1)

            def out_proj(t, d, k):
                if not (isinstance(t, int) and t == 0):
                    pe.wait_ge(S["fin_ok"], TT * t)
                for m in range(MD):
                    pe.wait_ge(S["yz_ok"], MD * t + m + 1)
                    i = mm(po[k][:], wout[d][:, m, k * P:(k + 1) * P], yz[:, m, :], start=(m == 0), stop=(m == MD - 1))
                i.then_inc(S["o_ps"], 1)

            def fusion(t, d):
                pe.wait_ge(S["sq_ok"], KD * (t + 1))
                pe.wait_ge(S["fo_ok"], KD * (t + 1))
                for j in range(TT):
                    for k in range(KD):
                        i = mm(po[1][:, j:j + 1], sq[:, k, j * P:(j + 1) * P], ones[:, 0:1],
                               start=(k == 0), stop=(k == KD - 1))
                i.then_inc(S["ss_ps"], 1)
                for h in range(2):
                    bank = po[2] if h == 0 else po[0]
                    for jj in range(2):
                        j = 2 * h + jj
                        for k in range(KD):
                            i = mm(bank[:, jj * DM:(jj + 1) * DM], fo[:, k, j * P:(j + 1) * P], wfus[d][:, k, :],
                                   start=(k == 0), stop=(k == KD - 1))
                    i.then_inc(S["f_ps"], 1)

            def front(t, d, s_next, turn, back):
                x_dbl(t, d)
                dt_proj(t, d, range(MD))
                if turn:
                    turn_x(s_next)
                if back:
                    out_proj(t - 2, d, 0)
                dead_sums(t, d)
                if back:
                    out_proj(t - 2, d, 1)
                dead_count(t)
                pe.wait_ge(S["xl_ok"], KD * (s_next + 1))
                pe.wait_ge(S["vc_ok"], MD * (t + 1))
                in_proj(t + 1, 1 - d, 0, range(MD))
                if back:
                    fusion(t - 2, d)
                state_sum(t, d)
                in_proj(t + 1, 1 - d, 1, range(MD))

            turn_x(0)
            pe.wait_ge(S["xl_ok"], KD)
            for half in range(2):
                in_proj(0, 0, half, range(MD))
            front(0, 0, 0, False, False)

            def slots(s, first):
                for d in range(DIRS):
                    t = 2 * s + d
                    front(t + 1, 1 - d, s + 1, d == 0, not (first and d == 0))

            slots(0, True)
            with pe.Fori(1, NSEQ) as s:
                slots(s, False)
            for k in range(KD):
                out_proj(2 * NSEQ - 1, 1, k)
            fusion(2 * NSEQ - 1, 1)

        @block.vector
        def _(dve):
            tt, ts, stt = nc.vector.tensor_tensor, nc.vector.tensor_scalar, nc.vector.scalar_tensor_tensor
            dve.wait_ge(S["ld_w"], 16 * (12 * DIRS + 1))
            dve.wait_ge(S["c_tab"], 7)
            for d in range(DIRS):
                for k in range(KD):
                    c = d * KD + k
                    i = ts(fo[:, 0, c * P:(c + 1) * P], ones[:], lnb[d][:, k:k + 1], None, ALU.mult)
            i.then_inc(S["prep_w"], 1)
            for d in range(DIRS):
                nc.vector.tensor_reduce(almin[d][:], amat[d][:, :, 1:NS], AX_X, ALU.min).then_inc(S["prep_v"], 1)
                dve.wait_ge(S["prep_v"], 2 * d + 1)
                ts(amat[d][:], amat[d][:], ALOG_TOP, None, ALU.min).then_inc(S["prep_v"], 1)
            for d in range(DIRS):
                nc.vector.tensor_reduce(wmean[:, d, :], wout[d][:], AX_X, ALU.add).then_inc(S["prep_v"], 1)
            dve.wait_ge(S["prep_v"], 3 * DIRS)
            ts(wmean[:], wmean[:], 1.0 / DM, None, ALU.mult).then_inc(S["prep_v"], 1)
            dve.wait_ge(S["prep_v"], 3 * DIRS + 1)
            dve.wait_ge(S["ct_ok"], 1)
            nc.vector.tensor_copy(cvec[:], po[0][:, 0:DM]).then_inc(S["prep_v"], 1)
            for d in range(DIRS):
                stage = (v, lg)[d][:].rearrange("p m n -> p (m n)").rearrange("p (k e) -> p k e", k=KD)
                nc.vector.tensor_copy(win[d][0][:], stage).then_inc(S["prep_v"], 1)
                dve.wait_ge(S["prep_v"], 3 * DIRS + 3 + d)
                tt(win[d][1][:], stage, win[d][0][:].bitcast(F32), ALU.subtract)
                for m in range(MD):
                    ts(wout[d][:, m, :], wout[d][:, m, :], wmean[:, d, m:m + 1], None, ALU.subtract)
                for k in range(KD):
                    ts(wfus[d][:, k, :], wfus[d][:, k, :], lng[d][:, k:k + 1], None, ALU.mult)
                tt(alb[d][:], almin[d][:], bdt[d][:], ALU.add)
                i = ts(alok[d][:], almin[d][:], DEAD_LOG, None, ALU.is_gt)
            i.then_inc(S["prep_w"], 1)

            def ln_stats(s):
                dve.wait_ge(S["gath"], 16 * TT * (s + 1))
                if not (isinstance(s, int) and s == 0):
                    dve.wait_ge(S["xn_ok"], TT * s)
                for j in range(TT):
                    i = nc.vector.bn_stats(stats[:, j, :], g[:, j, :])
                i.then_inc(S["gt2"], 1)
                wait_apart(dve, S["gt2"], s + 1)
                for j in range(TT):
                    i = nc.vector.bn_aggr(mv[:, j, :], stats[:, j, :])
                i.then_inc(S["st_ok"], 1)

            def ln_apply(s):
                dve.wait_ge(S["lnr_ok"], s + 1)
                if not (isinstance(s, int) and s == 0):
                    dve.wait_ge(S["xt_ps"], KD * s)
                for j in range(TT):
                    ts(xn[:, j, :], g[:, j, :], mv[:, j, 0:1], rstd[:, j:j + 1], ALU.subtract, ALU.mult
                       ).then_inc(S["xn_ok"], 1)

            def xt_low(s):
                for k in range(KD):
                    dve.wait_ge(S["xt_ok"], KD * s + k + 1)
                    tt(xt[1][:, k, :], pj[k][:], xt[0][:, k, :].bitcast(F32), ALU.subtract).then_inc(S["xl_ok"], 1)

            def conv(t, d):
                for pair, n in ((0, 0), (0, 1), (0, 2), (1, 0), (1, 1), (1, 2)):
                    tap = TAPS - 2 - n
                    shift = -(n + 1) if d == 0 else n + 1
                    for m in (2 * pair, 2 * pair + 1):
                        if n == 0:
                            dve.wait_ge(S["u_ok"], MD * t + m + 1)
                            dve.wait_ge(S["a_ok"], MD * t + m + 1)
                        else:
                            dve.wait_ge(S["cv"], PAD * MD * t + 6 * pair + 2 * (n - 1) + m % 2 + 1)
                        stt(uc[d][:, m, :], u[:, m, PAD + shift:PAD + shift + SEQ], convw[d][:, m, tap:tap + 1],
                            uc[d][:, m, :], ALU.mult, ALU.add).then_inc(S["cv"], 1)

            def bc_product(t, d):
                dve.wait_ge(S["xd_ok"], t + 1)
                if not (isinstance(t, int) and t == 0):
                    dve.wait_ge(S["s_ps"], t)
                    dve.wait_ge(S["qd_ps"], t)
                tt(bcp[:], px[NS:2 * NS, :], xd[d][0:NS, :], ALU.mult).then_inc(S["bc_ok"], 1)
                nc.vector.tensor_reduce(xmax[2 * NS:NX, :], xd_rows(d), AX_X, ALU.max,
                                        apply_absolute_value=True).then_inc(S["xm_ok"], 1)

            def dead_test(t, d):
                dve.wait_ge(S["qd_ps"], t + 1)
                if not (isinstance(t, int) and t == 0):
                    dve.wait_ge(S["cnt_ps"], t)
                tt(dgt[:], alb[d][:], px[:, 0:MD], ALU.subtract).then_inc(S["gt_ok"], 1)
                dve.wait_ge(S["gt_ok"], 2 * t + 1)
                stt(dgt[:], dgt[:], DEAD_LOG, alok[d][:], ALU.is_gt, ALU.mult).then_inc(S["gt_ok"], 1)

            def dead_mask(t, d):
                dve.wait_ge(S["cnt_ps"], t + 1)
                nc.vector.tensor_reduce(dct[:], px[:, 8:8 + MD], AX_X, ALU.add).then_inc(S["fl_ok"], 1)
                dve.wait_ge(S["fl_ok"], 4 * t + 1)
                ts(dall[:], dct[:], DI - 0.5, None, ALU.is_gt).then_inc(S["fl_ok"], 1)
                ts(live[0:1, d:d + 1], dct[0:1, :], DI - 0.5, None, ALU.is_le).then_inc(S["fl_ok"], 1)
                dve.wait_ge(S["fl_ok"], 4 * t + 2)
                ts(smask[:], smask0[:], dall[0:NS, :], None, ALU.mult).then_inc(S["fl_ok"], 1)

            def softplus(t, tiles):
                for m in tiles:
                    dve.wait_ge(S["y_ok"], MD * t + m + 1)
                    ts(wk[:, m, :], y[:, m, :], 1.0, None, ALU.add).then_inc(S["w_ok"], 1)
                for m in tiles:
                    dve.wait_ge(S["w_ok"], MD * t + m + 1)
                    dve.wait_ge(S["l_ok"], MD * t + m + 1)
                    stt(wk[:, m, :], wk[:, m, :], 1.0, lg[:, m, :], ALU.subtract, ALU.subtract).then_inc(S["g_ok"], 1)
                for m in tiles:
                    dve.wait_ge(S["g_ok"], MD * t + m + 1)
                    tt(wk[:, m, :], y[:, m, :], wk[:, m, :], ALU.subtract).then_inc(S["d0_ok"], 1)
                for m in tiles:
                    dve.wait_ge(S["d0_ok"], MD * t + m + 1)
                    stt(v[:, m, :], v[:, m, :], 0.0, wk[:, m, :], ALU.max, ALU.add).then_inc(S["dt_ok"], 1)

            def scan(t, d):
                step = slice(None) if d == 0 else slice(None, None, -1)
                for m in range(MD):
                    dve.wait_ge(S["da_ok"], MD * t + m + 1)
                    dve.wait_ge(S["tp_ok"], MD * t + m + 1)
                    nc.vector.tensor_tensor_scan(tp[:, m, step], y[:, m, step], tp[:, m, step], 0.0, ALU.mult, ALU.add
                                                 ).then_inc(S["h_ok"], 1)

            def dead_part(t, d):
                dve.wait_ge(S["s_ps"], t + 1)
                for m in range(MD):
                    tt(qq[:, m, :], v[:, m, :], pss[d][:], ALU.mult).then_inc(S["q_ok"], 1)
                for m in range(MD):
                    dve.wait_ge(S["q_ok"], MD * t + m + 1)
                    stt(qq[:, m, :], qq[:, m, :], dp[d][:, m:m + 1], uc[d][:, m, :], ALU.add, ALU.mult
                        ).then_inc(S["q2_ok"], 1)

            def outputs(t, d):
                for m in range(MD):
                    dve.wait_ge(S["h_ok"], MD * t + m + 1)
                    tt(tp[:, m, :], tp[:, m, :], bb[d][:, 1, :], ALU.mult).then_inc(S["hc_ok"], 1)

            def more_states(t, d):
                wait_apart(dve, S["fl_ok"], 4 * t + 3)
                go = dve.value_load(live[0:1, d:d + 1], min_val=0, max_val=1)
                step = slice(None) if d == 0 else slice(None, None, -1)
                with dve.If(go > 0):
                    with dve.Fori(1, NS) as n:
                        c = dve.snap(dve_count)
                        if not (isinstance(t, int) and t < 2):
                            dve.wait_ge(S["ss_ps"], t - 1)
                        dve.wait_ge(S["e_bc"], 32 * c + 32)
                        for m in range(MD):
                            at = MD * c + m + 1
                            dve.wait_ge(S["e_y"], at)
                            tt(eh, wk[:, m, :], bb[1 - d][:, 0, :], ALU.mult).then_inc(S["e_tp"], 1)
                            dve.wait_ge(S["e_tp"], at)
                            dve.wait_ge(S["e_da"], at)
                            nc.vector.tensor_tensor_scan(sq[:, 0, step], y[:, m, step], sq[:, 0, step], 0.0, ALU.mult, ALU.add
                                                         ).then_inc(S["e_h"], 1)
                            dve.wait_ge(S["e_h"], at + 1)
                            tt(eh, eh, bb[1 - d][:, 1, :], ALU.mult).then_inc(S["e_hc"], 1)
                            dve.wait_ge(S["e_hc"], at)
                            dve.wait_ge(S["q2_ok"], MD * (t + 1))
                            tt(qq[:, m, :], qq[:, m, :], eh, ALU.add).then_inc(S["e_y"], 1)
                        dve.reg_add(dve_count, dve_count, 1)
                    wait_apart(dve, S["e_y"], dve.snap(dve_count) * MD + 1)
                with dve.Else():
                    dve.nop()

            def sums(t):
                for m in range(MD):
                    dve.wait_ge(S["hc_ok"], MD * t + m + 1)
                    dve.wait_ge(S["q2_ok"], MD * t + m + 1)
                    tt(tp[:, m, :], tp[:, m, :], qq[:, m, :], ALU.add).then_inc(S["yv_ok"], 1)

            def row_var(t):
                dve.wait_ge(S["ss_ps"], t + 1)
                if not (isinstance(t, int) and t == 0):
                    dve.wait_ge(S["fin_ok"], TT * t)
                ts(r2[:], po[1][:, 0:TT], 1.0 / DM, EPS, ALU.mult, ALU.add).then_inc(S["rv_ok"], 1)

            def finish(t, d, s_of):
                dve.wait_ge(S["rr_ok"], t + 1)
                if d == 0:
                    dve.wait_ge(S["h0_ok"], s_of + 1)
                elif not (isinstance(s_of, int) and s_of == 0):
                    dve.wait_ge(S["h1_st"], 16 * s_of)
                if d == 1:
                    dve.wait_ge(S["fin_ok"], TT * t)
                for j in range(TT):
                    bank = po[2] if j < 2 else po[0]
                    dve.wait_ge(S["f_ps"], 2 * t + j // 2 + 1)
                    src = h0c[:, bass.ds(s_of % 2, 1), j, :].squeeze(1)
                    dst = src if d == 0 else h1o[:, j, :]
                    stt(dst, bank[:, (j % 2) * DM:(j % 2 + 1) * DM], r2[:, j:j + 1], src,
                        ALU.mult, ALU.add).then_inc(S["fin_ok"], 1)

            dve_count = dve.alloc_register("dve_states")
            dve.reg_mov(dve_count, 0)
            dve.nop().then_inc(S["e_h"], 1)
            dve.nop().then_inc(S["e_y"], 1)

            ln_stats(0)
            ln_apply(0)
            xt_low(0)
            conv(0, 0)
            bc_product(0, 0)
            softplus(0, range(2))
            dead_test(0, 0)
            softplus(0, range(2, MD))
            dead_mask(0, 0)

            def slots(s, first):
                for d in range(DIRS):
                    t = 2 * s + d
                    conv(t + 1, 1 - d)
                    if not first:
                        row_var(t - 2)
                    if d == 0:
                        ln_stats(s + 1)
                    dead_part(t, d)
                    if not first:
                        finish(t - 2, d, s - 1)
                    if d == 0:
                        ln_apply(s + 1)
                    scan(t, d)
                    bc_product(t + 1, 1 - d)
                    more_states(t, d)
                    outputs(t, d)
                    sums(t)
                    if d == 0:
                        xt_low(s + 1)
                    dead_test(t + 1, 1 - d)
                    softplus(t + 1, range(MD))
                    dead_mask(t + 1, 1 - d)

            slots(0, True)
            with dve.Fori(1, NSEQ) as s:
                slots(s, False)
            row_var(2 * NSEQ - 2)
            finish(2 * NSEQ - 2, 0, NSEQ - 1)
            row_var(2 * NSEQ - 1)
            finish(2 * NSEQ - 1, 1, NSEQ - 1)


NCH = 32
BB = 16
NG = 4
NQ = 4
HD = 16
S_A = 32
NE = 8
QK = NQ + NG
BANKS = (2, 3, 0, 1)
V_BANK = (3, 1)
TOP = 2
PAIR = 512
X_ROWS = NSEQ * SEQ + PAIR
PICKS = 12
ROUTES = 20
TABLES = 8 + NQ * (3 + NG) + 2 + 2 * NE
NT = NSEQ * SEQ // P
MASKED = -3.0e38


def attention_stage(nc, w, h1_dram, base_dram, xd_dram, arrived, lg_all):
    ctx = ExitStack()
    with ctx:
        def sb(name, shape, dt=F32):
            return ctx.enter_context(nc.sbuf_tensor(name, shape, dt))

        wq = sb("a_wq", [P, KD, NQ + 1, P])
        wv = sb("a_wv", [P, KD, NG * HD])
        wp = sb("a_wp", [NG * HD, NQ, DM])
        wr = sb("a_wr", [P, KD, NE])
        lnw = sb("a_lnw", [P, 2, KD])
        lnb = sb("a_lnb", [P, 2, KD])
        ident = sb("a_ident", [P, P])
        cmask = sb("a_cmask", [P, S_A])
        vmask = sb("a_vmask", [P, NG * HD])
        nh = sb("a_nh", [P, TT])

        h1 = sb("a_h1", [P, TT, DM])
        stats = sb("a_stats", [P, TT, 6])
        mv = sb("a_mv", [P, TT, 2])
        ve = sb("a_ve", [P, 2, TT])
        rs1 = sb("a_rs1", [P, 2, TT])
        mean = sb("a_mean", [P, (NCH + 2) * TT])
        r1 = sb("a_r1", [P, (NCH + 2) * TT])
        core = sb("a_core", [P, TT, DM])
        lt = sb("a_lt", [P, KD, SEQ])
        qt = sb("a_qt", [P, BB, NQ, S_A])
        kb = sb("a_kb", [P, BB, NG, S_A])
        vd = sb("a_vd", [P, TT, 4, NG * HD])
        spread = sb("a_spread", [P, P])
        bmask = sb("a_bmask", [P, 4])
        vb = sb("a_vb", [P, BB, NG * HD])
        ss = sb("a_ss", [P, BB, NG, S_A])
        mx = sb("a_mx", [P, BB, NG])
        sm = sb("a_sm", [P, BB, NG])
        rs = sb("a_rs", [P, BB, NG])
        pt = sb("a_pt", [P, BB, P])
        ao = sb("a_ao", [NG * HD, NQ, SEQ])
        hb = sb("a_hb", [P, TT, DM])
        fi = sb("a_fi", [P, TT, DM])
        hh = sb("a_hh", [P, TT, DM])
        bs = sb("a_bs", [P, TT, DM])
        st2 = sb("a_st2", [P, TT, 6])
        mv2 = sb("a_mv2", [P, TT, 2])
        ve2 = sb("a_ve2", [P, TT])
        rr2 = sb("a_rr2", [P, TT])
        x2 = sb("a_x2", [P, TT, DM])
        x2t = sb("a_x2t", [P, KD, SEQ])

        lgc = sb("a_lgc", [P, TT, NE])
        expert = sb("a_expert", [P, NE])
        seen = sb("a_seen", [P, NE])
        ones = sb("a_ones", [P, P], BF16)
        before = sb("a_before", [P, P], BF16)
        top = sb("a_top", [P, TOP, TT])
        pick = sb("a_pick", [P, TT])
        flag = sb("a_flag", [P, TT, NE])
        rest = sb("a_rest", [P, TT, NE])
        hot = [sb(f"a_hot{k}", [P, TT, NE]) for k in range(TOP)]
        both = sb("a_both", [P, TT, NE], BF16)
        row = sb("a_row", [P, TT, NE])
        hrow = [sb(f"a_hrow{k}", [P, TT, NE]) for k in range(TOP)]
        dest = sb("a_dest", [P, TOP, TT])
        idx = sb("a_idx", [P, TOP, TT], I32)
        xs = sb("a_xs", [P, TT, DM])

        A = [ctx.enter_context(nc.psum_tensor(f"a_pa{i}", [P, SEQ], F32)) for i in range(4)]
        B = [ctx.enter_context(nc.psum_tensor(f"a_pb{i}", [P, SEQ], F32)) for i in range(4)]

        names = """c0 ld_w ld_h ld_hb st1 rq1 core_ok t1_ps lt_ok qk_ps qk_ok vn_ps vd_ok v_ps v_ok s_ps s_ok mx_ok
          sub_ok ex_ok su_ok rc_ok p_ok pt_ps pt_ok av_ps ao_ok pr_ps fi_ok hh_ok bs_ok st2 ve2 rr2 x2_ok t2_ps x2t_ok
          lg_ps lg_ok st_b rt rk_ps xs_ok scat""".split()
        S = {n: ctx.enter_context(nc.semaphore("a_" + n)) for n in names}
        block = ctx.enter_context(nc.Block())

        def wait_apart(eng, *waits):
            waits = [(s, v if isinstance(v, int) else eng.to_reg(v)) for s, v in waits]
            eng.wait_ge(S["c0"], 1)
            for semaphore, value in waits:
                if not (isinstance(value, int) and value <= 0):
                    eng.wait_ge(semaphore, value)

        def after(eng, name, value):
            if not (isinstance(value, int) and value <= 0):
                eng.wait_ge(S[name], value)

        h1_v = h1_dram.rearrange("(s b) c -> b s c", s=NSEQ)

        @block.sync
        def _(sp):
            for dst, name in ((wq, "wq"), (wv, "wv"), (wr, "wr")):
                src = w[name].rearrange("(k p) j e -> p k j e", p=P) if name == "wq" else \
                    w[name].rearrange("(k p) e -> p k e", p=P)
                sp.dma_start(dst[:], src).then_inc(S["ld_w"], 16)
            sp.dma_start(wp[:], w["wp"]).then_inc(S["ld_w"], 16)
            sp.dma_start(lnw[:], w["lnw"]).then_inc(S["ld_w"], 16)
            sp.dma_start(lnb[:], w["lnb"]).then_inc(S["ld_w"], 16)

            def load(dst, c, name):
                b0 = c * BB if isinstance(c, int) else (c * BB) % SEQ
                for j in range(TT):
                    sp.dma_start(dst[:, j, :], h1_v[bass.ds(b0 + 4 * j, 4), :, :]).then_inc(S[name], 16)

            load(h1, 0, "ld_h")
            sp.wait_ge(S["core_ok"], TT)
            load(h1, 1, "ld_h")

            def results(c):
                sp.wait_ge(S["bs_ok"], c + 1)
                sp.dma_start(base_dram[:, bass.ds(c * TT, TT), :], bs[:]).then_inc(S["st_b"], 16)

            def slot(c):
                sp.wait_ge(S["core_ok"], TT * (c + 2))
                load(h1, c + 2, "ld_h")
                after(sp, "bs_ok", c)
                load(hb, c, "ld_hb")
                if not (isinstance(c, int) and c == 0):
                    results(c - 1)

            slot(0)
            slot(1)
            with sp.Fori(2, NCH) as c:
                slot(c)
            results(NCH - 1)
            sp.wait_ge(S["st_b"], 16 * NCH)
            sp.wait_ge(S["ld_h"], 16 * TT * (NCH + 2))

        @block.gpsimd
        def _(pool):
            pool.memset(nh[:], -0.5).then_inc(S["c0"], 1)
            pool.wait_ge(S["c0"], 1)
            done = 1
            for tile in (ident, cmask, vmask, bmask, spread, kb):
                pool.memset(tile[:], 0.0).then_inc(S["c0"], 1)
                done += 1
                pool.wait_ge(S["c0"], done)
            pool.affine_select(out=ident[:], in_=ident[:], compare_op=ALU.not_equal, fill=1.0, base=0,
                               pattern=[[-1, P]], channel_multiplier=1).then_inc(S["c0"], 1)
            pool.wait_ge(S["c0"], done + 1)
            done += 1
            for q in range(NQ):
                rows = slice(S_A * q, S_A * (q + 1))
                pool.affine_select(out=cmask[rows, :], in_=cmask[rows, :], compare_op=ALU.is_ge, fill=MASKED, base=0,
                                   pattern=[[-1, S_A]], channel_multiplier=1).then_inc(S["c0"], 1)
                pool.wait_ge(S["c0"], done + 1)
                pool.memset(vmask[rows, HD * q:HD * (q + 1)], 1.0).then_inc(S["c0"], 1)
                pool.wait_ge(S["c0"], done + 2)
                pool.memset(bmask[rows, q:q + 1], 1.0).then_inc(S["c0"], 1)
                pool.wait_ge(S["c0"], done + 3)
                for n in range(NG):
                    pool.tensor_copy(spread[rows, S_A * n:S_A * (n + 1)], ident[rows, rows]).then_inc(S["c0"], 1)
                    pool.wait_ge(S["c0"], done + 4 + n)
                done += 3 + NG
            pool.memset(ones[:], 1.0).then_inc(S["c0"], 1)
            pool.wait_ge(S["c0"], done + 1)
            pool.affine_select(out=before[:], in_=ones[:], compare_op=ALU.is_gt, fill=0.0, base=0,
                               pattern=[[1, P]], channel_multiplier=-1).then_inc(S["c0"], 1)
            pool.wait_ge(S["c0"], done + 2)
            done += 2
            for e in range(NE):
                pool.memset(expert[:, e:e + 1], float(e)).then_inc(S["c0"], 1)
                pool.wait_ge(S["c0"], done + 1)
                pool.memset(seen[:, e:e + 1], float(e * X_ROWS)).then_inc(S["c0"], 1)
                pool.wait_ge(S["c0"], done + 2)
                done += 2

            def scales1(c):
                wait_apart(pool, (S["st1"], 2 * c + 2), (S["core_ok"], TT * c))
                pool.tensor_scalar(ve[:, 0, :], mv[:, :, 1], 1.0, EPS, ALU.mult, ALU.add).then_inc(S["rq1"], 1)
                pool.tensor_scalar(ve[:, 1, :], mv[:, :, 1], 1.0 + EPS, EPS * EPS, ALU.mult, ALU.add
                                   ).then_inc(S["rq1"], 1)
                pool.wait_ge(S["rq1"], 3 * c + 2)
                pool.tensor_tensor(rs1[:], ve[:], nh[:].unsqueeze(1).to_broadcast([P, 2, TT]), ALU.pow
                                   ).then_inc(S["rq1"], 1)

            def scales2(c):
                wait_apart(pool, (S["st2"], 2 * c + 2), (S["x2_ok"], TT * c))
                pool.tensor_scalar(ve2[:], mv2[:, :, 1], 1.0, EPS, ALU.mult, ALU.add).then_inc(S["ve2"], 1)
                pool.wait_ge(S["ve2"], c + 1)
                pool.tensor_tensor(rr2[:], ve2[:], nh[:], ALU.pow).then_inc(S["rr2"], 1)

            def per_row(tile, i):
                return tile[:, 4 * i:4 * i + 4, :].unsqueeze(3).to_broadcast([P, 4, NG, S_A])

            def subtract_max(c):
                for n, i in enumerate(BANKS):
                    pool.wait_ge(S["mx_ok"], 4 * c + n + 1)
                    pool.tensor_tensor(ss[:, 4 * i:4 * i + 4], ss[:, 4 * i:4 * i + 4], per_row(mx, i),
                                       ALU.subtract).then_inc(S["sub_ok"], 1)

            def normalise(c):
                for n, i in enumerate(BANKS):
                    pool.wait_ge(S["rc_ok"], 4 * c + n + 1)
                    pool.tensor_tensor(ss[:, 4 * i:4 * i + 4], ss[:, 4 * i:4 * i + 4], per_row(rs, i),
                                       ALU.mult).then_inc(S["p_ok"], 1)

            def base(c):
                pool.wait_ge(S["hh_ok"], 2 * (c + 1))
                after(pool, "st_b", 16 * c)
                pool.tensor_tensor(bs[:], hh[:], hb[:], ALU.add).then_inc(S["bs_ok"], 1)

            def send(c):
                wait_apart(pool, (S["rt"], ROUTES * (c + 1) - 1), (S["xs_ok"], c + 1))
                for j in range(TT):
                    for k in range(TOP):
                        pool.indirect_dma_start(out=xd_dram, out_offset=bass.IndirectOffsetOnAxis(
                            ap=idx[:, k, j:j + 1].bitcast(U32), axis=0), in_=xs[:, j, :], in_offset=None
                            ).then_inc(S["scat"], 16)

            scales1(0)
            scales1(1)

            def slot(c):
                subtract_max(c)
                if not (isinstance(c, int) and c == 0):
                    base(c - 1)
                    scales2(c - 1)
                normalise(c)
                scales1(c + 2)
                if not (isinstance(c, int) and c < 2):
                    send(c - 2)

            slot(0)
            slot(1)
            with pool.Fori(2, NCH) as c:
                slot(c)
            base(NCH - 1)
            scales2(NCH - 1)
            send(NCH - 2)
            send(NCH - 1)
            pool.wait_ge(S["scat"], 16 * TT * TOP * NCH)

        @block.scalar
        def _(act):
            act.wait_ge(S["ld_w"], 16 * 6)

            def lt_copy(c):
                for k in range(KD):
                    act.wait_ge(S["t1_ps"], KD * c + k + 1)
                    act.activation(lt[:, k, :], B[k][:], ACT.Identity, bias=lnb[:, 0, k:k + 1],
                                   scale=lnw[:, 0, k:k + 1]).then_inc(S["lt_ok"], 1)

            def q_copy(c, q):
                act.wait_ge(S["qk_ps"], (NQ + 1) * c + q + 1)
                after(act, "s_ps", 4 * c)
                act.activation(qt[:, :, q, :], B[q % 2][:].rearrange("p (b s) -> p b s", b=BB), ACT.Copy
                               ).then_inc(S["qk_ok"], 1)

            def k_copy(c):
                act.wait_ge(S["qk_ps"], (NQ + 1) * (c + 1))
                for g in range(NG):
                    rows = slice(32 * g, 32 * (g + 1))
                    act.activation(kb[rows, :, g, :], B[0][rows, :].rearrange("p (b s) -> p b s", b=BB), ACT.Copy
                                   ).then_inc(S["qk_ok"], 1)

            def exp(c, n):
                i = BANKS[n]
                act.wait_ge(S["sub_ok"], 4 * c + n + 1)
                act.activation(ss[:, 4 * i:4 * i + 4], ss[:, 4 * i:4 * i + 4], ACT.Exp, scale=HD ** -0.5
                               ).then_inc(S["ex_ok"], 1)

            def pt_copy(c):
                for n, i in enumerate(BANKS):
                    act.wait_ge(S["pt_ps"], 4 * c + n + 1)
                    after(act, "av_ps", 4 * c)
                    act.activation(pt[:, 4 * i:4 * i + 4, :], A[i][:].rearrange("p (b n) -> p b n", b=4), ACT.Copy
                                   ).then_inc(S["pt_ok"], 1)

            def ao_copy(c):
                for n, i in enumerate(BANKS):
                    act.wait_ge(S["av_ps"], 4 * c + n + 1)
                    after(act, "pr_ps", 2 * c)
                    src = B[i][0:NG * HD, :].rearrange("p (b q s) -> p b q s", b=4, q=NQ)
                    dst = ao[:, :, i * P:(i + 1) * P].rearrange("p q (b s) -> p b q s", b=4)
                    act.activation(dst, src, ACT.Copy).then_inc(S["ao_ok"], 1)

            def x2t_copy(c):
                for k in range(KD):
                    act.wait_ge(S["t2_ps"], KD * c + k + 1)
                    after(act, "lg_ps", c)
                    act.activation(x2t[:, k, :], A[k][:], ACT.Identity, bias=lnb[:, 1, k:k + 1],
                                   scale=lnw[:, 1, k:k + 1]).then_inc(S["x2t_ok"], 1)

            def rows_copy(c):
                act.wait_ge(S["x2_ok"], TT * (c + 1))
                after(act, "scat", 16 * TT * TOP * c)
                act.activation(xs[:], x2[:], ACT.Copy).then_inc(S["xs_ok"], 1)

            act.wait_ge(S["c0"], TABLES)
            lt_copy(0)
            for q in range(NQ):
                q_copy(0, q)
            k_copy(0)
            act.wait_ge(S["vn_ps"], 1)
            lt_copy(1)

            def slot(c):
                exp(c, 0)
                exp(c, 1)
                q_copy(c + 1, 0)
                exp(c, 2)
                q_copy(c + 1, 1)
                exp(c, 3)
                q_copy(c + 1, 2)
                q_copy(c + 1, 3)
                k_copy(c + 1)
                if not (isinstance(c, int) and c == 0):
                    x2t_copy(c - 1)
                pt_copy(c)
                ao_copy(c)
                act.wait_ge(S["vn_ps"], c + 2)
                lt_copy(c + 2)
                if not (isinstance(c, int) and c == 0):
                    rows_copy(c - 1)

            slot(0)
            slot(1)
            with act.Fori(2, NCH) as c:
                slot(c)
            x2t_copy(NCH - 1)
            rows_copy(NCH - 1)

        @block.tensor
        def _(pe):
            mm = nc.tensor.matmul
            pe.wait_ge(S["ld_w"], 16 * 6)
            pe.wait_ge(S["c0"], TABLES)

            def turn1(c):
                pe.wait_ge(S["core_ok"], TT * (c + 1))
                for k in range(KD):
                    if k == 0:
                        after(pe, "ao_ok", 4 * (c - 1))
                        after(pe, "qk_ok", QK * c)
                    for j in range(TT):
                        i = nc.tensor.transpose(B[k][:, j * P:(j + 1) * P], core[:, j, k * P:(k + 1) * P], ident[:])
                    i.then_inc(S["t1_ps"], 1)

            def qk(c):
                pe.wait_ge(S["lt_ok"], KD * (c + 1))
                for q in range(NQ + 1):
                    if q >= 2:
                        pe.wait_ge(S["qk_ok"], QK * c + q - 1)
                    for k in range(KD):
                        i = mm(B[q % 2][:], wq[:, k, q, :], lt[:, k, :], start=(k == 0), stop=(k == KD - 1))
                    i.then_inc(S["qk_ps"], 1)

            def values(c):
                after(pe, "ao_ok", 4 * c)
                for j in range(TT):
                    for k in range(KD):
                        n = mm(B[2][:, j * 64:(j + 1) * 64], lt[:, k, j * P:(j + 1) * P], wv[:, k, :],
                               start=(k == 0), stop=(k == KD - 1))
                n.then_inc(S["vn_ps"], 1)

            def spread_values(c):
                after(pe, "ao_ok", 4 * c)
                pe.wait_ge(S["qk_ok"], QK * (c + 1) + NQ)
                for i in range(2):
                    pe.wait_ge(S["vd_ok"], TT * c + 2 * i + 2)
                    for jj in range(2):
                        n = mm(B[V_BANK[i]][:, jj * 256:(jj + 1) * 256], spread[:],
                               vd[:, 2 * i + jj, :, :].rearrange("p b n -> p (b n)"), start=True, stop=True)
                    n.then_inc(S["v_ps"], 1)

            def scores(c):
                pe.wait_ge(S["qk_ok"], QK * (c + 1))
                after(pe, "pt_ok", 4 * c)
                for n, i in enumerate(BANKS):
                    if n == 2:
                        after(pe, "hh_ok", 2 * c)
                    for b in range(4):
                        o = mm(A[i][:, b * P:(b + 1) * P], qt[:, 4 * i + b].rearrange("p q s -> p (q s)"),
                               kb[:, 4 * i + b].rearrange("p g t -> p (g t)"), start=True, stop=True)
                    o.then_inc(S["s_ps"], 1)

            def turn_p(c):
                for n, i in enumerate(BANKS):
                    pe.wait_ge(S["p_ok"], 4 * c + n + 1)
                    if n == 2:
                        after(pe, "x2t_ok", KD * c)
                    for b in range(4):
                        o = nc.tensor.transpose(A[i][:, b * P:(b + 1) * P],
                                                ss[:, 4 * i + b, :, :].rearrange("p g t -> p (g t)"), ident[:])
                    o.then_inc(S["pt_ps"], 1)

            def products(c):
                pe.wait_ge(S["qk_ok"], QK * (c + 2))
                pe.wait_ge(S["v_ok"], 2 * (c + 1))
                after(pe, "lg_ok", 2 * c)
                if not (isinstance(c, int) and c < 2):
                    pe.wait_ge(S["rt"], ROUTES * (c - 2) + PICKS + 2)
                for n, i in enumerate(BANKS):
                    pe.wait_ge(S["pt_ok"], 4 * c + n + 1)
                    for b in range(4):
                        o = mm(B[i][0:NG * HD, b * P:(b + 1) * P], vb[:, 4 * i + b, :], pt[:, 4 * i + b, :],
                               start=True, stop=True)
                    o.then_inc(S["av_ps"], 1)

            def project(c):
                pe.wait_ge(S["ao_ok"], 4 * (c + 1))
                for i in range(2):
                    for jj in range(2):
                        j = 2 * i + jj
                        for q in range(NQ):
                            n = mm(A[i][:, jj * DM:(jj + 1) * DM], ao[:, q, j * P:(j + 1) * P], wp[:, q, :],
                                   start=(q == 0), stop=(q == NQ - 1))
                    n.then_inc(S["pr_ps"], 1)

            def turn2(c, last=False):
                pe.wait_ge(S["x2_ok"], TT * (c + 1))
                if last:
                    pe.wait_ge(S["hh_ok"], 2 * (c + 1))
                else:
                    pe.wait_ge(S["s_ok"], 4 * (c + 2))
                for k in range(KD):
                    for j in range(TT):
                        i = nc.tensor.transpose(A[k][:, j * P:(j + 1) * P], x2[:, j, k * P:(k + 1) * P], ident[:])
                    i.then_inc(S["t2_ps"], 1)

            def router(c):
                pe.wait_ge(S["x2t_ok"], KD * (c + 1))
                pe.wait_ge(S["vd_ok"], TT * (c + 2))
                for j in range(TT):
                    for k in range(KD):
                        i = mm(B[2][:, j * NE:(j + 1) * NE], x2t[:, k, j * P:(j + 1) * P], wr[:, k, :],
                               start=(k == 0), stop=(k == KD - 1))
                i.then_inc(S["lg_ps"], 1)

            def ranks(c):
                pe.wait_ge(S["rt"], ROUTES * c + PICKS)
                if not isinstance(c, int):
                    pe.wait_ge(S["vd_ok"], TT * (c + 3))
                for j in range(TT + 1):
                    out = B[2][:, (TT + j) * NE:(TT + j + 1) * NE]
                    for i in range(j):
                        n = mm(out, ones[:], both[:, i, :], start=(i == 0), stop=(j == TT and i == TT - 1))
                    if j < TT:
                        n = mm(out, before[:], both[:, j, :], start=(j == 0), stop=True)
                n.then_inc(S["rk_ps"], 1)

            turn1(0)
            qk(0)
            values(0)
            turn1(1)

            def slot(c):
                scores(c)
                qk(c + 1)
                if not (isinstance(c, int) and c == 0):
                    turn2(c - 1)
                    spread_values(c)
                    if not (isinstance(c, int) and c < 2):
                        ranks(c - 2)
                    router(c - 1)
                else:
                    spread_values(c)
                turn_p(c)
                products(c)
                project(c)
                values(c + 1)
                turn1(c + 2)

            slot(0)
            slot(1)
            with pe.Fori(2, NCH) as c:
                slot(c)
            turn2(NCH - 1, True)
            ranks(NCH - 2)
            router(NCH - 1)
            pe.wait_ge(S["lg_ok"], 2 * NCH)
            pe.wait_ge(S["rt"], ROUTES * (NCH - 2) + PICKS + 2)
            ranks(NCH - 1)

        @block.vector
        def _(dve):
            tt, ts, stt = nc.vector.tensor_tensor, nc.vector.tensor_scalar, nc.vector.scalar_tensor_tensor

            def stats1(c):
                dve.wait_ge(S["ld_h"], 16 * TT * (c + 1))
                for j in range(TT):
                    i = nc.vector.bn_stats(stats[:, j, :], h1[:, j, :])
                i.then_inc(S["st1"], 1)
                wait_apart(dve, (S["st1"], 2 * c + 1))
                for j in range(TT):
                    i = nc.vector.bn_aggr(mv[:, j, :], stats[:, j, :])
                i.then_inc(S["st1"], 1)

            def normalise(c):
                dve.wait_ge(S["st1"], 2 * c + 2)
                cols = bass.ds(c * TT, TT)
                nc.vector.tensor_copy(mean[:, cols], mv[:, :, 0])
                dve.wait_ge(S["rq1"], 3 * c + 3)
                nc.vector.tensor_copy(r1[:, cols], rs1[:, 0, :])
                after(dve, "t1_ps", KD * c)
                for j in range(TT):
                    ts(core[:, j, :], h1[:, j, :], mv[:, j, 0:1], rs1[:, 1, j:j + 1], ALU.subtract, ALU.mult
                       ).then_inc(S["core_ok"], 1)

            def v_parts(c):
                dve.wait_ge(S["vn_ps"], c + 1)
                after(dve, "v_ps", 2 * c)
                for j in range(TT):
                    tt(vd[:, j, :, :], B[2][:, j * 64:(j + 1) * 64].unsqueeze(1).to_broadcast([P, 4, NG * HD]),
                       bmask[:].unsqueeze(2).to_broadcast([P, 4, NG * HD]), ALU.mult).then_inc(S["vd_ok"], 1)

            def v_copy(c):
                for i in range(2):
                    dve.wait_ge(S["v_ps"], 2 * c + i + 1)
                    after(dve, "av_ps", 4 * c)
                    tt(vb[:, 8 * i:8 * i + 8, :], B[V_BANK[i]][:].rearrange("p (b n) -> p b n", b=8),
                       vmask[:].unsqueeze(1).to_broadcast([P, 8, NG * HD]), ALU.mult).then_inc(S["v_ok"], 1)

            def maxima(c):
                for n, i in enumerate(BANKS):
                    part = ss[:, 4 * i:4 * i + 4]
                    dve.wait_ge(S["s_ps"], 4 * c + n + 1)
                    after(dve, "pt_ps", 4 * c)
                    tt(part, A[i][:].rearrange("p (b g t) -> p b g t", b=4, g=NG),
                       cmask[:].unsqueeze(1).unsqueeze(1).to_broadcast([P, 4, NG, S_A]), ALU.add
                       ).then_inc(S["s_ok"], 1)
                    dve.wait_ge(S["s_ok"], 4 * c + n + 1)
                    nc.vector.tensor_reduce(mx[:, 4 * i:4 * i + 4, :], part, AX_X, ALU.max).then_inc(S["mx_ok"], 1)

            def sums(c):
                for n, i in enumerate(BANKS):
                    dve.wait_ge(S["ex_ok"], 4 * c + n + 1)
                    nc.vector.tensor_reduce(sm[:, 4 * i:4 * i + 4, :], ss[:, 4 * i:4 * i + 4], AX_X, ALU.add
                                            ).then_inc(S["su_ok"], 1)
                    dve.wait_ge(S["su_ok"], 4 * c + n + 1)
                    nc.vector.reciprocal(rs[:, 4 * i:4 * i + 4, :], sm[:, 4 * i:4 * i + 4, :]).then_inc(S["rc_ok"], 1)

            def first_input(c):
                dve.wait_ge(S["ld_hb"], 16 * TT * (c + 1))
                cols = c * TT
                for j in range(TT):
                    ts(fi[:, j, :], hb[:, j, :], mean[:, bass.ds(cols + j, 1)], r1[:, bass.ds(cols + j, 1)],
                       ALU.subtract, ALU.mult).then_inc(S["fi_ok"], 1)

            def add_projection(c):
                for i in range(2):
                    dve.wait_ge(S["pr_ps"], 2 * c + i + 1)
                    dve.wait_ge(S["fi_ok"], TT * (c + 1))
                    after(dve, "bs_ok", c)
                    tt(hh[:, 2 * i:2 * i + 2, :], A[i][:].rearrange("p (j e) -> p j e", j=2),
                       fi[:, 2 * i:2 * i + 2, :], ALU.add).then_inc(S["hh_ok"], 1)

            def stats2(c):
                for j in range(TT):
                    dve.wait_ge(S["hh_ok"], 2 * c + j // 2 + 1)
                    i = nc.vector.bn_stats(st2[:, j, :], hh[:, j, :])
                i.then_inc(S["st2"], 1)
                wait_apart(dve, (S["st2"], 2 * c + 1))
                for j in range(TT):
                    i = nc.vector.bn_aggr(mv2[:, j, :], st2[:, j, :])
                i.then_inc(S["st2"], 1)

            def normalise2(c):
                dve.wait_ge(S["rr2"], c + 1)
                after(dve, "xs_ok", c)
                after(dve, "t2_ps", KD * c)
                for j in range(TT):
                    ts(x2[:, j, :], hh[:, j, :], mv2[:, j, 0:1], rr2[:, j:j + 1], ALU.subtract, ALU.mult
                       ).then_inc(S["x2_ok"], 1)

            def keep_logits(c):
                dve.wait_ge(S["lg_ps"], c + 1)
                nc.vector.tensor_copy(lg_all[:, bass.ds(c * TT, TT), :],
                                      B[2][:, 0:TT * NE].rearrange("p (j e) -> p j e", j=TT)).then_inc(S["lg_ok"], 1)
                if not (isinstance(c, int) and c == 0):
                    dve.wait_ge(S["rt"], ROUTES * (c - 1) + PICKS)
                nc.vector.tensor_copy(lgc[:], B[2][:, 0:TT * NE].rearrange("p (j e) -> p j e", j=TT)
                                      ).then_inc(S["lg_ok"], 1)

            def per_token(col):
                return col.unsqueeze(2).to_broadcast([P, TT, NE])

            def per_expert(tile):
                return tile[:].unsqueeze(1).to_broadcast([P, TT, NE])

            def pick_experts(c):
                dve.wait_ge(S["lg_ok"], 2 * (c + 1))
                n = 0
                for k in range(TOP):
                    src = (lgc, rest)[k]
                    nc.vector.tensor_reduce(top[:, k, :], src[:], AX_X, ALU.max).then_inc(S["rt"], 1)
                    dve.wait_ge(S["rt"], ROUTES * c + n + 1)
                    tt(flag[:], src[:], per_token(top[:, k, :]), ALU.is_lt).then_inc(S["rt"], 1)
                    dve.wait_ge(S["rt"], ROUTES * c + n + 2)
                    stt(flag[:], flag[:], float(NE), per_expert(expert), ALU.mult, ALU.add).then_inc(S["rt"], 1)
                    dve.wait_ge(S["rt"], ROUTES * c + n + 3)
                    nc.vector.tensor_reduce(pick[:], flag[:], AX_X, ALU.min).then_inc(S["rt"], 1)
                    dve.wait_ge(S["rt"], ROUTES * c + n + 4)
                    tt(hot[k][:], per_expert(expert), per_token(pick[:]), ALU.is_equal).then_inc(S["rt"], 1)
                    dve.wait_ge(S["rt"], ROUTES * c + n + 5)
                    if k == 0:
                        stt(rest[:], hot[0][:], MASKED, lgc[:], ALU.mult, ALU.add).then_inc(S["rt"], 1)
                        dve.wait_ge(S["rt"], ROUTES * c + n + 6)
                    n += 6
                tt(both[:], hot[0][:], hot[1][:], ALU.add).then_inc(S["rt"], 1)

            def next_rows(c):
                dve.wait_ge(S["rk_ps"], c + 1)
                tt(row[:], B[2][:, TT * NE:2 * TT * NE].rearrange("p (j e) -> p j e", j=TT), per_expert(seen), ALU.add
                   ).then_inc(S["rt"], 1)
                dve.wait_ge(S["rt"], ROUTES * c + PICKS + 1)
                tt(seen[:], seen[:], B[2][:, 2 * TT * NE:(2 * TT + 1) * NE], ALU.add).then_inc(S["rt"], 1)

            def place(c):
                at = ROUTES * c + PICKS
                for k in range(TOP):
                    tt(hrow[k][:], hot[k][:], row[:], ALU.mult).then_inc(S["rt"], 1)
                for k in range(TOP):
                    dve.wait_ge(S["rt"], at + 3 + k)
                    nc.vector.tensor_reduce(dest[:, k, :], hrow[k][:], AX_X, ALU.add).then_inc(S["rt"], 1)
                dve.wait_ge(S["rt"], at + 6)
                after(dve, "scat", 16 * TT * TOP * c)
                nc.vector.tensor_copy(idx[:], dest[:]).then_inc(S["rt"], 1)
                nc.vector.tensor_copy(arrived[:, :, bass.ds(c * TT, TT)], dest[:]).then_inc(S["rt"], 1)
                dve.wait_ge(S["rt"], at + 8)

            dve.wait_ge(S["c0"], TABLES)
            stats1(0)
            normalise(0)
            v_parts(0)
            stats1(1)
            normalise(1)

            def slot(c):
                first = isinstance(c, int) and c == 0
                if not first:
                    add_projection(c - 1)
                maxima(c)
                if not first:
                    stats2(c - 1)
                sums(c)
                if not first:
                    normalise2(c - 1)
                stats1(c + 2)
                v_copy(c)
                normalise(c + 2)
                if not first:
                    keep_logits(c - 1)
                    if not (isinstance(c, int) and c < 2):
                        next_rows(c - 2)
                first_input(c)
                if not (isinstance(c, int) and c < 2):
                    place(c - 2)
                if not first:
                    pick_experts(c - 1)
                v_parts(c + 1)

            slot(0)
            slot(1)
            with dve.Fori(2, NCH) as c:
                slot(c)
            add_projection(NCH - 1)
            stats2(NCH - 1)
            normalise2(NCH - 1)
            keep_logits(NCH - 1)
            next_rows(NCH - 2)
            place(NCH - 2)
            pick_experts(NCH - 1)
            next_rows(NCH - 1)
            place(NCH - 1)


NTILE = NSEQ * SEQ // P
FF = 512
MF = FF // P
CAP = -(-NSEQ * SEQ * TOP * 5 // (NE * 4))
HALF = 256
HT = HALF // P
MAX_PAIRS = NSEQ * SEQ // PAIR
MAX_TURNS = NSEQ * SEQ * TOP // PAIR + NE
NOWHERE = float(1 << 20)
GT = 4
NGT = NTILE // GT


def routing_stage(nc, lg_all, arrived, src_row, prob, plan):
    ctx = ExitStack()
    with ctx:
        def sb(name, shape, dt=F32):
            return ctx.enter_context(nc.sbuf_tensor(name, shape, dt))

        block_shape = [P, NTILE, NE]
        ident = sb("r_ident", [P, P])
        same = sb("r_same", [P, P])
        later = sb("r_later", [P, P])
        below = sb("r_below", [P, P])
        ones = sb("r_ones", [P, P])
        expert = sb("r_expert", [P, NE])
        row0 = sb("r_row0", [P, NE])
        steps = sb("r_steps", [P, MAX_PAIRS - 1])
        sums = sb("r_sums", [P, NE])
        shift = sb("r_shift", [P, NE])
        m = sb("r_m", [P, TOP, NTILE])
        pick = sb("r_pick", [P, NTILE])
        flag = sb("r_flag", block_shape)
        rest = sb("r_rest", block_shape)
        hot = [sb(f"r_hot{k}", block_shape) for k in range(TOP)]
        both = sb("r_both", block_shape)
        rank = sb("r_rank", block_shape)
        total = sb("r_total", [P, NE])
        dst = sb("r_dst", [P, TOP, NTILE])
        keep = sb("r_keep", [P, TOP, NTILE])
        kdst = sb("r_kdst", [P, TOP, NTILE])
        ex = sb("r_ex", [P, NTILE])
        over = sb("r_over", [P, NE, MAX_PAIRS - 1])
        turns = sb("r_turns", [P, NE])
        planf = sb("r_planf", [1, 3, NE])
        ps_same = [ctx.enter_context(nc.psum_tensor(f"r_ps{i}", [P, SEQ], F32)) for i in range(2)]
        ps_part = [ctx.enter_context(nc.psum_tensor(f"r_pp{i}", [P, SEQ], F32)) for i in range(2)]
        ps_base = ctx.enter_context(nc.psum_tensor("r_pb", [P, 2, NE], F32))
        S = {n: ctx.enter_context(nc.semaphore("r_" + n)) for n in "tab rows seq both_ok tot_ok counted ex_ok".split()}
        block = ctx.enter_context(nc.Block())

        @block.gpsimd
        def _(pool):
            n = 0
            for tile, value in ((ident, 0.0), (same, 0.0), (later, 0.0), (below, 0.0), (ones, 1.0)):
                pool.memset(tile[:], value).then_inc(S["tab"], 1)
                n += 1
                pool.wait_ge(S["tab"], n)
            pool.affine_select(out=ident[:], in_=ident[:], compare_op=ALU.not_equal, fill=1.0, base=0,
                               pattern=[[-1, P]], channel_multiplier=1).then_inc(S["tab"], 1)
            n += 1
            pool.wait_ge(S["tab"], n)
            for q in range(4):
                rows = slice(S_A * q, S_A * (q + 1))
                for g in range(4):
                    cols = slice(S_A * g, S_A * (g + 1))
                    pool.tensor_copy(same[rows, cols], ident[rows, rows]).then_inc(S["tab"], 1)
                    n += 1
                    pool.wait_ge(S["tab"], n)
                    if q >= g:
                        pool.tensor_scalar(later[rows, cols], ident[rows, rows], -1.0, None, ALU.mult
                                           ).then_inc(S["tab"], 1)
                        n += 1
                        pool.wait_ge(S["tab"], n)
                    pool.affine_select(out=below[rows, cols], in_=ones[rows, cols], compare_op=ALU.is_gt, fill=0.0,
                                       base=0, pattern=[[1, S_A]], channel_multiplier=-1).then_inc(S["tab"], 1)
                    n += 1
                    pool.wait_ge(S["tab"], n)
            assert n == TABLES_R

        @block.scalar
        def _(act):
            act.wait_ge(S["seq"], 11)
            act.activation(ex[:], ex[:], ACT.Exp).then_inc(S["ex_ok"], 1)

        @block.tensor
        def _(pe):
            pe.wait_ge(S["tab"], TABLES_R)
            pe.wait_ge(S["both_ok"], 1)
            flat = both[:].rearrange("p t e -> p (t e)")
            for i in range(2):
                cols = slice(SEQ * i, SEQ * (i + 1))
                nc.tensor.matmul(ps_same[i][:], same[:], flat[:, cols], start=True, stop=True)
                nc.tensor.matmul(ps_part[i][:], later[:], flat[:, cols], start=True, stop=True)
            pe.wait_ge(S["tot_ok"], 1)
            nc.tensor.matmul(ps_base[:, 0, :], below[:], total[:], start=True, stop=True)
            nc.tensor.matmul(ps_base[:, 1, :], ones[:], total[:], start=True, stop=True).then_inc(S["counted"], 1)

        @block.vector
        def _(dve):
            tt, ts, stt = nc.vector.tensor_tensor, nc.vector.tensor_scalar, nc.vector.scalar_tensor_tensor
            for e in range(NE):
                nc.vector.memset(expert[:, e:e + 1], float(e)).then_inc(S["rows"], 1)
            dve.wait_ge(S["rows"], NE)

            def per_expert(row):
                return row[:].unsqueeze(1).to_broadcast(block_shape)

            def per_token(col):
                return col.unsqueeze(2).to_broadcast(block_shape)

            n = 0
            for k in range(TOP):
                src = lg_all if k == 0 else rest
                nc.vector.tensor_reduce(m[:, k, :], src[:], AX_X, ALU.max).then_inc(S["seq"], 1)
                n += 1
                dve.wait_ge(S["seq"], n)
                tt(flag[:], src[:], per_token(m[:, k, :]), ALU.is_lt).then_inc(S["seq"], 1)
                n += 1
                dve.wait_ge(S["seq"], n)
                stt(flag[:], flag[:], float(NE), per_expert(expert), ALU.mult, ALU.add).then_inc(S["seq"], 1)
                n += 1
                dve.wait_ge(S["seq"], n)
                nc.vector.tensor_reduce(pick[:], flag[:], AX_X, ALU.min).then_inc(S["seq"], 1)
                n += 1
                dve.wait_ge(S["seq"], n)
                if k == 1:
                    tt(ex[:], m[:, 1, :], m[:, 0, :], ALU.subtract).then_inc(S["seq"], 1)
                    n += 1
                tt(hot[k][:], per_expert(expert), per_token(pick[:]), ALU.is_equal).then_inc(S["seq"], 1)
                n += 1
                dve.wait_ge(S["seq"], n)
                if k == 0:
                    stt(rest[:], hot[0][:], MASKED, lg_all[:], ALU.mult, ALU.add).then_inc(S["seq"], 1)
                    n += 1
                    dve.wait_ge(S["seq"], n)
            tt(both[:], hot[0][:], hot[1][:], ALU.add).then_inc(S["both_ok"], 1)
            dve.wait_ge(S["both_ok"], 1)
            nc.vector.tensor_reduce(total[:], both[:].rearrange("p t e -> p e t"), AX_X, ALU.add).then_inc(S["tot_ok"], 1)
            for e in range(NE):
                nc.vector.memset(row0[:, e:e + 1], float(e * X_ROWS)).then_inc(S["rows"], 1)
            for i in range(MAX_PAIRS - 1):
                nc.vector.memset(steps[:, i:i + 1], float(PAIR * (i + 1))).then_inc(S["rows"], 1)
            dve.wait_ge(S["rows"], 2 * NE + MAX_PAIRS - 1)
            dve.wait_ge(S["ex_ok"], 1)
            ts(pick[:], ex[:], 1.0, None, ALU.add).then_inc(S["seq"], 1)
            n += 1
            dve.wait_ge(S["seq"], n)
            nc.vector.reciprocal(m[:, 0, :], pick[:]).then_inc(S["seq"], 1)
            n += 1
            dve.wait_ge(S["seq"], n)
            tt(m[:, 1, :], ex[:], m[:, 0, :], ALU.mult).then_inc(S["seq"], 1)
            n += 1

            dve.wait_ge(S["counted"], 1)
            half = NTILE // 2
            for i in range(2):
                same_v = ps_same[i][:].rearrange("p (t e) -> p t e", e=NE)
                for e in range(NE):
                    start = 0.0 if i == 0 else rank[:, half - 1, e:e + 1]
                    out = rank[:, half * i:half * (i + 1), e]
                    nc.vector.tensor_tensor_scan(out, ones[:, 0:half], same_v[:, :, e], start, ALU.mult, ALU.add
                                                 ).then_inc(S["seq"], 1)
                    n += 1
                dve.wait_ge(S["seq"], n)
            for i in range(2):
                part = ps_part[i][:].rearrange("p (t e) -> p t e", e=NE)
                rows = rank[:, half * i:half * (i + 1), :]
                tt(rows, rows, part, ALU.add).then_inc(S["seq"], 1)
                n += 1
            dve.wait_ge(S["seq"], n)
            tt(rank[:], rank[:], ps_base[:, 0, :].unsqueeze(1).to_broadcast(block_shape), ALU.add).then_inc(S["seq"], 1)
            n += 1
            dve.wait_ge(S["seq"], n)
            ts(flag[:], rank[:], CAP - 0.5, NOWHERE, ALU.is_gt, ALU.mult).then_inc(S["seq"], 1)
            n += 1
            dve.wait_ge(S["seq"], n)
            shape = [P, NE, MAX_PAIRS - 1]
            tt(over[:], ps_base[:, 1, :].unsqueeze(2).to_broadcast(shape), steps[:].unsqueeze(1).to_broadcast(shape),
               ALU.is_gt).then_inc(S["seq"], 1)
            tt(planf[:, 1, :], ps_base[0:1, 1, :], row0[0:1, :], ALU.add).then_inc(S["seq"], 1)
            n += 2
            dve.wait_ge(S["seq"], n)
            nc.vector.tensor_reduce(turns[:], over[:], AX_X, ALU.add).then_inc(S["seq"], 1)
            n += 1
            dve.wait_ge(S["seq"], n)
            ts(turns[:], turns[:], 1.0, None, ALU.add).then_inc(S["seq"], 1)
            n += 1
            dve.wait_ge(S["seq"], n)
            nc.vector.tensor_tensor_scan(sums[:], ones[:, 0:NE], turns[:], 0.0, ALU.mult, ALU.add
                                         ).then_inc(S["seq"], 1)
            n += 1
            dve.wait_ge(S["seq"], n)
            tt(shift[:], sums[:], turns[:], ALU.subtract).then_inc(S["seq"], 1)
            nc.vector.tensor_copy(planf[:, 0, :], turns[0:1, :]).then_inc(S["seq"], 1)
            nc.vector.tensor_copy(planf[:, 2, :], sums[0:1, :]).then_inc(S["seq"], 1)
            n += 3
            dve.wait_ge(S["seq"], n)
            stt(shift[:], shift[:], float(PAIR), row0[:], ALU.mult, ALU.subtract).then_inc(S["seq"], 1)
            nc.vector.tensor_copy(plan[:], planf[:]).then_inc(S["seq"], 1)
            n += 2
            dve.wait_ge(S["seq"], n)
            tt(rank[:], flag[:], per_expert(shift), ALU.add).then_inc(S["seq"], 1)
            n += 1
            dve.wait_ge(S["seq"], n)
            for k in range(TOP):
                tt(hot[k][:], hot[k][:], rank[:], ALU.mult).then_inc(S["seq"], 1)
                n += 1
                dve.wait_ge(S["seq"], n)
                nc.vector.tensor_reduce(dst[:, k, :], hot[k][:], AX_X, ALU.add).then_inc(S["seq"], 1)
                n += 1
                dve.wait_ge(S["seq"], n)
            ts(keep[:], dst[:], NOWHERE / 2, None, ALU.is_lt).then_inc(S["seq"], 1)
            tt(kdst[:], dst[:], arrived[:], ALU.add).then_inc(S["seq"], 1)
            n += 2
            dve.wait_ge(S["seq"], n)
            tt(kdst[:], kdst[:], keep[:], ALU.mult).then_inc(S["seq"], 1)
            n += 1
            dve.wait_ge(S["seq"], n)
            nc.vector.tensor_copy(src_row[:], kdst[:]).then_inc(S["seq"], 1)
            n += 1
            tt(prob[:], m[:], keep[:], ALU.mult).then_inc(S["seq"], 1)
            n += 1
            dve.wait_ge(S["seq"], n)


TABLES_R = 6 + 16 + 10 + 16


def expert_stage(nc, w1_dram, w2_dram, lnw_dram, xd_dram, y_dram, plan):
    ctx = ExitStack()
    with ctx:
        def sb(name, shape, dt=F32):
            return ctx.enter_context(nc.sbuf_tensor(name, shape, dt))

        ident = sb("e_ident", [P, P])
        ln = sb("e_ln", [P, 2, KD])
        w1s = sb("e_w1s", [P, KD, FF])
        w2s = sb("e_w2s", [P, MF, DM])
        w1 = [[sb(f"e_w1{i}{h}", [P, KD, FF], F32R) for h in range(2)] for i in range(2)]
        w2 = [[sb(f"e_w2{i}{h}", [P, MF, DM], F32R) for h in range(2)] for i in range(2)]
        x = [sb(f"e_x{i}", [P, HT, DM]) for i in range(2)]
        xf = sb("e_xf", [P, KD, HALF])
        xt = [[sb(f"e_xt{i}{h}", [P, KD, HALF], F32R) for h in range(2)] for i in range(2)]
        af = sb("e_af", [P, MF, HALF])
        a = [[sb(f"e_a{i}{h}", [P, MF, HALF], F32R) for h in range(2)] for i in range(2)]
        y = [sb(f"e_y{i}", [P, HT, DM]) for i in range(2)]
        zero = sb("e_zero", [P, PAIR // P, DM])
        pt = [ctx.enter_context(nc.psum_tensor(f"e_pt{i}", [P, KD, HALF], F32)) for i in range(2)]
        p1 = [ctx.enter_context(nc.psum_tensor(f"e_p1{i}", [P, 2, HALF], F32)) for i in range(4)]
        p2 = [ctx.enter_context(nc.psum_tensor(f"e_p2{i}", [P, HT, DM], F32)) for i in range(2)]
        names = "c0 zeroed zst ld_w w_ok ld_x0 ld_x1 t_ps xf_ok xt_ok split f1_ps af_ok a_ok f2_ps y_ok st0 st1".split()
        S = {n: ctx.enter_context(nc.semaphore("e_" + n)) for n in names}
        block = ctx.enter_context(nc.Block())

        def wait_apart(eng, *waits):
            waits = [(S[s], v if isinstance(v, int) else eng.to_reg(v)) for s, v in waits]
            eng.wait_ge(S["c0"], 1)
            for semaphore, value in waits:
                eng.wait_ge(semaphore, value)

        def experts(eng, name, turn, weights=None):
            done = eng.alloc_register(name)
            eng.reg_mov(done, 0)
            with eng.Fori(0, NE // 2) as pair:
                for i in range(2):
                    e = 2 * pair + i
                    turns = eng.value_load(plan[0:1, 0, bass.ds(e, 1)], min_val=1, max_val=MAX_PAIRS)
                    if weights:
                        weights(pair, i, eng.snap(done))
                    with eng.Fori(0, turns) as c:
                        turn(pair, i, c, eng.snap(done))
                        eng.reg_add(done, done, 1)
            return eng.snap(done)

        @block.sync
        def _(sp):
            sp.wait_ge(S["zeroed"], 1)
            for e in range(NE):
                row = sp.value_load(plan[0:1, 1, e:e + 1], min_val=0, max_val=NE * X_ROWS - PAIR)
                sp.dma_start(xd_dram[bass.ds(row, PAIR), :].rearrange("(p j) c -> p j c", p=P), zero[:]
                             ).then_inc(S["zst"], 16)
            sp.wait_ge(S["zst"], 16 * NE)

            def turn(pair, i, c, q):
                for n in range(2):
                    sp.wait_ge(S["t_ps"], 2 * q + n + 1)
                    rows = xd_dram[bass.ds((2 * pair + i) * X_ROWS + c * PAIR + n * HALF, HALF), :]
                    sp.dma_start(x[n][:], rows.rearrange("(p j) c -> p j c", p=P)).then_inc(S[f"ld_x{n}"], 16)

            q = experts(sp, "e_sp", turn)
            total = sp.value_load(plan[0:1, 2, NE - 1:NE], min_val=NE, max_val=MAX_TURNS)
            zeros = sp.alloc_register("e_zeros")
            sp.reg_mov(zeros, NE)
            with sp.Fori(total, MAX_TURNS + 1) as c:
                sp.dma_start(y_dram[bass.ds(c * PAIR, PAIR), :].rearrange("(p j) c -> p j c", p=P), zero[:]
                             ).then_inc(S["zst"], 16)
                sp.reg_add(zeros, zeros, 1)
            sp.wait_ge(S["t_ps"], 2 * q + 1)
            sp.dma_start(x[0][:], xd_dram[0:HALF, :].rearrange("(p j) c -> p j c", p=P)).then_inc(S["ld_x0"], 16)
            wait_apart(sp, ("ld_x0", 16 * q + 16), ("zst", 16 * sp.snap(zeros)))

        @block.gpsimd
        def _(pool):
            pool.memset(zero[:], 0.0).then_inc(S["zeroed"], 1)
            pool.wait_ge(S["zeroed"], 1)
            pool.memset(ident[:], 0.0).then_inc(S["c0"], 1)
            pool.wait_ge(S["c0"], 1)
            pool.affine_select(out=ident[:], in_=ident[:], compare_op=ALU.not_equal, fill=1.0, base=0,
                               pattern=[[-1, P]], channel_multiplier=1).then_inc(S["c0"], 1)
            for n in range(2):
                pool.dma_start(ln[:, n, :], lnw_dram[:, n, :]).then_inc(S[f"st{n}"], 16)

            def split_weights(e, i):
                wait_apart(pool, ("ld_w", 32 * e + 32))
                for raw, parts in ((w1s, w1[i]), (w2s, w2[i])):
                    pool.tensor_copy(parts[0][:], raw[:]).then_inc(S["w_ok"], 1)
                for n, (raw, parts) in enumerate(((w1s, w1[i]), (w2s, w2[i]))):
                    pool.wait_ge(S["w_ok"], 4 * e + 1 + n)
                    pool.tensor_tensor(parts[1][:], raw[:], parts[0][:].bitcast(F32), ALU.subtract
                                       ).then_inc(S["w_ok"], 1)

            def load_weights(e):
                pool.dma_start(w1s[:], w1_dram[bass.ds(e * DM, DM), :].rearrange("(k p) f -> p k f", p=P)
                               ).then_inc(S["ld_w"], 16)
                pool.dma_start(w2s[:], w2_dram[bass.ds(e * FF, FF), :].rearrange("(m p) c -> p m c", p=P)
                               ).then_inc(S["ld_w"], 16)

            load_weights(0)
            split_weights(0, 0)
            pool.wait_ge(S["w_ok"], 4)
            load_weights(1)

            def weights(pair, i, q):
                e = 2 * pair + i + 1
                pool.wait_ge(S["f2_ps"], 2 * q + 2)
                split_weights(e, 1 - i)
                pool.wait_ge(S["w_ok"], 4 * e + 4)
                load_weights((e + 1) % NE)

            def turn(pair, i, c, q):
                for n in range(2):
                    pool.wait_ge(S["y_ok"], 2 * q + n + 3)
                    rows = y_dram[bass.ds(q * PAIR + n * HALF, HALF), :]
                    pool.dma_start(rows.rearrange("(p j) c -> p j c", p=P), y[n][:]).then_inc(S[f"st{n}"], 16)

            q = experts(pool, "e_pool", turn, weights)
            wait_apart(pool, ("st0", 16 * q + 16), ("st1", 16 * q + 16))
            pool.wait_ge(S["ld_w"], 32 * (NE + 2))

        @block.tensor
        def _(pe):
            mm = nc.tensor.matmul
            pe.nop().then_inc(S["t_ps"], 2)
            pe.nop().then_inc(S["f1_ps"], 1)
            pe.nop().then_inc(S["f2_ps"], 2)
            pe.wait_ge(S["c0"], 2)

            def turn_rows(q, n):
                pe.wait_ge(S[f"ld_x{n}"], 16 * q + 16)
                pe.wait_ge(S["xf_ok"], 2 * q + n + 1)
                for k in range(KD):
                    for j in range(HT):
                        i = nc.tensor.transpose(pt[n][:, k, j * P:(j + 1) * P], x[n][:, j, k * P:(k + 1) * P], ident[:])
                i.then_inc(S["t_ps"], 1)

            pe.wait_ge(S["ld_x0"], 16)
            for k in range(KD):
                for j in range(HT):
                    i = nc.tensor.transpose(pt[0][:, k, j * P:(j + 1) * P], x[0][:, j, k * P:(k + 1) * P], ident[:])
            i.then_inc(S["t_ps"], 1)

            def first_product(q, n, i):
                pe.wait_ge(S["xt_ok"], 2 * q + n + 3)
                pe.wait_ge(S["af_ok"], 4 * q + 2 * n + 1)
                for m in range(MF):
                    bank = p1[2 * n + m // 2]
                    for k in range(KD):
                        for s, (wp, xp) in enumerate(PARTS):
                            o = mm(bank[:, m % 2, :], w1[i][wp][:, k, m * P:(m + 1) * P], xt[n][xp][:, k, :],
                                   start=(k == 0 and s == 0), stop=(k == KD - 1 and s == 2))
                    if m % 2:
                        o.then_inc(S["f1_ps"], 1)

            def second_product(q, n, i):
                pe.wait_ge(S["y_ok"], 2 * q + n + 1)
                for j in range(HT):
                    for m in range(MF):
                        if j == 0 and m % 2 == 0:
                            pe.wait_ge(S["a_ok"], 4 * q + 2 * n + m // 2 + 3)
                        for s, (wp, ap) in enumerate(PARTS):
                            o = mm(p2[n][:, j, :], a[n][ap][:, m, j * P:(j + 1) * P], w2[i][wp][:, m, :],
                                   start=(m == 0 and s == 0), stop=(m == MF - 1 and s == 2))
                o.then_inc(S["f2_ps"], 1)

            def turn(pair, i, c, q):
                turn_rows(q, 1)
                pe.wait_ge(S["w_ok"], 8 * pair + 4 * i + 4)
                first_product(q, 0, i)
                first_product(q, 1, i)
                second_product(q, 0, i)
                turn_rows(q + 1, 0)
                second_product(q, 1, i)

            experts(pe, "e_pe", turn)

        @block.scalar
        def _(act):
            act.nop().then_inc(S["af_ok"], 3)
            act.nop().then_inc(S["xf_ok"], 2)
            for n in range(2):
                act.wait_ge(S[f"st{n}"], 16)

            def move(q, n):
                act.wait_ge(S["t_ps"], 2 * q + n + 3)
                act.wait_ge(S["xt_ok"], 2 * q + n + 2)
                for k in range(KD):
                    o = act.activation(xf[:, k, :], pt[n][:, k, :], ACT.Identity, bias=ln[:, 1, k:k + 1],
                                       scale=ln[:, 0, k:k + 1])
                o.then_inc(S["xf_ok"], 1)

            move(0, 0)

            def turn(pair, i, c, q):
                move(q, 1)
                for n in range(2):
                    for b in range(2):
                        act.wait_ge(S["f1_ps"], 4 * q + 2 * n + b + 2)
                        act.wait_ge(S["a_ok"], 4 * q + 2 * n + b + 1)
                        act.activation(af[:, 2 * b:2 * b + 2, :], p1[2 * n + b][:], ACT.Gelu_apprx_tanh
                                       ).then_inc(S["af_ok"], 1)
                move(q + 1, 0)

            experts(act, "e_act", turn)

        @block.vector
        def _(dve):
            tt = nc.vector.tensor_tensor
            dve.nop().then_inc(S["xt_ok"], 2)
            dve.nop().then_inc(S["y_ok"], 2)
            dve.nop().then_inc(S["a_ok"], 2)

            def split_x(q, n, first=False):
                dve.wait_ge(S["xf_ok"], 2 * q + n + 3)
                if not first:
                    dve.wait_ge(S["f1_ps"], 4 * q + 2 * n - 1)
                nc.vector.tensor_copy(xt[n][0][:], xf[:]).then_inc(S["split"], 1)
                dve.wait_ge(S["split"], 6 * q + n + 1)
                tt(xt[n][1][:], xf[:], xt[n][0][:].bitcast(F32), ALU.subtract).then_inc(S["xt_ok"], 1)

            split_x(0, 0, True)

            def split_a(q, n):
                dve.wait_ge(S["f2_ps"], 2 * q + n + 1)
                for b in range(2):
                    part = slice(2 * b, 2 * b + 2)
                    dve.wait_ge(S["af_ok"], 4 * q + 2 * n + b + 4)
                    nc.vector.tensor_copy(a[n][0][:, part, :], af[:, part, :]).then_inc(S["split"], 1)
                    dve.wait_ge(S["split"], 6 * q + 2 * n + b + 3)
                    tt(a[n][1][:, part, :], af[:, part, :], a[n][0][:, part, :].bitcast(F32), ALU.subtract
                       ).then_inc(S["a_ok"], 1)

            def y_out(q, n):
                dve.wait_ge(S["f2_ps"], 2 * q + n + 3)
                dve.wait_ge(S[f"st{n}"], 16 * q + 16)
                nc.vector.tensor_copy(y[n][:], p2[n][:]).then_inc(S["y_ok"], 1)

            def turn(pair, i, c, q):
                split_x(q, 1)
                split_a(q, 0)
                split_a(q, 1)
                y_out(q, 0)
                split_x(q + 1, 0)
                y_out(q, 1)

            experts(dve, "e_dve", turn)


def combine_stage(nc, base_dram, y_dram, out, src_row, prob):
    ctx = ExitStack()
    with ctx:
        def sb(name, shape, dt=F32):
            return [ctx.enter_context(nc.sbuf_tensor(f"{name}{i}", shape, dt)) for i in range(2)]

        b, idx, o = sb("o_b", [P, GT, DM]), sb("o_idx", [P, TOP, GT], I32), sb("o_o", [P, GT, DM])
        yr = sb("o_y", [P, TOP, GT, DM])
        names = "c0 ld0 ld1 idx_ok gath0 gath1 part sum st0 st1".split()
        S = {n: ctx.enter_context(nc.semaphore("o_" + n)) for n in names}
        block = ctx.enter_context(nc.Block())
        out_v = out.rearrange("(s b) c -> b s c", s=NSEQ)

        def steps(eng, step):
            for i in range(2):
                step(0, i)
            with eng.Fori(1, NGT // 2) as h:
                for i in range(2):
                    step(h, i)

        @block.sync
        def _(sp):
            def step(h, i):
                g = 2 * h + i
                if not isinstance(h, int):
                    sp.wait_ge(S["part"], GT * (g - 1))
                sp.dma_start(b[i][:], base_dram[:, bass.ds(g * GT, GT), :]).then_inc(S[f"ld{i}"], 16)

            steps(sp, step)
            for i in range(2):
                sp.wait_ge(S[f"ld{i}"], 16 * NGT // 2)

        @block.scalar
        def _(act):
            def step(h, i):
                g = 2 * h + i
                act.wait_ge(S["sum"], GT * (g + 1))
                for j in range(GT):
                    act.dma_start(out_v[bass.ds(g * 4 * GT + 4 * j, 4), :, :], o[i][:, j, :]).then_inc(S[f"st{i}"], 16)

            steps(act, step)
            for i in range(2):
                act.wait_ge(S[f"st{i}"], 16 * GT * NGT // 2)

        @block.gpsimd
        def _(pool):
            pool.nop().then_inc(S["c0"], 1)

            def step(h, i):
                g = 2 * h + i
                if not isinstance(h, int):
                    pool.wait_ge(S[f"gath{i}"], 16 * TOP * GT * h)
                pool.tensor_copy(idx[i][:], src_row[:, :, bass.ds(g * GT, GT)]).then_inc(S["idx_ok"], 1)
                pairs = [(S["idx_ok"], g + 1)] + ([] if isinstance(h, int) else [(S["sum"], GT * (g - 1))])
                pairs = [(s, v if isinstance(v, int) else pool.to_reg(v)) for s, v in pairs]
                pool.wait_ge(S["c0"], 1)
                for s, v in pairs:
                    pool.wait_ge(s, v)
                for j in range(GT):
                    for k in range(TOP):
                        pool.indirect_dma_start(out=yr[i][:, k, j, :], out_offset=None, in_=y_dram,
                                                in_offset=bass.IndirectOffsetOnAxis(
                                                    ap=idx[i][:, k, j:j + 1].bitcast(U32), axis=0)
                                                ).then_inc(S[f"gath{i}"], 16)

            steps(pool, step)

        @block.vector
        def _(dve):
            stt = nc.vector.scalar_tensor_tensor

            def step(h, i):
                g = 2 * h + i
                dve.wait_ge(S[f"ld{i}"], 16 * (h + 1))
                dve.wait_ge(S[f"gath{i}"], 16 * TOP * GT * (h + 1))
                if not isinstance(h, int):
                    dve.wait_ge(S[f"st{i}"], 16 * GT * h)
                for j in range(GT):
                    stt(yr[i][:, 0, j, :], yr[i][:, 0, j, :], prob[:, 0, bass.ds(g * GT + j, 1)], b[i][:, j, :],
                        ALU.mult, ALU.add).then_inc(S["part"], 1)
                for j in range(GT):
                    dve.wait_ge(S["part"], GT * g + j + 1)
                    stt(o[i][:, j, :], yr[i][:, 1, j, :], prob[:, 1, bass.ds(g * GT + j, 1)], yr[i][:, 0, j, :],
                        ALU.mult, ALU.add).then_inc(S["sum"], 1)

            steps(dve, step)


def build(nc, h, out):
    h1_dram = nc.dram_tensor("h1_rows", [NSEQ * SEQ, DM], F32).ap()
    base_dram = nc.dram_tensor("base_rows", [P, NTILE, DM], F32).ap()
    xd_dram = nc.dram_tensor("expert_in", [NE * X_ROWS, DM], F32).ap()
    y_dram = nc.dram_tensor("expert_out", [(MAX_TURNS + 1) * PAIR, DM], F32).ap()
    mamba_w = [{k[:-1]: v for k, v in h.items() if k.endswith(str(d))} for d in range(DIRS)]
    mamba_stage(nc, h["ids"], h["table"], mamba_w, h1_dram)
    with ExitStack() as ctx:
        arrived = ctx.enter_context(nc.sbuf_tensor("arrived", [P, TOP, NTILE], F32))
        src_row = ctx.enter_context(nc.sbuf_tensor("src_row", [P, TOP, NTILE], I32))
        prob = ctx.enter_context(nc.sbuf_tensor("prob", [P, TOP, NTILE], F32))
        plan = ctx.enter_context(nc.sbuf_tensor("plan", [1, 3, NE], I32))
        lg_all = ctx.enter_context(nc.sbuf_tensor("lg_all", [P, NTILE, NE], F32))
        attention_stage(nc, h, h1_dram, base_dram, xd_dram, arrived, lg_all)
        routing_stage(nc, lg_all, arrived, src_row, prob, plan)
        expert_stage(nc, h["moe_w1"], h["moe_w2"], h["ln2"], xd_dram, y_dram, plan)
        combine_stage(nc, base_dram, y_dram, out, src_row, prob)


def per_chunk(v):
    return v.reshape(-1, P).T


def mamba_layout(i):
    out = {}
    for d, suffix in enumerate("fb"):
        def g(name):
            return i[f"L0_attn_{name}_{suffix}"]
        wx = g("Wx")
        out[f"Win{d}"] = g("Win").T
        out[f"Wx{d}"] = np.concatenate([wx[RK:], wx[:RK]]).T
        out[f"Wdt{d}"] = g("Wdt").T
        out[f"Wout{d}"] = g("Wout").T
        out[f"Wfuse{d}"] = i["L0_attn_Wfuse"][:, DM * d:DM * (d + 1)].T
        out[f"convw{d}"] = g("convw")
        out[f"Alog{d}"] = g("Alog")
        for name in ("convb", "bdt", "Dp", "ln_g", "ln_b"):
            out[f"{name}{d}"] = per_chunk(g(name))
    out["bfuse0"] = i["L0_attn_bfuse"].reshape(1, DM)
    return out


def attention_layout(i):
    f = "L0_ffn_"
    w = i[f + "qkv_weight"].reshape(NG, NQ + 2, HD, DM)
    wq = np.zeros((DM, NQ + 1, NG, S_A), w.dtype)
    wq[..., :HD] = w[:, :NQ + 1].transpose(3, 1, 0, 2)
    ln = {n: np.stack([per_chunk(i[f + "ln1_" + n]), per_chunk(i[f + "ln2_" + n])], 1) for n in ("weight", "bias")}
    return dict(
        wq=wq.reshape(DM, NQ + 1, P),
        wv=w[:, NQ + 1].transpose(2, 0, 1).reshape(DM, NG * HD),
        wp=i[f + "proj_weight"].reshape(DM, NG, NQ, HD).transpose(1, 3, 2, 0).reshape(NG * HD, NQ, DM),
        wr=i[f + "router_weight"],
        lnw=ln["weight"],
        lnb=ln["bias"],
        ln2=np.stack([per_chunk(i[f + "ln2_weight"]), per_chunk(i[f + "ln2_bias"])], 1),
        moe_w1=i[f + "moe_w1"].reshape(NE * DM, FF),
        moe_w2=i[f + "moe_w2"].reshape(NE * FF, DM),
    )


def ids_layout(x):
    ids = x.reshape(NSEQ, TT, P).transpose(2, 0, 1).reshape(P, NSEQ * TT)
    return np.concatenate([ids, np.zeros((P, 2 * TT), ids.dtype)], 1)


def kernel(**inputs):
    import concourse.bacc as _bacc
    from concourse.bass_utils import run_bass_kernel_spmd as _run

    i = {k: np.asarray(v) for k, v in inputs.items()}
    arrays = {**mamba_layout(i), **attention_layout(i), "ids": ids_layout(i["x"]), "table": i["L0_tok_W"].T}
    arrays = {k: np.ascontiguousarray(v) for k, v in arrays.items()}
    nc = _bacc.Bacc("TRN2", target_bir_lowering=False, num_devices=1)
    handles = {k: nc.dram_tensor("in_" + k, v.shape, mybir.dt.from_np(v.dtype), kind="ExternalInput").ap()
               for k, v in arrays.items()}
    out = nc.dram_tensor("out", [NSEQ * SEQ, DM], F32, kind="ExternalOutput").ap()
    build(nc, handles, out)
    results = _run(nc, [{"in_" + k: v for k, v in arrays.items()}], core_ids=[0]).results
    return np.asarray(results[0]["out"]).reshape(NSEQ, SEQ, DM)
```
